# Optimizing a Trainium2 kernel written in Bass

```python
import numpy as np
import jax
import jax.numpy as jnp

def _softmax(x, axis=-1):
    return jax.nn.softmax(x, axis=axis)

def _gelu(x):
    return jax.nn.gelu(x, approximate=True)

def _silu(x):
    return jax.nn.silu(x)

def _sigmoid(x):
    return jax.nn.sigmoid(x)

def _layernorm(x, axis=-1, eps=1e-05):
    m = jnp.mean(x, axis=axis, keepdims=True)
    v = jnp.var(x, axis=axis, keepdims=True)
    return (x - m) / jnp.sqrt(v + eps)

def _scatter_add(tgt, idx, src, axis=0):
    return tgt.at[idx].add(src)

def _segment_sum(src, seg, n):
    return jax.ops.segment_sum(src, seg, n)
kernel_name = 'mk_gps_d1_gnn_r8_ba238c'

def setup_inputs(seed: int=0):
    np.random.seed(seed)
    _w = jnp.asarray

    def _rec_inputs():
        import jax
        import jax.numpy as jnp
        _gk = jax.random.key(seed)
        x = -0.0003713 + 1 * jax.random.normal(jax.random.fold_in(_gk, 1), (6250, 256), jnp.float32)
        src = jax.random.randint(jax.random.fold_in(_gk, 2), (100000,), 0, 6250, jnp.int32)
        dst = jnp.minimum((6250 * jax.random.uniform(jax.random.fold_in(_gk, 3), (100000,)) ** 2.0).astype(jnp.int32), 49999)
        _o = jnp.argsort(dst, stable=True)
        src = src[_o]
        dst = dst[_o]
        edge_attr_3 = -1.09012e-05 + 0.99985 * jax.random.normal(jax.random.fold_in(_gk, 11), (100000, 3), jnp.float32)
        return (x, src, dst, edge_attr_3)
    x, src, dst, edge_attr_3 = _rec_inputs()

    def _L0_gnn_setup():
        import jax, jax.numpy as jnp
        import numpy as np
        N = 6250
        E = 50000
        IN = 256
        H = 8
        D = 32
        EF = 3
        key = jax.random.key(seed)
        ks = jax.random.split(key, 8)
        x = jax.random.normal(ks[0], (N, IN), dtype=jnp.float32)
        edge_index = jax.random.randint(ks[1], (2, E), 0, N, dtype=jnp.int64)
        edge_attr = jax.random.normal(ks[2], (E, EF), dtype=jnp.float32)
        W = jax.random.normal(ks[3], (H * D, IN), dtype=jnp.float32) * np.float32(np.sqrt(2.0 / (IN + H * D)))
        a_src = jax.random.normal(ks[4], (H, D), dtype=jnp.float32) * np.float32(np.sqrt(2.0 / (H + D)))
        a_dst = jax.random.normal(ks[5], (H, D), dtype=jnp.float32) * np.float32(np.sqrt(2.0 / (H + D)))
        edge_W = jax.random.normal(ks[6], (H * D, EF), dtype=jnp.float32) * np.float32(np.sqrt(2.0 / (EF + H * D)))
        edge_b = jnp.zeros((H * D,), dtype=jnp.float32)
        bias = jnp.zeros((H * D,), dtype=jnp.float32)
        return {'x': x, 'W': W, 'a_src': a_src, 'a_dst': a_dst, 'edge_W': edge_W, 'edge_b': edge_b, 'bias': bias, 'edge_attr': edge_attr, 'edge_index': edge_index}
    _L0_gnn_all = _L0_gnn_setup()
    _L0_gnn_in = {k: v for k, v in _L0_gnn_all.items() if k in ('W', 'a_src', 'a_dst', 'edge_W', 'edge_b', 'bias')}
    del _L0_gnn_all

    def _L0_mix_setup():
        import jax, jax.numpy as jnp
        import numpy as np
        EPS_NORM = 1e-06
        EPS_ATTN = 1e-06
        HEADS = 8

        def rmsnorm(x, w):
            ms = jnp.mean(x * x, axis=-1, keepdims=True)
            return w * (x * jax.lax.rsqrt(ms + EPS_NORM))

        def linear_attention(x, w_qkv, w_out, b_out):
            B, N, D = x.shape
            hd = D // HEADS
            qkv = (x @ w_qkv).reshape(B, N, 3, HEADS, hd)
            q, k, v = (qkv[:, :, 0], qkv[:, :, 1], qkv[:, :, 2])
            q = jax.nn.elu(q) + 1.0
            k = jax.nn.elu(k) + 1.0
            kv = jnp.einsum('bnhd,bnhm->bhdm', k, v)
            z = 1.0 / (jnp.einsum('bnhd,bhd->bnh', q, k.sum(axis=1)) + EPS_ATTN)
            out = jnp.einsum('bnhd,bhdm,bnh->bnhm', q, kv, z)
            out = out.reshape(B, N, D)
            return out @ w_out + b_out
        key = jax.random.key(seed)
        ks = jax.random.split(key, 4)
        B, N, D = (16, 1024, 256)
        x = jax.random.normal(ks[0], (B, N, D), dtype=jnp.float32)
        w_norm1 = jnp.ones((D,), dtype=jnp.float32)
        w_qkv = jax.random.normal(ks[1], (D, 3 * D), dtype=jnp.float32) * 0.02
        w_out = jax.random.normal(ks[2], (D, D), dtype=jnp.float32) * 0.02
        b_out = jnp.zeros((D,), dtype=jnp.float32)
        w_norm2 = jnp.ones((D,), dtype=jnp.float32)
        return {'x': x, 'w_norm1': w_norm1, 'w_qkv': w_qkv, 'w_out': w_out, 'b_out': b_out, 'w_norm2': w_norm2}
    _L0_mix_all = _L0_mix_setup()
    _L0_mix_in = {k: v for k, v in _L0_mix_all.items() if k in ('w_norm1', 'w_qkv', 'w_out', 'b_out', 'w_norm2')}
    del _L0_mix_all

    def _L0_ffn_setup():
        import jax, jax.numpy as jnp
        import numpy as np
        B, S, D, H, E, K = (8, 1024, 256, 1024, 8, 2)
        key = jax.random.key(seed)
        ks = jax.random.split(key, 7)
        s_in = 1.0 / np.sqrt(D)
        s_hid = 1.0 / np.sqrt(H)
        return {'x': jax.random.normal(ks[0], (B, S, D), dtype=jnp.float32), 'Wg': jax.random.uniform(ks[1], (E, D), jnp.float32, -s_in, s_in), 'bg': jax.random.uniform(ks[2], (E,), jnp.float32, -s_in, s_in), 'W1': jax.random.uniform(ks[3], (E, H, D), jnp.float32, -s_in, s_in), 'b1': jax.random.uniform(ks[4], (E, H), jnp.float32, -s_in, s_in), 'W2': jax.random.uniform(ks[5], (E, D, H), jnp.float32, -s_hid, s_hid), 'b2': jax.random.uniform(ks[6], (E, D), jnp.float32, -s_hid, s_hid)}
    _L0_ffn_all = _L0_ffn_setup()
    _L0_ffn_in = {k: v for k, v in _L0_ffn_all.items() if k in ('Wg', 'bg', 'W1', 'b1', 'W2', 'b2')}
    del _L0_ffn_all
    return {'x': x, 'src': src, 'dst': dst, 'edge_attr_3': edge_attr_3, 'L0_gnn_W': _L0_gnn_in['W'], 'L0_gnn_a_src': _L0_gnn_in['a_src'], 'L0_gnn_a_dst': _L0_gnn_in['a_dst'], 'L0_gnn_edge_W': _L0_gnn_in['edge_W'], 'L0_gnn_edge_b': _L0_gnn_in['edge_b'], 'L0_gnn_bias': _L0_gnn_in['bias'], 'L0_mix_w_norm1': _L0_mix_in['w_norm1'], 'L0_mix_w_qkv': _L0_mix_in['w_qkv'], 'L0_mix_w_out': _L0_mix_in['w_out'], 'L0_mix_b_out': _L0_mix_in['b_out'], 'L0_mix_w_norm2': _L0_mix_in['w_norm2'], 'L0_ffn_Wg': _L0_ffn_in['Wg'], 'L0_ffn_bg': _L0_ffn_in['bg'], 'L0_ffn_W1': _L0_ffn_in['W1'], 'L0_ffn_b1': _L0_ffn_in['b1'], 'L0_ffn_W2': _L0_ffn_in['W2'], 'L0_ffn_b2': _L0_ffn_in['b2']}

def reference(x, src, dst, edge_attr_3, L0_gnn_W, L0_gnn_a_src, L0_gnn_a_dst, L0_gnn_edge_W, L0_gnn_edge_b, L0_gnn_bias, L0_mix_w_norm1, L0_mix_w_qkv, L0_mix_w_out, L0_mix_b_out, L0_mix_w_norm2, L0_ffn_Wg, L0_ffn_bg, L0_ffn_W1, L0_ffn_b1, L0_ffn_W2, L0_ffn_b2):
    import jax
    import jax.numpy as jnp

    def _L0_gnn_ref(x, W, a_src, a_dst, edge_W, edge_b, bias, edge_attr, edge_index):
        import jax, jax.numpy as jnp
        import numpy as np
        N = 6250
        E = 50000
        IN = 256
        H = 8
        D = 32
        EF = 3
        n = x.shape[0]
        h = (x @ W.T).reshape(n, H, D)
        src, dst = (edge_index[0], edge_index[1])
        h_src = h[src]
        h_dst = h[dst]
        alpha = jnp.einsum('ehd,hd->eh', h_src, a_src) + jnp.einsum('ehd,hd->eh', h_dst, a_dst)
        enc = jax.nn.relu(edge_attr @ edge_W.T + edge_b).reshape(-1, H, D)
        alpha = alpha + jnp.sum(enc * h_dst, axis=-1)
        alpha = jnp.where(alpha >= 0, alpha, 0.2 * alpha)
        amax = jax.ops.segment_max(alpha, dst, num_segments=n)
        ex = jnp.exp(alpha - amax[dst])
        denom = jax.ops.segment_sum(ex, dst, num_segments=n)
        attn = ex / jnp.maximum(denom[dst], 1e-10)
        out = jax.ops.segment_sum(h_src * attn[..., None], dst, num_segments=n)
        return out.reshape(n, H * D) + bias

    def _L0_mix_ref(x, w_norm1, w_qkv, w_out, b_out, w_norm2):
        import jax, jax.numpy as jnp
        import numpy as np
        EPS_NORM = 1e-06
        EPS_ATTN = 1e-06
        HEADS = 8

        def rmsnorm(x, w):
            ms = jnp.mean(x * x, axis=-1, keepdims=True)
            return w * (x * jax.lax.rsqrt(ms + EPS_NORM))

        def linear_attention(x, w_qkv, w_out, b_out):
            B, N, D = x.shape
            hd = D // HEADS
            qkv = (x @ w_qkv).reshape(B, N, 3, HEADS, hd)
            q, k, v = (qkv[:, :, 0], qkv[:, :, 1], qkv[:, :, 2])
            q = jax.nn.elu(q) + 1.0
            k = jax.nn.elu(k) + 1.0
            kv = jnp.einsum('bnhd,bnhm->bhdm', k, v)
            z = 1.0 / (jnp.einsum('bnhd,bhd->bnh', q, k.sum(axis=1)) + EPS_ATTN)
            out = jnp.einsum('bnhd,bhdm,bnh->bnhm', q, kv, z)
            out = out.reshape(B, N, D)
            return out @ w_out + b_out
        h = x + linear_attention(rmsnorm(x, w_norm1), w_qkv, w_out, b_out)
        return h + rmsnorm(h, w_norm2)

    def _L0_ffn_ref(x, Wg, bg, W1, b1, W2, b2):
        import jax, jax.numpy as jnp
        import numpy as np
        B, S, D, H, E, K = (8, 1024, 256, 1024, 8, 2)
        gate_scores = jnp.einsum('bsd,ed->bse', x, Wg) + bg
        topk_scores, topk_idx = jax.lax.top_k(gate_scores, K)
        topk_probs = jax.nn.softmax(topk_scores, axis=-1)
        combine = jnp.sum(topk_probs[..., None] * jax.nn.one_hot(topk_idx, E, dtype=x.dtype), axis=-2)
        out = jnp.zeros_like(x)
        for e in range(E):
            h = jax.nn.relu(jnp.einsum('bsd,hd->bsh', x, W1[e]) + b1[e])
            y = jnp.einsum('bsh,dh->bsd', h, W2[e]) + b2[e]
            out = out + combine[..., e:e + 1] * y
        return out
    edge_index = jnp.stack([src, dst])
    xn = _layernorm(x, axis=-1)
    x = x + _L0_gnn_ref(xn, L0_gnn_W, L0_gnn_a_src, L0_gnn_a_dst, L0_gnn_edge_W, L0_gnn_edge_b, L0_gnn_bias, edge_attr_3, edge_index) + _L0_mix_ref(xn[None], L0_mix_w_norm1, L0_mix_w_qkv, L0_mix_w_out, L0_mix_b_out, L0_mix_w_norm2)[0]
    x = x + _L0_ffn_ref(_layernorm(x, axis=-1)[None], L0_ffn_Wg, L0_ffn_bg, L0_ffn_W1, L0_ffn_b1, L0_ffn_W2, L0_ffn_b2)[0]
    return x

_drawn_inputs = setup_inputs


def setup_inputs(seed=0):
    import zlib

    import numpy as np

    out = dict(_drawn_inputs(seed))
    spreads = {'L0_gnn_edge_b': (0.0, 0.366),
     'L0_gnn_bias': (0.0, 0.1),
     'L0_mix_w_norm1': (1.0, 0.6),
     'L0_mix_b_out': (0.0, 0.1),
     'L0_mix_w_norm2': (1.0, 0.2)}
    factors = {'L0_mix_w_qkv': 8.0,
     'L0_mix_w_out': 8.0,
     'L0_ffn_bg': 5.032,
     'L0_ffn_b1': 8.0,
     'L0_ffn_b2': 8.0}
    for name, (base, spread) in spreads.items():
        noise = np.random.default_rng([zlib.crc32(name.encode()), seed]).standard_normal(out[name].shape)
        drawn = base * np.exp(spread * noise) if base else spread * noise
        out[name] = jnp.asarray(drawn.astype(out[name].dtype))
    for name, factor in factors.items():
        out[name] = (out[name] * factor).astype(out[name].dtype)
    return out
```

```python
from contextlib import ExitStack

import numpy as np

import concourse.bass as bass
from concourse import mybir

ALU = mybir.AluOpType
ACT = mybir.ActivationFunctionType
AX = mybir.AxisListType
F32 = mybir.dt.float32
BF16 = mybir.dt.bfloat16
I32 = mybir.dt.int32

P = 128
D = 256
KC = D // P
HEADS = 8
HD = D // HEADS
N = 6250
NT = 50
NP = NT * P
LAST = N // P
LAST_ROWS = N - LAST * P
HC = D + 2 * HEADS
HX = D + HEADS
QC = 3 * D
COL_V, COL_QK, COL_S = D, 2 * D, 4 * D
WALL = COL_S + 2 * HEADS
E = 100000
ET = 784
COUNT_P = 112
NS = 440
SG = 4
assert ET % COUNT_P == 0 and (ET - 2) * P >= E
assert 2 * NS >= (-(-E // P) + (NT - 2) + (NT - 1)) and NS <= SG * P
LN_EPS = 1e-5
RMS_EPS = 1e-6
ATT_EPS = 1e-6


class Steps:

    def __init__(self, base=0):
        self.base, self.n = base, 0

    def last(self):
        self.n += 1
        return self.base + self.n


def build_constants(nc, c):
    with nc.semaphore("pool_step") as pool_step, nc.Block() as block:

        @block.gpsimd
        def _(pool):
            step = Steps()
            nc.gpsimd.memset(c.ident[:], 0.0).then_inc(pool_step, 1)
            pool.wait_ge(pool_step, step.last())
            nc.gpsimd.affine_select(out=c.ident[:], in_=c.ident[:], compare_op=ALU.not_equal, fill=1.0,
                                    base=0, pattern=[[-1, P]], channel_multiplier=1).then_inc(pool_step, 1)
            pool.wait_ge(pool_step, step.last())
            nc.gpsimd.tensor_copy(c.ident16[:], c.ident[:])
            nc.gpsimd.memset(c.ones[:], 1.0)
            nc.gpsimd.memset(c.minus_half[:], -0.5)
            nc.gpsimd.iota(c.lane16[:], [[1, P]], base=0, channel_multiplier=0,
                           allow_small_or_imprecise_dtypes=True)


def fold_weights(nc, c, W, WT, a_src, a_dst, w_norm1, w_qkv, wall):
    with ExitStack() as ctx:
        sb = lambda name, shape, dt=F32: ctx.enter_context(nc.sbuf_tensor(name, shape, dt))
        sem = lambda name: ctx.enter_context(nc.semaphore(name))
        w_rows = sb("w_rows", [P, KC, D])
        att = sb("att", [P, KC, 2 * HEADS])
        norm1 = sb("norm1", [P, KC])
        weights_in, att_zero, att_in, folded, scaled = (
            sem("weights_in"), sem("att_zero"), sem("att_in"), sem("folded"), sem("scaled"))
        block = ctx.enter_context(nc.Block())

        @block.sync
        def _(sp):
            sp.dma_start(w_rows[:], W.rearrange("(c p) k -> p c k", p=P)).then_inc(weights_in, 16)
            sp.dma_start(wall[:, :, 0:D], WT.rearrange("(c p) n -> p c n", p=P)).then_inc(weights_in, 16)
            qkv = w_qkv.rearrange("(c p) n -> p c n", p=P)
            sp.dma_start(wall[:, :, COL_QK:COL_QK + 2 * D], qkv[:, :, 0:2 * D]).then_inc(weights_in, 16)
            sp.dma_start(wall[:, :, COL_V:COL_V + D], qkv[:, :, 2 * D:3 * D]).then_inc(weights_in, 16)
            sp.dma_start(norm1[:], w_norm1.rearrange("(c p) -> p c", p=P),
                         allow_slow_non_contiguous=True).then_inc(weights_in, 16)
            sp.wait_ge(att_zero, 1)
            for h in range(HEADS):
                rows = slice(HD * h % P, HD * h % P + HD)
                for j, a in enumerate((a_dst, a_src)):
                    sp.dma_start(att[rows, HD * h // P, j * HEADS + h:j * HEADS + h + 1],
                                 a[h, :].rearrange("(d o) -> d o", o=1),
                                 allow_slow_non_contiguous=True).then_inc(att_in, 16)

        @block.vector
        def _(dve):
            nc.vector.memset(att[:], 0.0).then_inc(att_zero, 1)
            dve.wait_ge(weights_in, 5 * 16)
            for k in range(KC):
                nc.vector.tensor_scalar(wall[:, k, COL_V:COL_S], wall[:, k, COL_V:COL_S], norm1[:, k:k + 1], None,
                                        ALU.mult).then_inc(scaled, 1)
            dve.wait_ge(folded, 1)
            nc.vector.tensor_copy(wall[:, :, COL_S:WALL], c.ps[0][:, 0:KC * 2 * HEADS].rearrange("p (k n) -> p k n", k=KC))

        @block.tensor
        def _(pe):
            pe.wait_ge(weights_in, 5 * 16)
            pe.wait_ge(att_in, 16 * 2 * HEADS)
            for k in range(KC):
                for m in range(KC):
                    last = nc.tensor.matmul(c.ps[0][:, k * 2 * HEADS:(k + 1) * 2 * HEADS],
                                            w_rows[:, m, k * P:(k + 1) * P], att[:, m, :],
                                            start=(m == 0), stop=(m == KC - 1))
            last.then_inc(folded, 1)


def project_nodes(nc, c, x, wall, hparts, htab, stab, qtab, xntab):
    with ExitStack() as ctx:
        sb = lambda name, shape, dt=F32: ctx.enter_context(nc.sbuf_tensor(name, shape, dt))
        sem = lambda name: ctx.enter_context(nc.semaphore(name))
        xt, xn = sb("xt", [P, 2, D]), sb("xn", [P, 2, D])
        xT = sb("xT", [P, 2, D])
        stats, mv = sb("stats", [P, 2, 6]), sb("mv", [P, 2, 2])
        rstd, ms, r1 = sb("rstd", [P, 2]), sb("ms", [P, 2]), sb("r1", [P, 2])
        hrow, rest = sb("hrow", [P, 2, HC]), sb("rest", [P, 2, HX])
        neg, pos, qk = sb("neg", [P, 2, 2 * D]), sb("pos", [P, 2, 2 * D]), sb("qk", [P, 2, 2 * D])
        v = sb("v", [P, 2, D])
        x_in = [sem(f"x_in{s}") for s in range(2)]
        x_used, xn_ready, r1_ready = sem("x_used"), sem("xn_ready"), sem("r1_ready")
        xT_made, xT_ready, proj_made = sem("xT_made"), sem("xT_ready"), sem("proj_made")
        hrow_ready, act_read, dve_read = sem("hrow_ready"), sem("act_read"), sem("dve_read")
        part1_ready, neg_ready, exp_ready = sem("part1_ready"), sem("neg_ready"), sem("exp_ready")
        parts_made, qk_ready, kv_used = sem("parts_made"), sem("qk_ready"), sem("kv_used")
        xn_out = [sem(f"xn_out{s}") for s in range(2)]
        h_out = [sem(f"h_out{s}") for s in range(2)]
        q_out = [sem(f"q_out{s}") for s in range(2)]
        mv_ready, rstd_ready, norm_step = sem("mv_ready"), sem("rstd_ready"), sem("norm_step")
        dve_step, pool_step = sem("dve_step"), sem("pool_step2")
        block = ctx.enter_context(nc.Block())

        xT_ps = [c.ps[b][:, 0:D] for b in (0, 1)]
        s_ps = [c.ps[b][:, D:D + 2 * HEADS] for b in (0, 1)]
        hv_ps = [c.ps[2], c.ps[3]]
        qk_ps = [c.ps[6], c.ps[7]]
        kv_ps = c.ps[4][:, :].rearrange("p (c n) -> p c n", c=KC)
        ksum_ps = c.ps[5][:, 0:D]

        def turns(eng, body):
            with eng.Fori(0, LAST // 2) as i:
                for s in range(2):
                    body(i * 2 + s, s, i, False)
            body(LAST, 0, LAST // 2, False)
            body(LAST + 1, 1, LAST // 2, True)

        @block.sync
        def _(sp):
            def load(t, s):
                sp.dma_start(xt[:, s, :], x[bass.ds(t * P, P), :]).then_inc(x_in[s], 16)

            load(0, 0)
            load(1, 1)

            def body(t, s, i, last):
                rows = bass.ds(t * P, P)
                sp.wait_ge(xn_ready, t + 1)
                sp.dma_start(xntab[rows, :], xn[:, s, :]).then_inc(xn_out[s], 16)
                if not (isinstance(t, int) and t >= LAST):
                    load(t + 2, s)
                sp.wait_ge(hrow_ready, t + 1)
                sp.dma_start(htab[rows, :], hrow[:, s, 0:D]).then_inc(h_out[s], 16)
                sp.dma_start(stab[rows, :], hrow[:, s, HX:HC]).then_inc(h_out[s], 16)
                sp.wait_ge(qk_ready, t + 1)
                sp.dma_start(qtab[rows, :], qk[:, s, 0:D]).then_inc(q_out[s], 16)

            turns(sp, body)
            for s in range(2):
                sp.wait_ge(xn_out[s], 16 * (NT // 2))
                sp.wait_ge(h_out[s], 32 * (NT // 2))
                sp.wait_ge(q_out[s], 16 * (NT // 2))

        @block.vector
        def _(dve):
            def normalise(t, s, i, reused):
                dve.wait_ge(x_in[s], 16 * (i + 1))
                nc.vector.bn_stats(stats[:, s, :], xt[:, s, :]).then_inc(dve_step, 1)
                wait_apart(dve, dve_step, t + 1, c.passed)
                nc.vector.bn_aggr(mv[:, s, :], stats[:, s, :]).then_inc(mv_ready, 1)
                if reused:
                    dve.wait_ge(xT_made, t - 1)
                    dve.wait_ge(xn_out[s], 16 * i)
                dve.wait_ge(rstd_ready, t + 1)
                nc.vector.tensor_scalar(xn[:, s, :], xt[:, s, :], mv[:, s, 0:1], rstd[:, s:s + 1],
                                        ALU.subtract, ALU.mult).then_inc(xn_ready, 1)
            def body(t, s, i, last):
                if not last:
                    reused = not (isinstance(t, int) and t < 1)
                    normalise(t + 1, 1 - s, i if s == 0 else i + 1, reused)
                dve.wait_ge(proj_made, t + 1)
                if not (isinstance(t, int) and t < 2):
                    dve.wait_ge(parts_made, t - 1)
                    dve.wait_ge(qk_ready, t - 1)
                nc.vector.tensor_scalar(neg[:, s, :], qk_ps[s][:], 0.0, None, ALU.min).then_inc(neg_ready, 1)
                dve.wait_ge(hrow_ready, t + 1)
                nc.vector.tensor_copy(hparts[:, bass.ds(t, 1), 0, :].rearrange("p o n -> p (o n)"),
                                      hrow[:, s, 0:HX]).then_inc(part1_ready, 1)

            normalise(0, 0, 0, False)
            body(0, 0, 0, False)
            body(1, 1, 0, False)
            with dve.Fori(1, LAST // 2) as i:
                for s in range(2):
                    body(i * 2 + s, s, i, False)
            body(LAST, 0, LAST // 2, False)
            body(LAST + 1, 1, LAST // 2, True)

        @block.tensor
        def _(pe):
            def transpose_x(t, s, reused=True):
                pe.wait_ge(xn_ready, t + 1)
                if reused:
                    pe.wait_ge(act_read, t - 1)
                for k in range(KC):
                    last = nc.tensor.transpose(xT_ps[s][:, k * P:(k + 1) * P], xn[:, s, k * P:(k + 1) * P],
                                               c.ident[:])
                last.then_inc(xT_made, 1)

            def project(t, s, reused=True):
                pe.wait_ge(xT_ready, t + 1)
                if reused:
                    pe.wait_ge(act_read, t - 1)
                    pe.wait_ge(neg_ready, t - 1)
                for out, lo, n in ((hv_ps[s][:, :], 0, 2 * D), (s_ps[s], COL_S, 2 * HEADS), (qk_ps[s][:, :], COL_QK, 2 * D)):
                    for k in range(KC):
                        last = nc.tensor.matmul(out, xT[:, s, k * P:(k + 1) * P], wall[:, k, lo:lo + n],
                                                start=(k == 0), stop=(k == KC - 1))
                last.then_inc(proj_made, 1)

            def sum_kv(t, s, rows, first=False, last=False):
                pe.wait_ge(qk_ready, t + 1)
                for m in range(KC):
                    nc.tensor.matmul(kv_ps[:, m, :], v[0:rows, s, m * P:(m + 1) * P], qk[0:rows, s, D:2 * D],
                                     start=(first and m == 0), stop=last, skip_group_check=True)
                nc.tensor.matmul(ksum_ps, c.ones[0:rows, :], qk[0:rows, s, D:2 * D], start=first, stop=last,
                                 skip_group_check=True).then_inc(kv_used, 1)

            transpose_x(0, 0, False)
            transpose_x(1, 1, False)
            project(0, 0, False)
            transpose_x(2, 0)
            project(1, 1, False)
            sum_kv(0, 0, P, first=True)
            with pe.Fori(1, LAST // 2) as i:
                for s in range(2):
                    t = i * 2 + s
                    transpose_x(t + 1, 1 - s)
                    project(t, s)
                    sum_kv(t - 1, 1 - s, P)
            transpose_x(LAST + 1, 1)
            project(LAST, 0)
            sum_kv(LAST - 1, 1, P)
            project(LAST + 1, 1)
            sum_kv(LAST, 0, LAST_ROWS, last=True)

        @block.scalar
        def _(act):
            def copy_xT(t, s, reused=True):
                act.wait_ge(xT_made, t + 1)
                if reused:
                    act.wait_ge(proj_made, t - 1)
                nc.scalar.copy(xT[:, s, :], xT_ps[s]).then_inc(xT_ready, 1)

            def evacuate(t, s, i, reused=True):
                act.wait_ge(proj_made, t + 1)
                if reused:
                    act.wait_ge(h_out[s], 32 * i)
                    act.wait_ge(parts_made, t - 1)
                nc.scalar.copy(hrow[:, s, D:HC], s_ps[s])
                nc.scalar.copy(hrow[:, s, 0:D], hv_ps[s][:, 0:D]).then_inc(hrow_ready, 1)
                act.wait_ge(r1_ready, t + 1)
                if reused:
                    act.wait_ge(qk_ready, t - 1)
                    act.wait_ge(kv_used, t - 1)
                nc.scalar.activation(v[:, s, :], hv_ps[s][:, D:2 * D], ACT.Copy, scale=r1[:, s:s + 1])
                act.wait_ge(neg_ready, t + 1)
                nc.scalar.activation(pos[:, s, :], qk_ps[s][:], ACT.Relu, scale=r1[:, s:s + 1])
                nc.scalar.activation(neg[:, s, :], neg[:, s, :], ACT.Exp, scale=r1[:, s:s + 1]).then_inc(exp_ready, 1)
                act.wait_ge(exp_ready, t + 1)
                act.sem_inc(act_read, 1)

            copy_xT(0, 0, False)
            copy_xT(1, 1, False)
            evacuate(0, 0, 0, False)
            copy_xT(2, 0)
            evacuate(1, 1, 0, False)
            with act.Fori(1, LAST // 2) as i:
                for s in range(2):
                    t = i * 2 + s
                    copy_xT(t + 1, 1 - s)
                    evacuate(t, s, i)
            copy_xT(LAST + 1, 1)
            evacuate(LAST, 0, LAST // 2)
            evacuate(LAST + 1, 1, LAST // 2)

        @block.gpsimd
        def _(pool):
            def inverse_norms(t, s, reused=True):
                step = Steps(t * 4)
                wait_apart(pool, mv_ready, t + 1, c.passed)
                nc.gpsimd.tensor_scalar(rstd[:, s:s + 1], mv[:, s, 1:2], LN_EPS, None,
                                        ALU.add).then_inc(norm_step, 1)
                pool.wait_ge(norm_step, step.last())
                nc.gpsimd.tensor_tensor(rstd[:, s:s + 1], rstd[:, s:s + 1], c.minus_half[:],
                                        ALU.pow).then_inc(rstd_ready, 1)
                pool.wait_ge(rstd_ready, t + 1)
                nc.gpsimd.tensor_tensor(ms[:, s:s + 1], rstd[:, s:s + 1], rstd[:, s:s + 1],
                                        ALU.mult).then_inc(norm_step, 1)
                pool.wait_ge(norm_step, step.last())
                nc.gpsimd.tensor_tensor(ms[:, s:s + 1], ms[:, s:s + 1], mv[:, s, 1:2],
                                        ALU.mult).then_inc(norm_step, 1)
                if reused:
                    pool.wait_ge(act_read, t - 1)
                wait_apart(pool, norm_step, step.last(), c.passed)
                nc.gpsimd.tensor_scalar(ms[:, s:s + 1], ms[:, s:s + 1], RMS_EPS, None,
                                        ALU.add).then_inc(norm_step, 1)
                pool.wait_ge(norm_step, step.last())
                nc.gpsimd.tensor_tensor(r1[:, s:s + 1], ms[:, s:s + 1], c.minus_half[:],
                                        ALU.pow).then_inc(r1_ready, 1)

            def body(t, s, i, reused=True, last=False):
                if not last:
                    inverse_norms(t + 1, 1 - s, reused or t == 1)
                step = Steps(t * 2)
                part = lambda j: hparts[:, bass.ds(t, 1), j, :].rearrange("p o n -> p (o n)")
                pool.wait_ge(exp_ready, t + 1)
                if reused:
                    pool.wait_ge(kv_used, t - 1)
                    pool.wait_ge(q_out[s], 16 * i)
                nc.gpsimd.tensor_tensor(qk[:, s, :], pos[:, s, :], neg[:, s, :], ALU.add).then_inc(qk_ready, 1)
                pool.wait_ge(hrow_ready, t + 1)
                pool.wait_ge(part1_ready, t + 1)
                nc.gpsimd.tensor_tensor(rest[:, s, :], hrow[:, s, 0:HX], part(0), ALU.subtract).then_inc(pool_step, 1)
                pool.wait_ge(pool_step, step.last())
                nc.gpsimd.tensor_copy(part(1), rest[:, s, :]).then_inc(pool_step, 1)
                pool.wait_ge(pool_step, step.last())
                nc.gpsimd.tensor_tensor(part(2), rest[:, s, :], part(1), ALU.subtract).then_inc(parts_made, 1)

            inverse_norms(0, 0, False)
            body(0, 0, 0, False)
            body(1, 1, 0, False)
            with pool.Fori(1, LAST // 2) as i:
                for s in range(2):
                    body(i * 2 + s, s, i)
            body(LAST, 0, LAST // 2)
            body(LAST + 1, 1, LAST // 2, last=True)


def wait_apart(eng, sem, value, passed):
    eng.wait_ge(sem, value)
    if not isinstance(value, int):
        eng.sem_inc(passed, 1)


def again(t, k):
    return not isinstance(t, int) or t >= k


def pipeline(eng, n, stages, unroll=2):
    far = max(lag for lag, _ in stages)

    def turn(T, r, j):
        for lag, fn in stages:
            t = T - lag if isinstance(T, int) else T + (r - lag)
            if not isinstance(T, int) or 0 <= t < n:
                fn(t, (r - lag) % unroll, j + (r - lag) // unroll)

    first = -(-(far + 4) // unroll) * unroll
    end = n // unroll * unroll
    for T in range(first):
        turn(T, T % unroll, T // unroll)
    with eng.Fori(first // unroll, end // unroll) as j:
        for r in range(unroll):
            turn(j * unroll, r, j)
    for T in range(end, n + far):
        turn(T, T % unroll, T // unroll)


def mix_nodes(nc, c, x, bias, w_out, b_out, w_norm2, qtab, xntab, ytab):
    with ExitStack() as ctx:
        sb = lambda name, shape, dt=F32: ctx.enter_context(nc.sbuf_tensor(name, shape, dt))
        sem = lambda name: ctx.enter_context(nc.semaphore(name))
        wo = sb("wo", [P, KC, D])
        rows_in = sb("rows_in", [P, 3, D])
        kv, mix, ksum = sb("kv", [P, KC, P]), sb("mix", [P, KC, D]), sb("ksum", [P, D])
        q, xn, xt = sb("q2", [P, 2, D]), sb("xn2", [P, 2, D]), sb("xt2", [P, 2, D])
        prod, qz = sb("prod", [P, 2, D]), sb("qz", [P, 2, D])
        den, z = sb("den", [P, 2, HEADS]), sb("z", [P, 2, HEADS])
        qT = sb("qT", [P, 2, D])
        h, junk = sb("h2", [P, 2, D]), sb("junk", [P, 2, D])
        ss, r2 = sb("ss", [P, 2]), sb("r2", [P, 2])
        y = sb("y", [P, 2, D])
        setup_in, kv_zero, kv_ready, mix_made, mix_ready = (
            sem("setup_in"), sem("kv_zero"), sem("kv_ready"), sem("mix_made"), sem("mix_ready"))
        tile_in = [sem(f"tile_in{s}") for s in range(2)]
        y_out = [sem(f"y_out{s}") for s in range(2)]
        prod_ready, dve_step = sem("prod_ready"), sem("dve_step3")
        biased, mean_ready = sem("biased"), sem("mean_ready")
        qz_ready, qT_made, qT_ready, att_made = sem("qz_ready"), sem("qT_made"), sem("qT_ready"), sem("att_made")
        based, h_ready, ss_ready, r2_ready = sem("based"), sem("h_ready"), sem("ss_ready"), sem("r2_ready")
        hb_ready, y_ready = sem("hb_ready"), sem("y_ready")
        block = ctx.enter_context(nc.Block())
        kv_ps = c.ps[4][:, :].rearrange("p (c n) -> p c n", c=KC)
        ksum_ps = c.ps[5][:, 0:D]
        mix_ps = c.ps[0][:, :].rearrange("p (c n) -> p c n", c=KC)
        qT_ps = [c.ps[b][:, 0:D] for b in (1, 2)]
        att_ps = [c.ps[b][:, 0:D] for b in (3, 6)]
        heads = lambda ap: ap.rearrange("p (h d) -> p h d", h=HEADS)

        @block.sync
        def _(sp):
            sp.dma_start(wo[:], w_out.rearrange("(c p) n -> p c n", p=P)).then_inc(setup_in, 16)
            for j, row in enumerate((bias, b_out, w_norm2)):
                sp.dma_start(rows_in[:, j, :], row.rearrange("(o d) -> o d", o=1).broadcast_to([P, D])
                             ).then_inc(setup_in, 16)

            def load(t, s, i):
                if again(t, 2):
                    sp.wait_ge(based, t - 1)
                    sp.wait_ge(qz_ready, t - 1)
                for buf, table in ((q, qtab), (xn, xntab), (xt, x)):
                    sp.dma_start(buf[:, s, :], table[bass.ds(t * P, P), :]).then_inc(tile_in[s], 16)

            def store(t, s, i):
                sp.wait_ge(y_ready, t + 1)
                sp.dma_start(ytab[bass.ds(t * P, P), :], y[:, s, :]).then_inc(y_out[s], 16)

            pipeline(sp, NT, [(0, load), (3, store)])
            for s in range(2):
                sp.wait_ge(y_out[s], 16 * (NT // 2))

        @block.gpsimd
        def _(pool):
            pool.wait_ge(setup_in, 4 * 16)
            pool.wait_ge(mix_ready, 1)

            def sums(t, s, i):
                pool.wait_ge(tile_in[s], 48 * (i + 1))
                if again(t, 2):
                    pool.wait_ge(qz_ready, t - 1)
                nc.gpsimd.tensor_tensor(prod[:, s, :], q[:, s, :], ksum[:], ALU.mult).then_inc(prod_ready, 1)
                nc.gpsimd.tensor_tensor(xn[:, s, :], xn[:, s, :], rows_in[:, 1, :], ALU.add)
                nc.gpsimd.tensor_tensor(xt[:, s, :], xt[:, s, :], rows_in[:, 0, :], ALU.add).then_inc(biased, 1)

            def norm(t, s, i):
                pool.wait_ge(h_ready, t + 1)
                if again(t, 2):
                    pool.wait_ge(y_ready, t - 1)
                    pool.wait_ge(y_out[s], 16 * i)
                pool.wait_ge(biased, t + 1)
                nc.gpsimd.tensor_tensor(y[:, s, :], h[:, s, :], xt[:, s, :], ALU.add).then_inc(based, 1)
                wait_apart(pool, ss_ready, t + 1, c.passed)
                nc.gpsimd.tensor_scalar(r2[:, s:s + 1], ss[:, s:s + 1], 1.0 / D, RMS_EPS, ALU.mult,
                                        ALU.add).then_inc(mean_ready, 1)
                pool.wait_ge(mean_ready, t + 1)
                nc.gpsimd.tensor_tensor(r2[:, s:s + 1], r2[:, s:s + 1], c.minus_half[:],
                                        ALU.pow).then_inc(r2_ready, 1)

            pipeline(pool, NT, [(0, sums), (1, norm)])

        @block.vector
        def _(dve):
            nc.vector.memset(kv[:], 0.0).then_inc(kv_zero, 1)
            dve.wait_ge(kv_zero, 1)
            for hd in range(HEADS):
                rows, lo = slice(HD * hd % P, HD * hd % P + HD), HD * hd % P
                nc.vector.tensor_copy(kv[rows, HD * hd // P, lo:lo + HD],
                                      kv_ps[rows, HD * hd // P, HD * hd:HD * hd + HD]).then_inc(kv_ready, 1)
            nc.vector.tensor_copy(ksum[:], ksum_ps)
            dve.wait_ge(mix_made, 1)
            nc.vector.tensor_copy(mix[:], mix_ps).then_inc(mix_ready, 1)

            def weigh(t, s, i):
                dve.wait_ge(prod_ready, t + 1)
                nc.vector.tensor_reduce(den[:, s, :], heads(prod[:, s, :]), AX.X, ALU.add).then_inc(dve_step, 1)
                dve.wait_ge(dve_step, 3 * t + 1)
                nc.vector.tensor_scalar(den[:, s, :], den[:, s, :], ATT_EPS, None, ALU.add).then_inc(dve_step, 1)
                dve.wait_ge(dve_step, 3 * t + 2)
                nc.vector.reciprocal(z[:, s, :], den[:, s, :]).then_inc(dve_step, 1)
                dve.wait_ge(dve_step, 3 * t + 3)
                if again(t, 2):
                    dve.wait_ge(qT_made, t - 1)
                nc.vector.tensor_tensor(heads(qz[:, s, :]), heads(q[:, s, :]),
                                        z[:, s, :].unsqueeze(2).broadcast_to([P, HEADS, HD]),
                                        ALU.mult).then_inc(qz_ready, 1)

            def add_residual(t, s, i):
                dve.wait_ge(att_made, t + 1)
                if again(t, 2):
                    dve.wait_ge(y_ready, t - 1)
                    dve.wait_ge(ss_ready, t - 1)
                dve.wait_ge(biased, t + 1)
                nc.vector.tensor_tensor(h[:, s, :], att_ps[s], xn[:, s, :], ALU.add).then_inc(h_ready, 1)

            def finish(t, s, i):
                dve.wait_ge(r2_ready, t + 1)
                nc.vector.scalar_tensor_tensor(out=h[:, s, :], in0=h[:, s, :], scalar=r2[:, s:s + 1],
                                               in1=rows_in[:, 2, :], op0=ALU.mult, op1=ALU.mult
                                               ).then_inc(hb_ready, 1)
                dve.wait_ge(hb_ready, t + 1)
                nc.vector.tensor_tensor(y[:, s, :], y[:, s, :], h[:, s, :], ALU.add).then_inc(y_ready, 1)

            pipeline(dve, NT, [(0, weigh), (1, add_residual), (2, finish)])

        @block.tensor
        def _(pe):
            pe.wait_ge(kv_ready, HEADS)
            pe.wait_ge(setup_in, 4 * 16)
            for m in range(KC):
                last = nc.tensor.matmul(mix_ps[:, m, :], kv[:, m, :], wo[:, m, :], start=True, stop=True)
            last.then_inc(mix_made, 1)
            pe.wait_ge(mix_ready, 1)

            def transpose_q(t, s, i):
                pe.wait_ge(qz_ready, t + 1)
                if again(t, 2):
                    pe.wait_ge(qT_ready, t - 1)
                for k in range(KC):
                    last = nc.tensor.transpose(qT_ps[s][:, k * P:(k + 1) * P], qz[:, s, k * P:(k + 1) * P],
                                               c.ident[:])
                last.then_inc(qT_made, 1)

            def attend(t, s, i):
                pe.wait_ge(qT_ready, t + 1)
                if again(t, 2):
                    pe.wait_ge(h_ready, t - 1)
                for k in range(KC):
                    last = nc.tensor.matmul(att_ps[s], qT[:, s, k * P:(k + 1) * P], mix[:, k, :],
                                            start=(k == 0), stop=(k == KC - 1))
                last.then_inc(att_made, 1)

            pipeline(pe, NT, [(0, transpose_q), (1, attend)])

        @block.scalar
        def _(act):
            def copy_qT(t, s, i):
                act.wait_ge(qT_made, t + 1)
                if again(t, 2):
                    act.wait_ge(att_made, t - 1)
                nc.scalar.copy(qT[:, s, :], qT_ps[s]).then_inc(qT_ready, 1)

            def squares(t, s, i):
                act.wait_ge(h_ready, t + 1)
                if again(t, 2):
                    act.wait_ge(r2_ready, t - 1)
                nc.scalar.activation(junk[:, s, :], h[:, s, :], ACT.Square,
                                     accum_out=ss[:, s:s + 1]).then_inc(ss_ready, 1)

            pipeline(act, NT, [(0, copy_qT), (1, squares)])


def plan_steps(nc, c, dst_t, src_t, attr_t, edge_w, wparts, dl, src, keys, blocks, block_row,
               attr_parts):
    with ExitStack() as ctx:
        sb = lambda name, shape, dt=F32: ctx.enter_context(nc.sbuf_tensor(name, shape, dt))
        sem = lambda name: ctx.enter_context(nc.semaphore(name))
        rows = ET // COUNT_P
        all_i, all_f = sb("all_i", [COUNT_P, rows * P], I32), sb("all_f", [COUNT_P, rows * P])
        below = sb("below", [COUNT_P, 2, rows * P], BF16)
        part = sb("part", [COUNT_P, NT])
        count = sb("count", [P, NT])
        ci, lo, hi = sb("ci", [P, NT], I32), sb("lo", [P, NT], I32), sb("hi", [P, NT], I32)
        steps_i = sb("steps_i", [P, NT], I32)
        lof, nsteps, some = sb("lof", [P, NT]), sb("nsteps", [P, NT]), sb("some", [P, NT])
        ends, starts = sb("ends", [P, NT]), sb("starts", [P, NT])
        base, dbase = sb("base", [P, NT]), sb("dbase", [P, NT])
        zero = sb("zero", [P, NT])
        pid = sb("pid", [P, SG])
        reached = sb("reached", [P, SG, 2, NT])
        nblocks, tbase, live = sb("nblocks", [P, SG]), sb("tbase", [P, SG]), sb("live", [P, SG])
        block_f, tile_f = sb("block_f", [P, SG]), sb("tile_f", [P, SG])
        block_i, tiles_i = sb("block_i", [P, SG], I32), sb("tiles_i", [P, SG, 2], I32)
        first_node = sb("first_node", [P, SG])
        dst_i, src_i = sb("dst_i", [P, 2 * SG, P], I32), sb("src_i", [P, 2 * SG, P], I32)
        dst_f, src_f = sb("dst_f", [P, 2 * SG, P]), sb("src_f", [P, 2 * SG, P])
        own = sb("own", [P, 2 * SG, P])
        attr = sb("attr", [P, 2 * SG, 4 * P])
        rest = sb("attr_rest", [P, 4 * P])
        split = sb("split", [P, SG, 3, 4, 2 * P], BF16)
        ew, ew_rest = sb("ew", [4, D]), sb("ew_rest", [4, D])
        ew_parts = sb("ew_parts", [4, 3, D], BF16)
        loaded, step_sem, counted, summed = sem("loaded"), sem("plan_step"), sem("counted"), sem("summed")
        tiles_ready, blocks_ready, tables_in = sem("tiles_ready"), sem("blocks_ready"), sem("tables_in")
        iota_ready, attr_in, split_ready = sem("iota_ready"), sem("attr_in"), sem("split_ready")
        fields_ready, turned, taken, stored = sem("fields_ready"), sem("turned"), sem("taken"), sem("stored")
        ew_ready, wparts_in = sem("ew_ready"), sem("wparts_in")
        block = ctx.enter_context(nc.Block())

        @block.sync
        def _(sp):
            sp.dma_start(all_i[:], dst_t.rearrange("(p r) e -> p (r e)", p=COUNT_P)).then_inc(loaded, 16)
            sp.dma_start(ew[:], edge_w).then_inc(loaded, 16)
            sp.wait_ge(ew_ready, 3)
            for j in range(3):
                for i in range(3):
                    row = (j * 3 + i) * 4
                    sp.dma_start(wparts[row:row + 4, :], ew_parts[:, j, :]).then_inc(wparts_in, 16)
            sp.wait_ge(blocks_ready, 1)
            sp.dma_start(blocks.rearrange("o (g p) -> p (o g)", p=P), block_i[:],
                         allow_slow_non_contiguous=True).then_inc(stored, 16)
            sp.wait_ge(stored, 16)
            sp.dma_start(block_row[:], blocks).then_inc(stored, 16)
            for g in range(SG):
                sp.wait_ge(split_ready, g + 1)
                for i in range(3):
                    sp.dma_start(attr_parts[i * 4:i * 4 + 4, g * P:(g + 1) * P, :].rearrange("c p e -> p c e"),
                                 split[:, g, i, :, :]).then_inc(stored, 16)
            sp.wait_ge(stored, 16 * (2 + 3 * SG))
            sp.wait_ge(wparts_in, 9 * 16)

        @block.gpsimd
        def _(pool):
            nc.gpsimd.iota(pid[:], [[P, SG]], base=0, channel_multiplier=1,
                           allow_small_or_imprecise_dtypes=True).then_inc(iota_ready, 1)
            pool.wait_ge(tiles_ready, 1)
            for g in range(SG):
                for e in range(2):
                    at = bass.IndirectOffsetOnAxis(ap=tiles_i[:, g, e:e + 1], axis=0)
                    j = 2 * g + e
                    nc.gpsimd.indirect_dma_start(dst_i[:, j, :], None, dst_t, at).then_inc(tables_in, 16)
                    nc.gpsimd.indirect_dma_start(src_i[:, j, :], None, src_t, at).then_inc(tables_in, 16)
                    nc.gpsimd.indirect_dma_start(attr[:, j, :], None, attr_t, at).then_inc(attr_in, 16)

        @block.vector
        def _(dve):
            step = Steps()

            def done(ins):
                ins.then_inc(step_sem, 1)
                dve.wait_ge(step_sem, step.last())

            V = nc.vector
            dve.wait_ge(loaded, 32)
            V.tensor_copy(ew_parts[:, 0, :], ew[:]).then_inc(ew_ready, 1)
            dve.wait_ge(ew_ready, 1)
            done(V.tensor_tensor(ew_rest[:], ew[:], ew_parts[:, 0, :], ALU.subtract))
            V.tensor_copy(ew_parts[:, 1, :], ew_rest[:]).then_inc(ew_ready, 1)
            dve.wait_ge(ew_ready, 2)
            V.tensor_tensor(ew_parts[:, 2, :], ew_rest[:], ew_parts[:, 1, :], ALU.subtract).then_inc(ew_ready, 1)
            done(V.memset(zero[:], 0.0))
            done(V.tensor_copy(all_f[:], all_i[:]))
            for b in range(NT):
                if b >= 2:
                    dve.wait_ge(counted, b - 1)
                V.tensor_scalar(below[:, b % 2, :], all_f[:], float(b * P), 0.0, ALU.is_lt, ALU.add,
                                accum_out=part[:, b:b + 1]).then_inc(counted, 1)
            dve.wait_ge(summed, 1)
            done(V.tensor_copy(count[:], c.ps[0][:, 0:NT]))
            done(V.tensor_copy(ci[:], count[:]))
            B = NT - 1
            done(V.tensor_single_scalar(lo[:], ci[:], 7, ALU.arith_shift_right))
            done(V.tensor_scalar(count[:], count[:], 127.0, None, ALU.add))
            done(V.tensor_copy(ci[:], count[:]))
            done(V.tensor_single_scalar(hi[:], ci[:], 7, ALU.arith_shift_right))
            done(V.tensor_copy(lof[:], lo[:]))
            done(V.tensor_copy(nsteps[:], hi[:]))
            done(V.tensor_tensor(some[:, 0:B], count[:, 1:NT], count[:, 0:B], ALU.is_gt))
            done(V.tensor_tensor(ends[:, 0:B], nsteps[:, 1:NT], lof[:, 0:B], ALU.subtract))
            done(V.tensor_tensor(ends[:, 0:B], ends[:, 0:B], some[:, 0:B], ALU.mult))
            done(V.tensor_scalar(ends[:, 0:B], ends[:, 0:B], 1.0, None, ALU.add))
            done(V.tensor_copy(steps_i[:, 0:B], ends[:, 0:B]))
            done(V.tensor_single_scalar(steps_i[:, 0:B], steps_i[:, 0:B], 1, ALU.arith_shift_right))
            done(V.tensor_copy(nsteps[:, 0:B], steps_i[:, 0:B]))
            done(V.tensor_tensor_scan(ends[:, 0:B], nsteps[:, 0:B], zero[:, 0:B], 0.0, ALU.add, ALU.add))
            done(V.tensor_tensor(starts[:, 0:B], ends[:, 0:B], nsteps[:, 0:B], ALU.subtract))
            done(V.scalar_tensor_tensor(out=base[:, 0:B], in0=starts[:, 0:B], scalar=-2.0, in1=lof[:, 0:B],
                                        op0=ALU.mult, op1=ALU.add))
            done(V.tensor_copy(dbase[:, 0:1], base[:, 0:1]))
            done(V.tensor_tensor(dbase[:, 1:B], base[:, 1:B], base[:, 0:B - 1], ALU.subtract))
            dve.wait_ge(iota_ready, 1)
            for g in range(SG):
                done(V.tensor_scalar(reached[:, g, 0, 0:B], starts[:, 0:B], pid[:, g:g + 1], None, ALU.is_le))
                done(V.tensor_tensor(reached[:, g, 1, 0:B], reached[:, g, 0, 0:B], dbase[:, 0:B], ALU.mult))
                done(V.tensor_reduce(nblocks[:, g:g + 1], reached[:, g, 0, 0:B], AX.X, ALU.add))
                done(V.tensor_reduce(tbase[:, g:g + 1], reached[:, g, 1, 0:B], AX.X, ALU.add))
            done(V.tensor_scalar(live[:], pid[:], ends[:, B - 1:B], None, ALU.is_lt))
            done(V.tensor_scalar(block_f[:], nblocks[:], -1.0 - B, None, ALU.add))
            done(V.tensor_tensor(block_f[:], block_f[:], live[:], ALU.mult))
            done(V.tensor_scalar(block_f[:], block_f[:], float(B), None, ALU.add))
            done(V.scalar_tensor_tensor(out=tile_f[:], in0=pid[:], scalar=2.0, in1=tbase[:], op0=ALU.mult,
                                        op1=ALU.add))
            done(V.tensor_scalar(tile_f[:], tile_f[:], -(ET - 2.0), None, ALU.add))
            done(V.tensor_tensor(tile_f[:], tile_f[:], live[:], ALU.mult))
            done(V.tensor_scalar(tile_f[:], tile_f[:], ET - 2.0, None, ALU.add))
            V.tensor_copy(block_i[:], block_f[:]).then_inc(blocks_ready, 1)
            done(V.tensor_copy(tiles_i[:, :, 0], tile_f[:]))
            done(V.tensor_scalar(tile_f[:], tile_f[:], 1.0, None, ALU.add))
            V.tensor_copy(tiles_i[:, :, 1], tile_f[:]).then_inc(tiles_ready, 1)
            done(V.tensor_scalar(first_node[:], block_f[:], float(P), None, ALU.mult))
            dve.wait_ge(tables_in, 4 * SG * 16)
            done(V.tensor_copy(dst_f[:], dst_i[:]))
            V.tensor_copy(src_f[:], src_i[:]).then_inc(fields_ready, 1)
            for g in range(SG):
                own_g, dst_g = own[:, 2 * g:2 * g + 2, :], dst_f[:, 2 * g:2 * g + 2, :]
                done(V.tensor_scalar(dst_g, dst_g, first_node[:, g:g + 1], None, ALU.subtract))
                done(V.tensor_scalar(own_g, dst_g, 0.0, None, ALU.is_ge))
                done(V.scalar_tensor_tensor(out=own_g, in0=dst_g, scalar=float(P), in1=own_g, op0=ALU.is_lt,
                                            op1=ALU.mult))
                done(V.tensor_scalar(first_node[:, g:g + 1], first_node[:, g:g + 1], 1.0, None, ALU.add))
                V.scalar_tensor_tensor(out=own_g, in0=dst_g, scalar=first_node[:, g:g + 1], in1=own_g,
                                       op0=ALU.add, op1=ALU.mult).then_inc(fields_ready, 1)
            for g in range(SG):
                lo_, hi_ = g * P, min(NS, (g + 1) * P)
                dve.wait_ge(turned, g + 1)
                for j, (field, out) in enumerate(((0, dl), (1, src), (2, keys))):
                    bank = c.ps[1 + 3 * (g % 2) + j][:, 0:2 * P].rearrange("p (e n) -> p n e", e=2)
                    done(V.tensor_copy(out[:, lo_:hi_, :], bank[:, 0:hi_ - lo_, :]))
                dve.sem_inc(taken, 1)
            dve.wait_ge(attr_in, 2 * SG * 16)
            for g in range(SG):
                for e in range(2):
                    a = attr[:, 2 * g + e, :]
                    cut = lambda i: split[:, g, i, :, e * P:(e + 1) * P]
                    r = rest[:].rearrange("p (c e) -> p c e", c=4)
                    a = a.rearrange("p (c e) -> p c e", c=4)
                    done(V.tensor_copy(cut(0), a))
                    done(V.tensor_tensor(r, a, cut(0), ALU.subtract))
                    done(V.tensor_copy(cut(1), r))
                    done(V.tensor_tensor(cut(2), r, cut(1), ALU.subtract))
                dve.sem_inc(split_ready, 1)

        @block.tensor
        def _(pe):
            pe.wait_ge(counted, NT)
            nc.tensor.matmul(c.ps[0][:, 0:NT], c.ones[0:COUNT_P, :], part[:], start=True, stop=True
                             ).then_inc(summed, 1)
            pe.wait_ge(fields_ready, 1 + SG)
            for g in range(SG):
                if g >= 2:
                    pe.wait_ge(taken, g - 1)
                for j, field in enumerate((dst_f, src_f, own)):
                    for e in range(2):
                        last = nc.tensor.transpose(c.ps[1 + 3 * (g % 2) + j][:, e * P:(e + 1) * P],
                                                   field[:, 2 * g + e, :], c.ident[:])
                last.then_inc(turned, 1)


QUAD = 4
TILES = 2 * QUAD
NQ = NS // QUAD
assert NS % QUAD == 0


def load_blocks(eng, block_row, q):
    return [eng.value_load(block_row[0:1, bass.ds(q * QUAD + k, 1)], min_val=0, max_val=NT - 1)
            for k in range(QUAD)]


def score_edges(nc, c, wparts, hparts, stab, attr_parts, dl, src, block_row, alpha):
    with ExitStack() as ctx:
        sb = lambda name, shape, dt=F32: ctx.enter_context(nc.sbuf_tensor(name, shape, dt))
        sem = lambda name: ctx.enter_context(nc.semaphore(name))
        att = sb("att_cols", [36, 2, QUAD * 2 * P], BF16)
        onehot, onehotT = sb("onehot", [P, 2, TILES, P], BF16), sb("onehotT", [P, 2, TILES, P], BF16)
        stage, ssrc = sb("src_stage", [P, 2, TILES], I32), sb("ssrc", [P, 2, TILES, HEADS])
        enc, prod = sb("enc", [P, 2, 2 * D]), sb("eprod", [P, 2, 2 * D])
        red = sb("red", [P, 2, TILES, HEADS])
        att_in = [sem(f"attr_in{s}") for s in range(2)]
        ssrc_in = [sem(f"ssrc_in{s}") for s in range(2)]
        staged, onehot_ready, turned, onehotT_ready = (
            sem("staged"), sem("onehot_ready"), sem("onehot_turned"), sem("onehotT_ready"))
        enc_made, enc_ready, hdst_made, prod_ready = (
            sem("enc_made"), sem("enc_ready"), sem("hdst_made"), sem("eprod_ready"))
        red_ready, sum_step, alpha_ready = sem("red_ready"), sem("sum_step"), sem("alpha_ready")
        block = ctx.enter_context(nc.Block())
        turn_ps = [c.ps[b][:, :].bitcast(BF16).rearrange("p (k e) -> p k e", k=TILES) for b in (0, 1)]
        enc_ps, hdst_ps = [c.ps[2], c.ps[3]], [c.ps[4], c.ps[5]]
        sdst_ps = [c.ps[b][:, 0:TILES * HEADS] for b in (6, 7)]

        @block.sync
        def _(sp):
            def load(q, s, i):
                if again(q, 2):
                    sp.wait_ge(enc_made, QUAD * (q - 1))
                for j in range(3):
                    sp.dma_start(att[12 * j:12 * j + 12, s, :],
                                 attr_parts[:, bass.ds(q * QUAD, QUAD), :].rearrange("c p e -> c (p e)")
                                 ).then_inc(att_in[s], 16)

            pipeline(sp, NQ, [(0, load)])

        @block.gpsimd
        def _(pool):
            def gather(q, s, i):
                if again(q, 2):
                    pool.wait_ge(ssrc_in[s], 16 * TILES * i)
                    pool.wait_ge(alpha_ready, q - 1)
                nc.gpsimd.tensor_copy(stage[:, s, :], src[:, bass.ds(q * QUAD, QUAD), :].rearrange(
                    "p n e -> p (n e)")).then_inc(staged, 1)
                wait_apart(pool, staged, q + 1, c.passed)
                for k in range(TILES):
                    nc.gpsimd.indirect_dma_start(
                        ssrc[:, s, k, :], None, stab,
                        bass.IndirectOffsetOnAxis(ap=stage[:, s, k:k + 1], axis=0)).then_inc(ssrc_in[s], 16)

            pipeline(pool, NQ, [(0, gather)])

        @block.tensor
        def _(pe):
            def turn(q, s, i):
                pe.wait_ge(onehot_ready, q + 1)
                if again(q, 2):
                    pe.wait_ge(onehotT_ready, q - 1)
                for k in range(TILES):
                    last = nc.tensor.transpose(turn_ps[s][:, k, :], onehot[:, s, k, :], c.ident16[:])
                last.then_inc(turned, 1)

            def expand(q, s, i):
                blk = load_blocks(pe, block_row, q)
                pe.wait_ge(att_in[s], 48 * (i + 1))
                pe.wait_ge(onehotT_ready, q + 1)
                if again(q, 2):
                    pe.wait_ge(alpha_ready, q - 1)
                for k in range(QUAD):
                    u, b = q * QUAD + k, k % 2
                    if again(u, 2):
                        pe.wait_ge(enc_ready, u - 1)
                    for e in range(2):
                        t = 2 * k + e
                        last = nc.tensor.matmul(enc_ps[b][:, e * D:(e + 1) * D], att[:, s, t * P:(t + 1) * P],
                                                wparts[:], start=True, stop=True)
                    last.then_inc(enc_made, 1)
                    if again(u, 2):
                        pe.wait_ge(prod_ready, u - 1)
                    rows = lambda j, lo, hi: hparts[:, bass.ds(blk[k], 1), j, lo:hi].rearrange("p o n -> p (o n)")
                    for e in range(2):
                        t = 2 * k + e
                        for j in range(3):
                            nc.tensor.matmul(hdst_ps[b][:, e * D:(e + 1) * D], onehotT[:, s, t, :], rows(j, 0, D),
                                             start=(j == 0), stop=(j == 2))
                        for j in range(3):
                            last = nc.tensor.matmul(sdst_ps[s][:, t * HEADS:(t + 1) * HEADS], onehotT[:, s, t, :],
                                                    rows(j, D, HX), start=(j == 0), stop=(j == 2))
                    last.then_inc(hdst_made, 1)

            pipeline(pe, NQ, [(0, turn), (1, expand)])

        @block.scalar
        def _(act):
            def copy_onehotT(q, s, i):
                act.wait_ge(turned, q + 1)
                if again(q, 2):
                    act.wait_ge(hdst_made, QUAD * (q - 1))
                nc.scalar.copy(onehotT[:, s, :, :], turn_ps[s]).then_inc(onehotT_ready, 1)

            def relu(q, s, i):
                for k in range(QUAD):
                    u, b = q * QUAD + k, k % 2
                    act.wait_ge(enc_made, u + 1)
                    if again(u, 2):
                        act.wait_ge(prod_ready, u - 1)
                    nc.scalar.activation(enc[:, b, :], enc_ps[b][:], ACT.Relu).then_inc(enc_ready, 1)

            pipeline(act, NQ, [(0, copy_onehotT), (1, relu)])

        @block.vector
        def _(dve):
            V = nc.vector

            def onehots(q, s, i):
                if again(q, 2):
                    dve.wait_ge(turned, q - 1)
                for k in range(TILES):
                    last = V.tensor_scalar(
                        onehot[:, s, k, :], c.lane16[:],
                        dl[:, bass.ds(q * QUAD + k // 2, 1), k % 2:k % 2 + 1].rearrange("p a b -> p (a b)"),
                        None, ALU.is_equal)
                last.then_inc(onehot_ready, 1)

            def score(q, s, i):
                for k in range(QUAD):
                    u, b = q * QUAD + k, k % 2
                    dve.wait_ge(enc_ready, u + 1)
                    dve.wait_ge(hdst_made, u + 1)
                    if again(u, 2):
                        dve.wait_ge(red_ready, u - 1)
                    V.tensor_tensor(prod[:, b, :], hdst_ps[b][:], enc[:, b, :], ALU.mult).then_inc(prod_ready, 1)
                    dve.wait_ge(prod_ready, u + 1)
                    V.tensor_reduce(red[:, s, 2 * k:2 * k + 2, :],
                                    prod[:, b, :].rearrange("p (e h d) -> p e h d", e=2, h=HEADS), AX.X, ALU.add
                                    ).then_inc(red_ready, 1)
                dve.wait_ge(red_ready, QUAD * (q + 1))
                r = red[:, s, :, :].rearrange("p k h -> p (k h)")
                V.tensor_tensor(r, sdst_ps[s], r, ALU.add).then_inc(sum_step, 1)
                dve.wait_ge(sum_step, 2 * q + 1)
                dve.wait_ge(ssrc_in[s], 16 * TILES * (i + 1))
                V.tensor_tensor(r, r, ssrc[:, s, :, :].rearrange("p k h -> p (k h)"), ALU.add).then_inc(sum_step, 1)
                dve.wait_ge(sum_step, 2 * q + 2)
                V.scalar_tensor_tensor(out=alpha[:, bass.ds(q * TILES * HEADS, TILES * HEADS)], in0=r, scalar=0.2,
                                       in1=r, op0=ALU.mult, op1=ALU.max).then_inc(alpha_ready, 1)

            pipeline(dve, NQ, [(0, onehots), (1, score)])


RANGES = P // HEADS
RC = 2 * NS // RANGES
RL = RC * P
FAR = 1e30
assert RC * RANGES == 2 * NS


def softmax_numerators(nc, c, keys, alpha, cross):
    with ExitStack() as ctx:
        sb = lambda name, shape, dt=F32: ctx.enter_context(nc.sbuf_tensor(name, shape, dt))
        sem = lambda name: ctx.enter_context(nc.semaphore(name))
        a, key = sb("a_rows", [P, RL]), sb("key_rows", [P, RL])
        cut, top = sb("cut", [P, RL + 1]), sb("top", [P, RL])
        edge = sb("edge_keys", [P, 2])
        ends = sb("range_ends", [P, 2])
        row = sb("range_rows", [HEADS, 2, RANGES])
        carried = sb("carried", [HEADS, RANGES + 1])
        carry = sb("carry", [P, 2])
        turned, copied, ready, dma, step_sem = (
            sem("rows_turned"), sem("rows_copied"), sem("rows_ready"), sem("carry_dma"), sem("softmax_step"))
        wants_dma, back, back_copied = sem("wants_dma"), sem("turned_back"), sem("back_copied")
        exp_ready, ordered = sem("num_exp_ready"), sem("ordered")
        block = ctx.enter_context(nc.Block())
        groups = [(g0, min(4, RC - g0)) for g0 in range(0, RC, 4)]
        by_head = lambda x: x.rearrange("p (g t h) -> p t g h", g=RANGES, h=HEADS)
        key_cols = keys[:].rearrange("p n e -> p (n e)").rearrange("p (g t) -> p t g", g=RANGES)

        @block.tensor
        def _(pe):
            pe.wait_ge(ordered, 2)
            for n, (g0, w) in enumerate(groups):
                for j in range(2):
                    m = 2 * n + j
                    if m >= 4:
                        pe.wait_ge(copied, m - 3)
                    for t in range(w):
                        last = nc.tensor.transpose(c.ps[m % 4][:, t * P:(t + 1) * P],
                                                   (top, cut)[j][:, (g0 + t) * P:(g0 + t + 1) * P], c.ident[:])
                    last.then_inc(turned, 1)
            for n, (g0, w) in enumerate(groups):
                pe.wait_ge(exp_ready, 1)
                if n >= 4:
                    pe.wait_ge(back_copied, n - 3)
                for t in range(w):
                    last = nc.tensor.transpose(c.ps[4 + n % 4][:, t * P:(t + 1) * P],
                                               a[:, (g0 + t) * P:(g0 + t + 1) * P], c.ident[:])
                last.then_inc(back, 1)

        @block.scalar
        def _(act):
            nc.scalar.copy(top[:].rearrange("p (t g h) -> p t g h", g=RANGES, h=HEADS), by_head(alpha[:])
                           ).then_inc(ordered, 1)
            for n, (g0, w) in enumerate(groups):
                for j, out in enumerate((a, key)):
                    act.wait_ge(turned, 2 * n + j + 1)
                    nc.scalar.copy(out[:, g0 * P:(g0 + w) * P], c.ps[(2 * n + j) % 4][:, 0:w * P]
                                   ).then_inc(copied, 1)
            act.wait_ge(ready, 1)
            nc.scalar.activation(a[:], a[:], ACT.Exp).then_inc(ready, 1)
            for n, (g0, w) in enumerate(groups):
                act.wait_ge(back, n + 1)
                nc.scalar.copy(by_head(alpha[:])[:, g0:g0 + w],
                               c.ps[4 + n % 4][:, 0:w * P].rearrange("p (t g h) -> p t g h", t=w, g=RANGES)
                               ).then_inc(back_copied, 1)

        @block.sync
        def _(sp):
            n = 0

            def move(out, in_):
                nonlocal n
                sp.dma_start(out, in_, allow_slow_non_contiguous=True).then_inc(dma, 16)
                n += 1
                sp.wait_ge(dma, 16 * n)

            sp.wait_ge(wants_dma, 1)
            move(edge[HEADS:P, 0:1], key[0:P - HEADS, RL - 1:RL])
            move(edge[0:P - HEADS, 1:2], key[HEADS:P, 0:1])
            for d in range(2):
                sp.wait_ge(wants_dma, 2 + 2 * d)
                move(cross[d, :, :].rearrange("j p -> p j"), ends[:])
                move(row[:], cross[d, :, :].rearrange("j (g h) -> h j g", h=HEADS))
                sp.wait_ge(wants_dma, 3 + 2 * d)
                move(cross[2 + d, 0, :].rearrange("(g h) -> h g", h=HEADS),
                     carried[:, 0:RANGES] if d == 0 else carried[:, 1:RANGES + 1])
                move(carry[:, d:d + 1], cross[2 + d, 0, :].rearrange("(p o) -> p o", o=1))

        @block.vector
        def _(dve):
            V, step = nc.vector, Steps()

            def done(ins):
                ins.then_inc(step_sem, 1)
                dve.wait_ge(step_sem, step.last())

            V.tensor_copy(cut[:, 0:RL].rearrange("p (t g h) -> p t g h", g=RANGES, h=HEADS),
                          key_cols.unsqueeze(3).broadcast_to([P, RC, RANGES, HEADS])).then_inc(ordered, 1)
            V.memset(edge[:, 0:1], -1.0)
            done(V.memset(edge[:, 1:2], -1.0))
            dve.wait_ge(copied, 2 * len(groups))
            dve.sem_inc(wants_dma, 1)
            done(V.tensor_scalar(top[:], key[:], 0.0, None, ALU.is_gt))
            done(V.tensor_tensor(a[:], a[:], top[:], ALU.mult))
            done(V.tensor_scalar(top[:], top[:], -1.0, FAR, ALU.add, ALU.mult))
            done(V.tensor_tensor(a[:], a[:], top[:], ALU.add))
            done(V.tensor_tensor(cut[:, 1:RL], key[:, 1:RL], key[:, 0:RL - 1], ALU.not_equal))
            dve.wait_ge(dma, 32)
            done(V.tensor_tensor(cut[:, 0:1], key[:, 0:1], edge[:, 0:1], ALU.not_equal))
            done(V.tensor_tensor(cut[:, RL:RL + 1], key[:, RL - 1:RL], edge[:, 1:2], ALU.not_equal))
            done(V.tensor_scalar(cut[:], cut[:], -FAR, None, ALU.mult))
            for d in range(2):
                if d == 0:
                    cuts, vals, out, last = cut[:, 0:RL], a[:], top[:], top[:, RL - 1:RL]
                else:
                    cuts, vals, out, last = cut[:, RL:0:-1], top[:, ::-1], top[:, ::-1], top[:, 0:1]
                if d == 0:
                    done(V.tensor_tensor_scan(out, cuts, vals, -FAR, ALU.add, ALU.max))
                else:
                    done(V.tensor_tensor_scan(key[:, ::-1], cuts, vals, -FAR, ALU.add, ALU.max))
                    last = key[:, 0:1]
                V.tensor_copy(ends[:, 1:2], last)
                done(V.tensor_reduce(ends[:, 0:1], cuts, AX.X, ALU.min))
                dve.sem_inc(wants_dma, 1)
                dve.wait_ge(dma, 32 + 32 + 64 * d)
                if d == 0:
                    done(V.memset(carried[:, 0:1], -FAR))
                    done(V.tensor_tensor_scan(carried[:, 1:], row[:, 0, :], row[:, 1, :], -FAR, ALU.add, ALU.max))
                else:
                    done(V.memset(carried[:, RANGES:], -FAR))
                    done(V.tensor_tensor_scan(carried[:, RANGES - 1::-1], row[:, 0, ::-1], row[:, 1, ::-1], -FAR,
                                              ALU.add, ALU.max))
                dve.sem_inc(wants_dma, 1)
                dve.wait_ge(dma, 32 + 64 + 64 * d)
                if d == 0:
                    done(V.tensor_tensor_scan(out, cuts, vals, carry[:, 0:1], ALU.add, ALU.max))
                else:
                    done(V.tensor_tensor_scan(key[:, ::-1], cuts, vals, carry[:, 1:2], ALU.add, ALU.max))
            done(V.tensor_scalar(top[:], a[:], -0.5 * FAR, None, ALU.is_gt))
            V.tensor_tensor(a[:], a[:], key[:], ALU.subtract).then_inc(ready, 1)
            dve.wait_ge(ready, 2)
            V.tensor_tensor(a[:], a[:], top[:], ALU.mult).then_inc(exp_ready, 1)


def sum_messages(nc, c, htab, dl, src, block_row, alpha, acc):
    with ExitStack() as ctx:
        sb = lambda name, shape, dt=F32: ctx.enter_context(nc.sbuf_tensor(name, shape, dt))
        sem = lambda name: ctx.enter_context(nc.semaphore(name))
        onehot = sb("onehot32", [P, 2, TILES, P])
        stage, msg = sb("src_stage2", [P, 2, TILES], I32), sb("msg", [P, 2, TILES, D])
        rows_in = [sem(f"msg_in{s}") for s in range(2)]
        staged, onehot_ready, msg_ready, sums_made = (
            sem("staged2"), sem("onehot32_ready"), sem("msg_ready"), sem("sums_made"))
        acc_ready = sem("acc_ready")
        block = ctx.enter_context(nc.Block())
        SB = 4
        sum_ps = [c.ps[b][:, 0:HX] for b in range(SB)]

        @block.gpsimd
        def _(pool):
            def gather(q, s, i):
                if again(q, 2):
                    pool.wait_ge(rows_in[s], 16 * TILES * i)
                    pool.wait_ge(sums_made, QUAD * (q - 1))
                nc.gpsimd.tensor_copy(stage[:, s, :], src[:, bass.ds(q * QUAD, QUAD), :].rearrange(
                    "p n e -> p (n e)")).then_inc(staged, 1)
                wait_apart(pool, staged, q + 1, c.passed)
                for k in range(TILES):
                    nc.gpsimd.indirect_dma_start(
                        msg[:, s, k, :], None, htab,
                        bass.IndirectOffsetOnAxis(ap=stage[:, s, k:k + 1], axis=0)).then_inc(rows_in[s], 16)

            pipeline(pool, NQ, [(0, gather)])

        @block.vector
        def _(dve):
            V = nc.vector
            V.memset(acc[:], 0.0).then_inc(acc_ready, 1)

            def weigh(q, s, i):
                if again(q, 2):
                    dve.wait_ge(sums_made, QUAD * (q - 1))
                for k in range(TILES):
                    last = V.tensor_scalar(
                        onehot[:, s, k, :], c.lane16[:],
                        dl[:, bass.ds(q * QUAD + k // 2, 1), k % 2:k % 2 + 1].rearrange("p a b -> p (a b)"),
                        None, ALU.is_equal)
                last.then_inc(onehot_ready, 1)
                dve.wait_ge(rows_in[s], 16 * TILES * (i + 1))
                for k in range(QUAD):
                    m = msg[:, s, 2 * k:2 * k + 2, :].rearrange("p e (h d) -> p (e h) d", h=HEADS)
                    w = alpha[:, bass.ds((q * QUAD + k) * 2 * HEADS, 2 * HEADS)]
                    V.tensor_tensor(m, m, w.unsqueeze(2).broadcast_to([P, 2 * HEADS, HD]), ALU.mult
                                    ).then_inc(msg_ready, 1)

            def accumulate(q, s, i):
                blk = load_blocks(dve, block_row, q)
                for k in range(QUAD):
                    u = q * QUAD + k
                    rows = acc[:, bass.ds(blk[k], 1), :].rearrange("p o n -> p (o n)")
                    dve.wait_ge(sums_made, u + 1)
                    dve.wait_ge(acc_ready, u + 1)
                    V.tensor_tensor(rows, sum_ps[k % SB], rows, ALU.add).then_inc(acc_ready, 1)

            pipeline(dve, NQ, [(0, weigh), (1, accumulate)])

        @block.tensor
        def _(pe):
            def reduce(q, s, i):
                pe.wait_ge(onehot_ready, q + 1)
                for k in range(QUAD):
                    u = q * QUAD + k
                    pe.wait_ge(msg_ready, u + 1)
                    if again(u, SB):
                        pe.wait_ge(acc_ready, u - SB + 2)
                    for e in range(2):
                        nc.tensor.matmul(sum_ps[k % SB][:, 0:D], onehot[:, s, 2 * k + e, :], msg[:, s, 2 * k + e, :],
                                         start=(e == 0), stop=(e == 1))
                    for e in range(2):
                        last = nc.tensor.matmul(sum_ps[k % SB][:, D:HX], onehot[:, s, 2 * k + e, :],
                                                alpha[:, bass.ds((q * TILES + 2 * k + e) * HEADS, HEADS)],
                                                start=(e == 0), stop=(e == 1))
                    last.then_inc(sums_made, 1)

            pipeline(pe, NQ, [(0, reduce)])


NN = NT - 1
EXPERTS = 8
HIDDEN = 1024
HIC = HIDDEN // P
TOPK = 2
MT = (TOPK * N + EXPERTS * (P - 1)) // P
BW = HIDDEN + D


def finish_nodes(nc, c, acc, ytab, x1tab, gate_w, gate_b, biases, normed, scores, bias_parts):
    with ExitStack() as ctx:
        sb = lambda name, shape, dt=F32: ctx.enter_context(nc.sbuf_tensor(name, shape, dt))
        sem = lambda name: ctx.enter_context(nc.semaphore(name))
        gw, gb = sb("gw", [P, KC, EXPERTS]), sb("gb", [P, EXPERTS])
        bias, bias_rest = sb("bias", [EXPERTS, BW]), sb("bias_rest", [EXPERTS, BW])
        bias16 = sb("bias16", [EXPERTS, 3, BW], BF16)
        y, part, x1 = sb("y7", [P, 2, D]), sb("part7", [P, 2, D]), sb("x17", [P, 2, D])
        den, rec = sb("den7", [P, 2, HEADS]), sb("rec7", [P, 2, HEADS])
        stats, mv, rstd = sb("stats7", [P, 2, 6]), sb("mv7", [P, 2, 2]), sb("rstd7", [P, 2])
        nT, fixed = sb("nT", [P, 2, D]), sb("normed_fixed", [P, 2, D])
        consts_in, bias_step, bias_out = sem("gate_in"), sem("bias_step"), sem("bias_out")
        y_in = [sem(f"y7_in{s}") for s in range(2)]
        x1_out = [sem(f"x1_out{s}") for s in range(2)]
        dve_step, x1_ready, mv_ready = sem("dve_step7"), sem("x1_ready"), sem("mv7_ready")
        eps_ready, rstd_ready, normed_ready = sem("eps_ready"), sem("rstd7_ready"), sem("normed_ready")
        turned, nT_ready, gate_made, gate_ready = sem("nT_made"), sem("nT_ready"), sem("gate_made"), sem("gate_ready")
        block = ctx.enter_context(nc.Block())
        nT_ps = [c.ps[b][:, 0:D] for b in (0, 1)]
        gate_ps = [c.ps[b][:, 0:EXPERTS] for b in (2, 3)]
        heads = lambda ap: ap.rearrange("p (h d) -> p h d", h=HEADS)
        at = lambda buf, t: buf[:, bass.ds(t, 1), :].rearrange("p o n -> p (o n)")

        @block.sync
        def _(sp):
            sp.dma_start(gw[:], gate_w.rearrange("(c p) n -> p c n", p=P)).then_inc(consts_in, 16)
            sp.dma_start(gb[:], gate_b.rearrange("(o d) -> o d", o=1).broadcast_to([P, EXPERTS])).then_inc(consts_in, 16)
            sp.dma_start(bias[:], biases).then_inc(consts_in, 16)

            def load(t, s, i):
                if again(t, 2):
                    sp.wait_ge(x1_ready, t - 1)
                sp.dma_start(y[:, s, :], ytab[bass.ds(t * P, P), :]).then_inc(y_in[s], 16)

            def store(t, s, i):
                sp.wait_ge(x1_ready, t + 1)
                sp.dma_start(x1tab[bass.ds(t * P, P), :], x1[:, s, :]).then_inc(x1_out[s], 16)

            pipeline(sp, NN, [(0, load), (1, store)])
            sp.wait_ge(bias_step, 5)
            sp.dma_start(bias_parts.rearrange("j e n -> e j n"), bias16[:]).then_inc(bias_out, 16)
            sp.wait_ge(bias_out, 16)
            for s in range(2):
                sp.wait_ge(x1_out[s], 16 * ((NN + 1 - s) // 2))

        @block.gpsimd
        def _(pool):
            pool.wait_ge(consts_in, 48)
            for n, (out, a, b) in enumerate(((bias16[:, 0, :], bias[:], None),
                                             (bias_rest[:], bias[:], bias16[:, 0, :]),
                                             (bias16[:, 1, :], bias_rest[:], None),
                                             (bias_rest[:], bias_rest[:], bias16[:, 1, :]),
                                             (bias16[:, 2, :], bias_rest[:], None))):
                ins = nc.gpsimd.tensor_copy(out, a) if b is None else nc.gpsimd.tensor_tensor(out, a, b, ALU.subtract)
                ins.then_inc(bias_step, 1)
                pool.wait_ge(bias_step, n + 1)

            def inverse(t, s, i):
                if again(t, 2):
                    pool.wait_ge(normed_ready, t - 1)
                wait_apart(pool, mv_ready, t + 1, c.passed)
                nc.gpsimd.tensor_scalar(rstd[:, s:s + 1], mv[:, s, 1:2], LN_EPS, None, ALU.add).then_inc(eps_ready, 1)
                pool.wait_ge(eps_ready, t + 1)
                nc.gpsimd.tensor_tensor(rstd[:, s:s + 1], rstd[:, s:s + 1], c.minus_half[:], ALU.pow
                                        ).then_inc(rstd_ready, 1)

            pipeline(pool, NN, [(0, inverse)])

        @block.vector
        def _(dve):
            V = nc.vector

            def add_graph(t, s, i):
                V.tensor_scalar(den[:, s, :], acc[:, bass.ds(t, 1), D:HX].rearrange("p o n -> p (o n)"), 1e-10, None,
                                ALU.max).then_inc(dve_step, 1)
                dve.wait_ge(dve_step, 4 * t + 1)
                V.reciprocal(rec[:, s, :], den[:, s, :]).then_inc(dve_step, 1)
                dve.wait_ge(dve_step, 4 * t + 2)
                V.tensor_tensor(heads(part[:, s, :]), heads(acc[:, bass.ds(t, 1), 0:D].rearrange("p o n -> p (o n)")),
                                rec[:, s, :].unsqueeze(2).broadcast_to([P, HEADS, HD]), ALU.mult).then_inc(dve_step, 1)
                dve.wait_ge(dve_step, 4 * t + 3)
                dve.wait_ge(y_in[s], 16 * (i + 1))
                if again(t, 2):
                    dve.wait_ge(x1_out[s], 16 * i)
                V.tensor_tensor(x1[:, s, :], y[:, s, :], part[:, s, :], ALU.add).then_inc(x1_ready, 1)
                dve.wait_ge(x1_ready, t + 1)
                V.bn_stats(stats[:, s, :], x1[:, s, :]).then_inc(dve_step, 1)
                wait_apart(dve, dve_step, 4 * t + 4, c.passed)
                V.bn_aggr(mv[:, s, :], stats[:, s, :]).then_inc(mv_ready, 1)

            def norm(t, s, i):
                dve.wait_ge(rstd_ready, t + 1)
                if again(t, 2):
                    dve.wait_ge(turned, t - 1)
                    dve.wait_ge(gate_ready, t - 1)
                V.tensor_scalar(fixed[:, s, :], x1[:, s, :], mv[:, s, 0:1], rstd[:, s:s + 1],
                                ALU.subtract, ALU.mult).then_inc(normed_ready, 1)

            def gate(t, s, i):
                dve.wait_ge(normed_ready, t + 1)
                V.tensor_copy(at(normed, t), fixed[:, s, :])
                dve.wait_ge(gate_made, t + 1)
                V.tensor_tensor(at(scores, t), gate_ps[s], gb[:], ALU.add).then_inc(gate_ready, 1)

            dve.wait_ge(consts_in, 48)
            pipeline(dve, NN, [(2, gate), (0, add_graph), (1, norm)])

        @block.tensor
        def _(pe):
            pe.wait_ge(consts_in, 48)

            def turn(t, s, i):
                pe.wait_ge(normed_ready, t + 1)
                if again(t, 2):
                    pe.wait_ge(nT_ready, t - 1)
                for k in range(KC):
                    last = nc.tensor.transpose(nT_ps[s][:, k * P:(k + 1) * P], fixed[:, s, k * P:(k + 1) * P],
                                               c.ident[:])
                last.then_inc(turned, 1)

            def gate(t, s, i):
                pe.wait_ge(nT_ready, t + 1)
                if again(t, 2):
                    pe.wait_ge(gate_ready, t - 1)
                for k in range(KC):
                    last = nc.tensor.matmul(gate_ps[s], nT[:, s, k * P:(k + 1) * P], gw[:, k, :],
                                            start=(k == 0), stop=(k == KC - 1))
                last.then_inc(gate_made, 1)

            pipeline(pe, NN, [(1, gate), (0, turn)])

        @block.scalar
        def _(act):
            def copy_nT(t, s, i):
                act.wait_ge(turned, t + 1)
                if again(t, 2):
                    act.wait_ge(gate_made, t - 1)
                nc.scalar.copy(nT[:, s, :], nT_ps[s]).then_inc(nT_ready, 1)

            pipeline(act, NN, [(0, copy_nT)])


def route(nc, c, scores, normed, xs, probs, slots, expert_row):
    with ExitStack() as ctx:
        sb = lambda name, shape, dt=F32: ctx.enter_context(nc.sbuf_tensor(name, shape, dt))
        sem = lambda name: ctx.enter_context(nc.semaphore(name))
        zeros = sb("zeros", [P, D])
        top, at = sb("top8", [P, NN, 8]), sb("at8", [P, NN, 8], mybir.dt.uint32)
        atf = sb("atf", [P, TOPK, NN])
        gap, one_plus = sb("gap", [P, NN]), sb("one_plus", [P, NN])
        expert_id = sb("expert_id", [P, EXPERTS])
        real = sb("real", [P, 1])
        chosen = sb("chosen", [P, TOPK, NN, EXPERTS])
        both = sb("both", [P, NN, EXPERTS])
        both16, before = sb("both16", [P, NN * EXPERTS], BF16), sb("before", [P, P], BF16)
        ones16 = sb("ones16", [P, P], BF16)
        place, total, running = (sb(n, [P, NN, EXPERTS]) for n in ("place", "total", "running"))
        nrows, ntiles, tend, tstart = (sb(n, [P, EXPERTS]) for n in ("nrows", "ntiles", "tend", "tstart"))
        ntiles_i = sb("ntiles_i", [P, EXPERTS], I32)
        zero = sb("zero8", [P, NN])
        tile_id, passed = sb("tile_id", [P, MT]), sb("passed", [P, MT, EXPERTS])
        expert_f = sb("expert_f", [P, MT])
        slot_f = sb("slot_f", [P, TOPK, NN])
        picked = sb("picked", [P, NN, EXPERTS])
        iota_ready, step_sem, zeroed, gap_ready, exp_ready = (
            sem("route_iota"), sem("route_step"), sem("xs_zeroed"), sem("gap_ready"), sem("exp8_ready"))
        both_ready, ranked, slots_ready, scattered = (
            sem("both_ready"), sem("ranked"), sem("slots_ready"), sem("scattered"))
        block = ctx.enter_context(nc.Block())

        @block.sync
        def _(sp):
            sp.wait_ge(iota_ready, 1)
            sp.dma_start(xs.rearrange("(p r) d -> p r d", p=P),
                         zeros[:].unsqueeze(1).broadcast_to([P, MT, D])).then_inc(zeroed, 16)

        @block.gpsimd
        def _(pool):
            nc.gpsimd.memset(zeros[:], 0.0).then_inc(iota_ready, 1)
            nc.gpsimd.iota(expert_id[:], [[1, EXPERTS]], base=0, channel_multiplier=0,
                           allow_small_or_imprecise_dtypes=True)
            nc.gpsimd.iota(real[:], [[0, 1]], base=0, channel_multiplier=1, allow_small_or_imprecise_dtypes=True)
            nc.gpsimd.iota(tile_id[:], [[1, MT]], base=0, channel_multiplier=0, allow_small_or_imprecise_dtypes=True)
            nc.gpsimd.memset(ones16[:], 1.0).then_inc(iota_ready, 1)
            pool.wait_ge(iota_ready, 2)
            nc.gpsimd.affine_select(out=before[:], in_=ones16[:], compare_op=ALU.is_gt, fill=0.0, base=0,
                                    pattern=[[1, P]], channel_multiplier=-1).then_inc(iota_ready, 1)
            pool.wait_ge(slots_ready, 1)
            pool.wait_ge(zeroed, 16)
            for t in range(NN):
                rows = P if t < LAST else LAST_ROWS
                for j in range(TOPK):
                    nc.gpsimd.indirect_dma_start(
                        xs, bass.IndirectOffsetOnAxis(ap=slots[0:rows, j, t:t + 1], axis=0),
                        normed[0:rows, t, :], None).then_inc(scattered, 16)
            pool.wait_ge(scattered, 16 * TOPK * NN)

        @block.scalar
        def _(act):
            act.wait_ge(gap_ready, 1)
            nc.scalar.activation(gap[:], gap[:], ACT.Exp).then_inc(exp_ready, 1)

        @block.tensor
        def _(pe):
            pe.wait_ge(both_ready, 1)
            pe.wait_ge(iota_ready, 3)
            nc.tensor.matmul(c.ps[0][:, 0:NN * EXPERTS], before[:], both16[:], start=True, stop=True)
            nc.tensor.matmul(c.ps[1][:, 0:NN * EXPERTS], ones16[:], both16[:], start=True, stop=True
                             ).then_inc(ranked, 1)

        @block.vector
        def _(dve):
            V, step = nc.vector, Steps()

            def done(ins):
                ins.then_inc(step_sem, 1)
                dve.wait_ge(step_sem, step.last())

            done(V.memset(zero[:], 0.0))
            for t in range(NN):
                last = V.max(top[:, t, :], scores[:, t, :])
            done(last)
            for t in range(NN):
                last = V.max_index(at[:, t, :], top[:, t, :], scores[:, t, :])
            done(last)
            V.tensor_tensor(gap[:], top[:, :, 1], top[:, :, 0], ALU.subtract).then_inc(gap_ready, 1)
            dve.wait_ge(exp_ready, 1)
            done(V.tensor_scalar(one_plus[:], gap[:], 1.0, None, ALU.add))
            done(V.reciprocal(probs[:, 0, :], one_plus[:]))
            V.tensor_tensor(probs[:, 1, :], probs[:, 0, :], gap[:], ALU.mult)
            dve.wait_ge(iota_ready, 3)
            done(V.tensor_copy(atf[:], at[:, :, 0:TOPK].rearrange("p t j -> p j t")))
            ids = expert_id[:].unsqueeze(1).broadcast_to([P, NN, EXPERTS])
            for j in range(TOPK):
                done(V.tensor_tensor(chosen[:, j, :, :], ids, atf[:, j, :].unsqueeze(2).broadcast_to([P, NN, EXPERTS]),
                                     ALU.is_equal))
            done(V.tensor_tensor(both[:], chosen[:, 0, :, :], chosen[:, 1, :, :], ALU.add))
            done(V.tensor_scalar(real[:], real[:], float(LAST_ROWS), None, ALU.is_lt))
            done(V.tensor_scalar(both[:, LAST, :], both[:, LAST, :], real[:], None, ALU.mult))
            V.tensor_copy(both16[:], both[:].rearrange("p t e -> p (t e)")).then_inc(both_ready, 1)
            dve.wait_ge(ranked, 1)
            flat = lambda ap: ap.rearrange("p t e -> p (t e)")
            done(V.tensor_copy(flat(place[:]), c.ps[0][:, 0:NN * EXPERTS]))
            done(V.tensor_copy(flat(total[:]), c.ps[1][:, 0:NN * EXPERTS]))
            for e in range(EXPERTS):
                last = V.tensor_tensor_scan(running[:, :, e], total[:, :, e], zero[:], 0.0, ALU.add, ALU.add)
            done(last)
            done(V.tensor_tensor(place[:], place[:], running[:], ALU.add))
            done(V.tensor_tensor(place[:], place[:], total[:], ALU.subtract))
            done(V.tensor_scalar(nrows[:], running[:, NN - 1, :], P - 1.0, None, ALU.add))
            done(V.tensor_copy(ntiles_i[:], nrows[:]))
            done(V.tensor_single_scalar(ntiles_i[:], ntiles_i[:], 7, ALU.arith_shift_right))
            done(V.tensor_copy(ntiles[:], ntiles_i[:]))
            done(V.tensor_tensor_scan(tend[:], ntiles[:], zero[:, 0:EXPERTS], 0.0, ALU.add, ALU.add))
            done(V.tensor_tensor(tstart[:], tend[:], ntiles[:], ALU.subtract))
            done(V.tensor_scalar(nrows[:], tstart[:], float(P), None, ALU.mult))
            done(V.tensor_tensor(place[:], place[:], nrows[:].unsqueeze(1).broadcast_to([P, NN, EXPERTS]), ALU.add))
            for j in range(TOPK):
                done(V.tensor_tensor(picked[:], place[:], chosen[:, j, :, :], ALU.mult))
                done(V.tensor_reduce(slot_f[:, j, :], picked[:], AX.X, ALU.add))
            V.tensor_copy(slots[:], slot_f[:]).then_inc(slots_ready, 1)
            done(V.tensor_tensor(passed[:], tstart[:].unsqueeze(1).broadcast_to([P, MT, EXPERTS]),
                                 tile_id[:].unsqueeze(2).broadcast_to([P, MT, EXPERTS]), ALU.is_le))
            done(V.tensor_reduce(expert_f[:], passed[:], AX.X, ALU.add))
            done(V.tensor_scalar(expert_f[:], expert_f[:], -1.0, None, ALU.add))
            V.tensor_copy(expert_row[:], expert_f[0:1, :])


def run_experts(nc, c, xs, ys, w1t, w2t, bias_parts, expert_row):
    with ExitStack() as ctx:
        sb = lambda name, shape, dt=F32: ctx.enter_context(nc.sbuf_tensor(name, shape, dt))
        sem = lambda name: ctx.enter_context(nc.semaphore(name))
        w1, w2 = sb("w1", [P, EXPERTS, KC, HIDDEN]), sb("w2", [P, EXPERTS, HIC, D])
        bias = sb("bias_rows", [3, EXPERTS, BW], BF16)
        ones16 = sb("ones3", [3, P], BF16)
        x, xT = sb("x9", [P, 2, D]), sb("x9T", [P, 2, D])
        h, hT = sb("h9", [P, HIDDEN]), sb("h9T", [P, HIDDEN])
        y = sb("y9", [P, 2, D])
        weights_in, ones_ready = sem("experts_in"), sem("ones3_ready")
        x_in = [sem(f"x9_in{s}") for s in range(2)]
        y_out = [sem(f"y9_out{s}") for s in range(2)]
        xT_made, xT_ready, h_made, h_ready = sem("x9T_made"), sem("x9T_ready"), sem("h9_made"), sem("h9_ready")
        hT_made, hT_ready, y_made, y_ready = sem("h9T_made"), sem("h9T_ready"), sem("y9_made"), sem("y9_ready")
        block = ctx.enter_context(nc.Block())
        xT_ps = [c.ps[0][:, 0:D], c.ps[7][:, 0:D]]
        h_ps, hT_ps = [c.ps[1], c.ps[2]], [c.ps[3], c.ps[4]]
        y_ps = [c.ps[5][:, 0:D], c.ps[6][:, 0:D]]

        @block.sync
        def _(sp):
            for e in range(EXPERTS):
                sp.dma_start(w1[:, e], w1t[e].rearrange("(c p) n -> p c n", p=P)).then_inc(weights_in, 16)
                sp.dma_start(w2[:, e], w2t[e].rearrange("(c p) n -> p c n", p=P)).then_inc(weights_in, 16)
            sp.dma_start(bias[:], bias_parts).then_inc(weights_in, 16)

            def load(t, s, i):
                if again(t, 2):
                    sp.wait_ge(xT_made, t - 1)
                sp.dma_start(x[:, s, :], xs[bass.ds(t * P, P), :]).then_inc(x_in[s], 16)

            def store(t, s, i):
                sp.wait_ge(y_ready, t + 1)
                sp.dma_start(ys[bass.ds(t * P, P), :], y[:, s, :]).then_inc(y_out[s], 16)

            pipeline(sp, MT, [(0, load), (2, store)])
            for s in range(2):
                sp.wait_ge(y_out[s], 16 * ((MT + 1 - s) // 2))

        @block.tensor
        def _(pe):
            pe.wait_ge(weights_in, 16 * (2 * EXPERTS + 1))
            pe.wait_ge(ones_ready, 1)

            def turn_x(t, s, i):
                pe.wait_ge(x_in[s], 16 * (i + 1))
                if again(t, 2):
                    pe.wait_ge(xT_ready, t - 1)
                for k in range(KC):
                    last = nc.tensor.transpose(xT_ps[s][:, k * P:(k + 1) * P], x[:, s, k * P:(k + 1) * P], c.ident[:])
                last.then_inc(xT_made, 1)

            def expert(t):
                return pe.value_load(expert_row[0:1, bass.ds(t, 1)], min_val=0, max_val=EXPERTS - 1)

            def hidden(t, s, i):
                e = expert(t)
                pe.wait_ge(xT_ready, t + 1)
                for n in range(2):
                    lo = n * 512
                    if again(t, 1):
                        pe.wait_ge(h_ready, 2 * t - 1 + n)
                    for k in range(KC):
                        nc.tensor.matmul(h_ps[n][:], xT[:, s, k * P:(k + 1) * P],
                                         w1[:, bass.ds(e, 1), k, lo:lo + 512].rearrange("p o n -> p (o n)"),
                                         start=(k == 0), stop=False)
                    nc.tensor.matmul(h_ps[n][:], ones16[:],
                                     bias[:, bass.ds(e, 1), lo:lo + 512].rearrange("p o n -> p (o n)"),
                                     start=False, stop=True).then_inc(h_made, 1)

            def turn_h(t, s, i):
                for n in range(2):
                    pe.wait_ge(h_ready, 2 * t + n + 1)
                    if again(t, 1):
                        pe.wait_ge(hT_ready, 2 * t - 1 + n)
                    for k in range(4):
                        lo = (4 * n + k) * P
                        last = nc.tensor.transpose(hT_ps[n][:, k * P:(k + 1) * P], h[:, lo:lo + P], c.ident[:])
                    last.then_inc(hT_made, 1)

            def output(t, s, i):
                e = expert(t)
                if again(t, 2):
                    pe.wait_ge(y_ready, t - 1)
                for k in range(HIC):
                    if k % 4 == 0:
                        pe.wait_ge(hT_ready, 2 * t + k // 4 + 1)
                    nc.tensor.matmul(y_ps[s], hT[:, k * P:(k + 1) * P],
                                     w2[:, bass.ds(e, 1), k, :].rearrange("p o n -> p (o n)"),
                                     start=(k == 0), stop=False)
                nc.tensor.matmul(y_ps[s], ones16[:], bias[:, bass.ds(e, 1), HIDDEN:BW].rearrange("p o n -> p (o n)"),
                                 start=False, stop=True).then_inc(y_made, 1)

            pipeline(pe, MT, [(0, turn_x), (2, turn_h), (1, hidden), (2, output)])

        @block.scalar
        def _(act):
            def copy_xT(t, s, i):
                act.wait_ge(xT_made, t + 1)
                if again(t, 2):
                    act.wait_ge(h_made, 2 * (t - 1))
                nc.scalar.copy(xT[:, s, :], xT_ps[s]).then_inc(xT_ready, 1)

            def relu(t, s, i):
                for n in range(2):
                    act.wait_ge(h_made, 2 * t + n + 1)
                    if again(t, 1):
                        act.wait_ge(hT_made, 2 * t - 1 + n)
                    nc.scalar.activation(h[:, n * 512:(n + 1) * 512], h_ps[n][:], ACT.Relu).then_inc(h_ready, 1)

            pipeline(act, MT, [(0, copy_xT), (1, relu)])

        @block.vector
        def _(dve):
            nc.vector.memset(ones16[:], 1.0).then_inc(ones_ready, 1)

            def copy_hT(t, s, i):
                for n in range(2):
                    dve.wait_ge(hT_made, 2 * t + n + 1)
                    if again(t, 1):
                        dve.wait_ge(y_made, t)
                    nc.vector.tensor_copy(hT[:, n * 512:(n + 1) * 512], hT_ps[n][:]).then_inc(hT_ready, 1)

            def copy_y(t, s, i):
                dve.wait_ge(y_made, t + 1)
                if again(t, 2):
                    dve.wait_ge(y_out[s], 16 * i)
                nc.vector.tensor_copy(y[:, s, :], y_ps[s]).then_inc(y_ready, 1)

            pipeline(dve, MT, [(0, copy_hT), (0, copy_y)])


def combine(nc, c, x1tab, ys, probs, slots, out):
    with ExitStack() as ctx:
        sb = lambda name, shape, dt=F32: ctx.enter_context(nc.sbuf_tensor(name, shape, dt))
        sem = lambda name: ctx.enter_context(nc.semaphore(name))
        R = 3
        x1, y = sb("x1_last", [P, R, D]), sb("y_last", [P, R, TOPK, D])
        x1_in = [sem(f"x1_in{s}") for s in range(R)]
        y_in = [sem(f"y_in{s}") for s in range(R)]
        out_done = [sem(f"out_done{s}") for s in range(R)]
        first, summed = sem("first_added"), sem("both_added")
        block = ctx.enter_context(nc.Block())
        rows = lambda t: P if t < LAST else LAST_ROWS

        @block.sync
        def _(sp):
            for t in range(NN + 1):
                if t < NN:
                    if t >= R:
                        sp.wait_ge(out_done[t % R], 16 * (t // R))
                    sp.dma_start(x1[0:rows(t), t % R, :], x1tab[t * P:t * P + rows(t), :]).then_inc(x1_in[t % R], 16)
                if t >= 1:
                    o = t - 1
                    sp.wait_ge(x1_in[o % R], 16 * (o // R + 1))
                    sp.wait_ge(summed, o + 1)
                    sp.dma_start(out[o * P:o * P + rows(o), :], x1[0:rows(o), o % R, :]).then_inc(out_done[o % R], 16)
            for s in range(R):
                sp.wait_ge(out_done[s], 16 * len(range(s, NN, R)))

        @block.gpsimd
        def _(pool):
            for t in range(NN):
                if t >= R:
                    pool.wait_ge(summed, t - R + 1)
                    pool.wait_ge(y_in[t % R], 32 * (t // R))
                for j in range(TOPK):
                    nc.gpsimd.indirect_dma_start(
                        y[0:rows(t), t % R, j, :], None, ys,
                        bass.IndirectOffsetOnAxis(ap=slots[0:rows(t), j, t:t + 1], axis=0)).then_inc(y_in[t % R], 16)

        @block.vector
        def _(dve):
            for t in range(NN):
                s, r = t % R, rows(t)
                dve.wait_ge(x1_in[s], 16 * (t // R + 1))
                dve.wait_ge(y_in[s], 32 * (t // R + 1))
                for j, sem_ in enumerate((first, summed)):
                    if j == 1:
                        dve.wait_ge(first, t + 1)
                    nc.vector.scalar_tensor_tensor(out=x1[0:r, s, :], in0=y[0:r, s, j, :],
                                                   scalar=probs[0:r, j, t:t + 1], in1=x1[0:r, s, :],
                                                   op0=ALU.mult, op1=ALU.add).then_inc(sem_, 1)


class Shared:
    pass


def build(nc, io):
    with ExitStack() as ctx:
        sb = lambda name, shape, dt=F32: ctx.enter_context(nc.sbuf_tensor(name, shape, dt))
        dram = lambda name, shape, dt=F32: nc.dram_tensor(name, shape, dt, kind="Internal").ap()
        c = Shared()
        c.ps = [ctx.enter_context(nc.psum_tensor(f"bank{b}", [P, 512], F32)) for b in range(8)]
        c.ident, c.ident16 = sb("ident", [P, P]), sb("ident16", [P, P], BF16)
        c.ones = sb("ones", [P, P])
        c.minus_half = sb("minus_half", [P, 1])
        c.passed = ctx.enter_context(nc.semaphore("passed"))
        c.lane16 = sb("lane16", [P, P], BF16)
        htab, stab = dram("htab", [NP, D]), dram("stab", [NP, HEADS])
        qtab, xntab = dram("qtab", [NP, D]), dram("xntab", [NP, D])
        ytab = dram("ytab", [NP, D])
        build_constants(nc, c)
        block_row = sb("block_row", [1, SG * P], I32)
        probs, slots = sb("probs", [P, TOPK, NN]), sb("slots", [P, TOPK, NN], I32)
        expert_row = sb("expert_row", [1, MT], I32)
        edge_ctx = ctx.enter_context(ExitStack())
        sb = lambda name, shape, dt=F32: edge_ctx.enter_context(nc.sbuf_tensor(name, shape, dt))
        dl, src, keys = sb("dl", [P, NS, 2]), sb("src", [P, NS, 2], I32), sb("keys", [P, NS, 2])
        blocks = dram("blocks", [1, SG * P], I32)
        attr_parts = dram("attr_parts", [12, SG * P, 2 * P], BF16)
        wparts = sb("wparts", [36, D], BF16)
        plan_steps(nc, c, io["dst"], io["src"], io["attr"], io["edge_w"], wparts, dl, src, keys, blocks, block_row,
                   attr_parts)
        alpha = sb("alpha", [P, 2 * NS * HEADS])
        with nc.sbuf_tensor("hparts", [P, NT, 3, HX], BF16) as hparts:
            with nc.sbuf_tensor("wall", [P, KC, WALL], F32) as wall:
                fold_weights(nc, c, io["W"], io["WT"], io["a_src"], io["a_dst"], io["w_norm1"], io["w_qkv"], wall)
                project_nodes(nc, c, io["x"], wall, hparts, htab, stab, qtab, xntab)
            mix_nodes(nc, c, io["x"], io["gnn_bias"], io["w_out"], io["b_out"], io["w_norm2"], qtab, xntab, ytab)
            score_edges(nc, c, wparts, hparts, stab, attr_parts, dl, src, block_row, alpha)
        softmax_numerators(nc, c, keys, alpha, dram("cross", [4, 2, P]))
        x1tab = dram("x1tab", [NP, D])
        xs, ys = dram("xs", [MT * P, D]), dram("ys", [MT * P, D])
        bias_parts = dram("bias_parts", [3, EXPERTS, BW], BF16)
        with nc.sbuf_tensor("normed", [P, NN, D], F32) as normed, nc.sbuf_tensor("scores", [P, NN, EXPERTS], F32) as scores:
            with nc.sbuf_tensor("acc", [P, NT, HX], F32) as acc:
                sum_messages(nc, c, htab, dl, src, block_row, alpha, acc)
                finish_nodes(nc, c, acc, ytab, x1tab, io["gate_w"], io["gate_b"], io["biases"], normed, scores,
                             bias_parts)
            route(nc, c, scores, normed, xs, probs, slots, expert_row)
        edge_ctx.close()
        run_experts(nc, c, xs, ys, io["w1t"], io["w2t"], bias_parts, expert_row)
        combine(nc, c, x1tab, ys, probs, slots, io["out"])
        if "dbg" in io:
            io["dbg"](nc, c, locals())


def layout(inp):
    f = lambda name: np.asarray(inp[name])
    x = np.zeros((NP, D), np.float32)
    x[:N] = f("x")

    def edges(name, fill):
        a = np.full(ET * P, fill, np.int32)
        a[:E] = f(name)
        return a.reshape(ET, P)

    attr = np.zeros((ET * P, 4), np.float32)
    attr[:E, :3], attr[:E, 3] = f("edge_attr_3"), 1.0
    attr = attr.reshape(ET, P, 4).transpose(0, 2, 1)
    return {
        "x": x,
        "W": f("L0_gnn_W"), "WT": f("L0_gnn_W").T,
        "a_src": f("L0_gnn_a_src"), "a_dst": f("L0_gnn_a_dst"),
        "w_norm1": f("L0_mix_w_norm1"), "w_qkv": f("L0_mix_w_qkv"),
        "gnn_bias": f("L0_gnn_bias"), "w_out": f("L0_mix_w_out"), "b_out": f("L0_mix_b_out"),
        "w_norm2": f("L0_mix_w_norm2"),
        "gate_w": f("L0_ffn_Wg").T, "gate_b": f("L0_ffn_bg"),
        "biases": np.concatenate([f("L0_ffn_b1"), f("L0_ffn_b2")], axis=1),
        "w1t": f("L0_ffn_W1").transpose(0, 2, 1), "w2t": f("L0_ffn_W2").transpose(0, 2, 1),
        "dst": edges("dst", 2 * NP), "src": edges("src", 0), "attr": attr.reshape(ET, 4 * P),
        "edge_w": np.concatenate([f("L0_gnn_edge_W").T, f("L0_gnn_edge_b")[None]]),
    }


def kernel(**inputs):
    import concourse.bacc as bacc
    from concourse.bass_utils import run_bass_kernel_spmd

    arrays = {f"in_{n}": np.ascontiguousarray(a) for n, a in layout(inputs).items()}
    nc = bacc.Bacc("TRN2", target_bir_lowering=False, num_devices=1)
    io = {n[3:]: nc.dram_tensor(n, a.shape, mybir.dt.from_np(a.dtype), kind="ExternalInput").ap()
          for n, a in arrays.items()}
    io["out"] = nc.dram_tensor("out", [N, D], F32, kind="ExternalOutput").ap()
    build(nc, io)
    r = run_bass_kernel_spmd(nc, [arrays], core_ids=[0])
    return r.results[0]["out"]
```

```python
from contextlib import ExitStack

import numpy as np

import concourse.bass as bass
from concourse import mybir

ALU = mybir.AluOpType
ACT = mybir.ActivationFunctionType
AX = mybir.AxisListType
F32 = mybir.dt.float32
BF16 = mybir.dt.bfloat16
I32 = mybir.dt.int32

P = 128
D = 256
KC = D // P
HEADS = 8
HD = D // HEADS
N = 6250
NT = 50
NP = NT * P
LAST = N // P
LAST_ROWS = N - LAST * P
HC = D + 2 * HEADS
HX = D + HEADS
QC = 3 * D
COL_V, COL_QK, COL_S = D, 2 * D, 4 * D
WALL = COL_S + 2 * HEADS
E = 100000
ET = 784
COUNT_P = 112
NS = 440
SG = 4
assert ET % COUNT_P == 0 and (ET - 2) * P >= E
assert 2 * NS >= (-(-E // P) + (NT - 2) + (NT - 1)) and NS <= SG * P
LN_EPS = 1e-5
RMS_EPS = 1e-6
ATT_EPS = 1e-6


class Steps:

    def __init__(self, base=0):
        self.base, self.n = base, 0

    def last(self):
        self.n += 1
        return self.base + self.n


def clear_after(nc, ctx, used):

    def clear():
        with nc.Block() as block:

            @block.gpsimd
            def _(pool):
                for s in used:
                    pool.sem_clear(s)

    ctx.callback(clear)


def semaphores(nc, ctx):
    made = []

    def sem(name):
        made.append(ctx.enter_context(nc.semaphore(name)))
        return made[-1]

    clear_after(nc, ctx, made)
    return sem


def gather_semaphores(c, n):
    return [c.gathered.pop() for _ in range(n)]


def build_constants(nc, c):
    with ExitStack() as ctx:
        pool_step = semaphores(nc, ctx)("pool_step")
        block = ctx.enter_context(nc.Block())

        @block.gpsimd
        def _(pool):
            step = Steps()
            nc.gpsimd.memset(c.ident[:], 0.0).then_inc(pool_step, 1)
            pool.wait_ge(pool_step, step.last())
            nc.gpsimd.affine_select(out=c.ident[:], in_=c.ident[:], compare_op=ALU.not_equal, fill=1.0,
                                    base=0, pattern=[[-1, P]], channel_multiplier=1).then_inc(pool_step, 1)
            pool.wait_ge(pool_step, step.last())
            nc.gpsimd.tensor_copy(c.ident16[:], c.ident[:])
            nc.gpsimd.memset(c.ones[:], 1.0)
            nc.gpsimd.memset(c.minus_half[:], -0.5)
            nc.gpsimd.iota(c.lane16[:], [[1, P]], base=0, channel_multiplier=0,
                           allow_small_or_imprecise_dtypes=True)


def fold_weights(nc, c, W, WT, a_src, a_dst, w_norm1, w_qkv, wall):
    with ExitStack() as ctx:
        sb = lambda name, shape, dt=F32: ctx.enter_context(nc.sbuf_tensor(name, shape, dt))
        sem = semaphores(nc, ctx)
        w_rows = sb("w_rows", [P, KC, D])
        att = sb("att", [P, KC, 2 * HEADS])
        norm1 = sb("norm1", [P, KC])
        weights_in, att_zero, att_in, folded, scaled = (
            sem("weights_in"), sem("att_zero"), sem("att_in"), sem("folded"), sem("scaled"))
        block = ctx.enter_context(nc.Block())

        @block.sync
        def _(sp):
            sp.dma_start(w_rows[:], W.rearrange("(c p) k -> p c k", p=P)).then_inc(weights_in, 16)
            sp.dma_start(wall[:, :, 0:D], WT.rearrange("(c p) n -> p c n", p=P)).then_inc(weights_in, 16)
            qkv = w_qkv.rearrange("(c p) n -> p c n", p=P)
            sp.dma_start(wall[:, :, COL_QK:COL_QK + 2 * D], qkv[:, :, 0:2 * D]).then_inc(weights_in, 16)
            sp.dma_start(wall[:, :, COL_V:COL_V + D], qkv[:, :, 2 * D:3 * D]).then_inc(weights_in, 16)
            sp.dma_start(norm1[:], w_norm1.rearrange("(c p) -> p c", p=P),
                         allow_slow_non_contiguous=True).then_inc(weights_in, 16)
            sp.wait_ge(att_zero, 1)
            for h in range(HEADS):
                rows = slice(HD * h % P, HD * h % P + HD)
                for j, a in enumerate((a_dst, a_src)):
                    sp.dma_start(att[rows, HD * h // P, j * HEADS + h:j * HEADS + h + 1],
                                 a[h, :].rearrange("(d o) -> d o", o=1),
                                 allow_slow_non_contiguous=True).then_inc(att_in, 16)

        @block.vector
        def _(dve):
            nc.vector.memset(att[:], 0.0).then_inc(att_zero, 1)
            dve.wait_ge(weights_in, 5 * 16)
            for k in range(KC):
                nc.vector.tensor_scalar(wall[:, k, COL_V:COL_S], wall[:, k, COL_V:COL_S], norm1[:, k:k + 1], None,
                                        ALU.mult).then_inc(scaled, 1)
            dve.wait_ge(folded, 1)
            nc.vector.tensor_copy(wall[:, :, COL_S:WALL], c.ps[0][:, 0:KC * 2 * HEADS].rearrange("p (k n) -> p k n", k=KC))

        @block.tensor
        def _(pe):
            pe.wait_ge(weights_in, 5 * 16)
            pe.wait_ge(att_in, 16 * 2 * HEADS)
            for k in range(KC):
                for m in range(KC):
                    last = nc.tensor.matmul(c.ps[0][:, k * 2 * HEADS:(k + 1) * 2 * HEADS],
                                            w_rows[:, m, k * P:(k + 1) * P], att[:, m, :],
                                            start=(m == 0), stop=(m == KC - 1))
            last.then_inc(folded, 1)


def wait_apart(eng, sem, value, passed):
    eng.wait_ge(sem, value)
    if not isinstance(value, int):
        eng.sem_inc(passed, 1)


def again(t, k):
    return not isinstance(t, int) or t >= k


def pipeline(eng, n, stages, unroll=2):
    stages = [(*stage, n)[:3] for stage in stages]
    far = max(lag for lag, _, _ in stages)

    def turn(T, r, j):
        for lag, fn, tiles in stages:
            t = T - lag if isinstance(T, int) else T + (r - lag)
            if not isinstance(T, int) or 0 <= t < tiles:
                fn(t, (r - lag) % unroll, j + (r - lag) // unroll)

    first = -(-(far + 4) // unroll) * unroll
    end = min(tiles for _, _, tiles in stages) // unroll * unroll
    for T in range(first):
        turn(T, T % unroll, T // unroll)
    with eng.Fori(first // unroll, end // unroll) as j:
        for r in range(unroll):
            turn(j * unroll, r, j)
    for T in range(end, max(lag + tiles for lag, _, tiles in stages)):
        turn(T, T % unroll, T // unroll)


def row_norms(nc, c, x, x_all, mean, rstd, r1):
    with ExitStack() as ctx:
        sb = lambda name, shape, dt=F32: ctx.enter_context(nc.sbuf_tensor(name, shape, dt))
        sem = semaphores(nc, ctx)
        CH = 5
        CT = NT // CH
        stats = sb("stats", [P, NT, 6])
        half, var, ms = sb("half_gap", [P, NT]), sb("var", [P, NT]), sb("ms", [P, NT])
        x_in = [sem(f"x_in{n}") for n in range(CH)]
        step_sem, var_ready, rstd_ready, ms_ready = sem("norm_step"), sem("var_ready"), sem("rstd_ready"), sem("ms_ready")
        block = ctx.enter_context(nc.Block())

        @block.sync
        def _(sp):
            for n in range(CH):
                sp.dma_start(x_all[:, n * CT:(n + 1) * CT, :],
                             x[n * CT * P:(n + 1) * CT * P, :].rearrange("(t p) d -> p t d", p=P)).then_inc(x_in[n], 16)

        @block.vector
        def _(dve):
            V, step = nc.vector, Steps()

            def done(ins):
                ins.then_inc(step_sem, 1)
                dve.wait_ge(step_sem, step.last())

            for n in range(CH):
                dve.wait_ge(x_in[n], 16)
                for t in range(n * CT, (n + 1) * CT):
                    last = V.bn_stats(stats[:, t, :], x_all[:, t, :])
            done(last)
            m0, m1, v0, v1 = (stats[:, :, j] for j in (1, 4, 2, 5))
            V.tensor_tensor(mean[:], m0, m1, ALU.add)
            V.tensor_tensor(half[:], m0, m1, ALU.subtract)
            done(V.tensor_tensor(var[:], v0, v1, ALU.add))
            V.tensor_scalar(mean[:], mean[:], 0.5, None, ALU.mult)
            done(V.tensor_scalar(half[:], half[:], 0.5, None, ALU.mult))
            done(V.tensor_tensor(half[:], half[:], half[:], ALU.mult))
            V.scalar_tensor_tensor(out=var[:], in0=var[:], scalar=1.0 / D, in1=half[:], op0=ALU.mult,
                                   op1=ALU.add).then_inc(var_ready, 1)
            dve.wait_ge(var_ready, 1)
            V.tensor_scalar(half[:], var[:], LN_EPS, None, ALU.add).then_inc(var_ready, 1)
            dve.wait_ge(rstd_ready, 1)
            done(V.tensor_tensor(ms[:], rstd[:], rstd[:], ALU.mult))
            done(V.tensor_tensor(ms[:], ms[:], var[:], ALU.mult))
            V.tensor_scalar(ms[:], ms[:], RMS_EPS, None, ALU.add).then_inc(ms_ready, 1)

        @block.gpsimd
        def _(pool):
            power = c.minus_half[:].broadcast_to([P, NT])
            pool.wait_ge(var_ready, 2)
            nc.gpsimd.tensor_tensor(rstd[:], half[:], power, ALU.pow).then_inc(rstd_ready, 1)
            pool.wait_ge(ms_ready, 1)
            nc.gpsimd.tensor_tensor(r1[:], ms[:], power, ALU.pow)


def project_nodes(nc, c, x_all, mean, rstd, r1, wall, hparts, htab, stab, qtab, xntab):
    with ExitStack() as ctx:
        sb = lambda name, shape, dt=F32: ctx.enter_context(nc.sbuf_tensor(name, shape, dt))
        sem = semaphores(nc, ctx)
        R = 4
        xn, xT = sb("xn", [P, R, D]), sb("xT", [P, R, D])
        hrow, rest = sb("hrow", [P, R, HC]), sb("rest", [P, 2, HX])
        neg, pos, qk = sb("neg", [P, 2, 2 * D]), sb("pos", [P, 2, 2 * D]), sb("qk", [P, R, 2 * D])
        v = sb("v", [P, R, D])
        scale = sb("scale", [P, 2])
        xn_ready, scale_ready = sem("xn_ready"), sem("scale_ready")
        xT_made, xT_ready, proj_made = sem("xT_made"), sem("xT_ready"), sem("proj_made")
        hrow_ready, exp_ready = sem("hrow_ready"), sem("exp_ready")
        part1_ready, neg_ready = sem("part1_ready"), sem("neg_ready")
        rest_ready, part2_ready, parts_made = sem("rest_ready"), sem("part2_ready"), sem("parts_made")
        qk_ready, kv_used = sem("qk_ready"), sem("kv_used")
        xn_out = [sem(f"xn_out{s}") for s in range(R)]
        h_out = [sem(f"h_out{s}") for s in range(R)]
        q_out = [sem(f"q_out{s}") for s in range(R)]
        block = ctx.enter_context(nc.Block())

        xT_ps = [c.ps[b][:, 0:D] for b in (0, 1)]
        s_ps = [c.ps[b][:, D:D + 2 * HEADS] for b in (0, 1)]
        hv_ps = [c.ps[2], c.ps[3]]
        qk_ps = [c.ps[6], c.ps[7]]
        kv_ps = c.ps[4][:, :].rearrange("p (c n) -> p c n", c=KC)
        ksum_ps = c.ps[5][:, 0:D]
        at = lambda buf, t: buf[:, bass.ds(t, 1)]

        @block.sync
        def _(sp):
            def store_xn(t, s, i):
                sp.wait_ge(xn_ready, t + 1)
                sp.dma_start(xntab[bass.ds(t * P, P), :], xn[:, s, :]).then_inc(xn_out[s], 16)

            def store(t, s, i):
                rows = bass.ds(t * P, P)
                sp.wait_ge(hrow_ready, t + 1)
                sp.dma_start(htab[rows, :], hrow[:, s, 0:D]).then_inc(h_out[s], 16)
                sp.dma_start(stab[rows, :], hrow[:, s, HX:HC]).then_inc(h_out[s], 16)
                sp.wait_ge(qk_ready, t + 1)
                sp.dma_start(qtab[rows, :], qk[:, s, 0:D]).then_inc(q_out[s], 16)

            pipeline(sp, NT, [(0, store_xn), (3, store)], R)
            for s in range(R):
                uses = len(range(s, NT, R))
                sp.wait_ge(xn_out[s], 16 * uses)
                sp.wait_ge(h_out[s], 32 * uses)
                sp.wait_ge(q_out[s], 16 * uses)

        @block.vector
        def _(dve):
            def normalise(t, s, i):
                if again(t, R):
                    dve.wait_ge(xT_made, t - R + 1)
                    dve.wait_ge(xn_out[s], 16 * i)
                nc.vector.tensor_scalar(xn[:, s, :], at(x_all, t).rearrange("p o n -> p (o n)"),
                                        at(mean, t), at(rstd, t), ALU.subtract, ALU.mult).then_inc(xn_ready, 1)

            def negative_part(t, s, i):
                if again(t, 2):
                    dve.wait_ge(qk_ready, t - 1)
                nc.vector.tensor_copy(scale[:, s % 2:s % 2 + 1], at(r1, t)).then_inc(scale_ready, 1)
                dve.wait_ge(proj_made, t + 1)
                nc.vector.tensor_scalar(neg[:, s % 2, :], qk_ps[s % 2][:], 0.0, None, ALU.min
                                        ).then_inc(neg_ready, 1)

            def first_part(t, s, i):
                dve.wait_ge(hrow_ready, t + 1)
                nc.vector.tensor_copy(hparts[:, bass.ds(t, 1), 0, :].rearrange("p o n -> p (o n)"),
                                      hrow[:, s, 0:HX]).then_inc(part1_ready, 1)

            pipeline(dve, NT, [(2, negative_part), (0, normalise), (2, first_part)], R)

        @block.tensor
        def _(pe):
            def transpose_x(t, s, i):
                pe.wait_ge(xn_ready, t + 1)
                if again(t, 2):
                    pe.wait_ge(exp_ready, t - 1)
                for k in range(KC):
                    last = nc.tensor.transpose(xT_ps[s % 2][:, k * P:(k + 1) * P], xn[:, s, k * P:(k + 1) * P],
                                               c.ident[:])
                last.then_inc(xT_made, 1)

            def project(t, s, i):
                pe.wait_ge(xT_ready, t + 1)
                if again(t, 2):
                    pe.wait_ge(exp_ready, t - 1)
                for out, lo, n in ((hv_ps[s % 2][:, :], 0, 2 * D), (s_ps[s % 2], COL_S, 2 * HEADS),
                                   (qk_ps[s % 2][:, :], COL_QK, 2 * D)):
                    for k in range(KC):
                        last = nc.tensor.matmul(out, xT[:, s, k * P:(k + 1) * P], wall[:, k, lo:lo + n],
                                                start=(k == 0), stop=(k == KC - 1))
                last.then_inc(proj_made, 1)

            def sum_kv(t, s, i):
                first, last = (t == 0, t == LAST) if isinstance(t, int) else (False, False)
                rows = LAST_ROWS if last else P
                pe.wait_ge(qk_ready, t + 1)
                if isinstance(t, int) and t > LAST:
                    return
                for m in range(KC):
                    nc.tensor.matmul(kv_ps[:, m, :], v[0:rows, s, m * P:(m + 1) * P], qk[0:rows, s, D:2 * D],
                                     start=(first and m == 0), stop=last, skip_group_check=True)
                nc.tensor.matmul(ksum_ps, c.ones[0:rows, :], qk[0:rows, s, D:2 * D], start=first, stop=last,
                                 skip_group_check=True).then_inc(kv_used, 1)

            pipeline(pe, NT, [(0, transpose_x), (3, sum_kv), (1, project)], R)

        @block.scalar
        def _(act):
            def copy_xT(t, s, i):
                act.wait_ge(xT_made, t + 1)
                if again(t, R):
                    act.wait_ge(proj_made, t - R + 1)
                nc.scalar.copy(xT[:, s, :], xT_ps[s % 2]).then_inc(xT_ready, 1)

            def evacuate(t, s, i):
                act.wait_ge(proj_made, t + 1)
                if again(t, R):
                    act.wait_ge(h_out[s], 32 * i)
                    act.wait_ge(parts_made, t - R + 1)
                    act.wait_ge(kv_used, t - R + 1)
                nc.scalar.copy(hrow[:, s, D:HC], s_ps[s % 2])
                nc.scalar.copy(hrow[:, s, 0:D], hv_ps[s % 2][:, 0:D]).then_inc(hrow_ready, 1)
                act.wait_ge(scale_ready, t + 1)
                nc.scalar.activation(v[:, s, :], hv_ps[s % 2][:, D:2 * D], ACT.Copy, scale=scale[:, s % 2:s % 2 + 1])
                act.wait_ge(neg_ready, t + 1)
                nc.scalar.activation(pos[:, s % 2, :], qk_ps[s % 2][:], ACT.Relu, scale=scale[:, s % 2:s % 2 + 1])
                nc.scalar.activation(neg[:, s % 2, :], neg[:, s % 2, :], ACT.Exp, scale=scale[:, s % 2:s % 2 + 1]
                                     ).then_inc(exp_ready, 1)

            pipeline(act, NT, [(0, copy_xT), (1, evacuate)], R)

        @block.gpsimd
        def _(pool):
            def feature_map(t, s, i):
                pool.wait_ge(exp_ready, t + 1)
                if again(t, R):
                    if not (isinstance(t, int) and t - R >= LAST):
                        pool.wait_ge(kv_used, t - R + 1)
                    pool.wait_ge(q_out[s], 16 * i)
                nc.gpsimd.tensor_tensor(qk[:, s, :], pos[:, s % 2, :], neg[:, s % 2, :], ALU.add
                                        ).then_inc(qk_ready, 1)

            def parts(t, s, i):
                part = lambda j: hparts[:, bass.ds(t, 1), j, :].rearrange("p o n -> p (o n)")
                pool.wait_ge(part1_ready, t + 1)
                if again(t, 2):
                    pool.wait_ge(parts_made, t - 1)
                nc.gpsimd.tensor_tensor(rest[:, s % 2, :], hrow[:, s, 0:HX], part(0), ALU.subtract
                                        ).then_inc(rest_ready, 1)
                pool.wait_ge(rest_ready, t + 1)
                nc.gpsimd.tensor_copy(part(1), rest[:, s % 2, :]).then_inc(part2_ready, 1)
                pool.wait_ge(part2_ready, t + 1)
                nc.gpsimd.tensor_tensor(part(2), rest[:, s % 2, :], part(1), ALU.subtract).then_inc(parts_made, 1)

            pipeline(pool, NT, [(1, feature_map), (1, parts)], R)


def mix_weights(nc, c, w_out, mix, ksum):
    with ExitStack() as ctx:
        sb = lambda name, shape, dt=F32: ctx.enter_context(nc.sbuf_tensor(name, shape, dt))
        sem = semaphores(nc, ctx)
        wo, kv = sb("wo", [P, KC, D]), sb("kv", [P, KC, P])
        wo_in, kv_zero, kv_ready, mix_made = sem("wo_in"), sem("kv_zero"), sem("kv_ready"), sem("mix_made")
        block = ctx.enter_context(nc.Block())
        kv_ps = c.ps[4][:, :].rearrange("p (c n) -> p c n", c=KC)
        mix_ps = c.ps[0][:, :].rearrange("p (c n) -> p c n", c=KC)

        @block.sync
        def _(sp):
            sp.dma_start(wo[:], w_out.rearrange("(c p) n -> p c n", p=P)).then_inc(wo_in, 16)

        @block.vector
        def _(dve):
            nc.vector.memset(kv[:], 0.0).then_inc(kv_zero, 1)
            dve.wait_ge(kv_zero, 1)
            for hd in range(HEADS):
                rows, lo = slice(HD * hd % P, HD * hd % P + HD), HD * hd % P
                nc.vector.tensor_copy(kv[rows, HD * hd // P, lo:lo + HD],
                                      kv_ps[rows, HD * hd // P, HD * hd:HD * hd + HD]).then_inc(kv_ready, 1)
            nc.vector.tensor_copy(ksum[:], c.ps[5][:, 0:D])
            dve.wait_ge(mix_made, 1)
            nc.vector.tensor_copy(mix[:], mix_ps)

        @block.tensor
        def _(pe):
            pe.wait_ge(kv_ready, HEADS)
            pe.wait_ge(wo_in, 16)
            for m in range(KC):
                last = nc.tensor.matmul(mix_ps[:, m, :], kv[:, m, :], wo[:, m, :], start=True, stop=True)
            last.then_inc(mix_made, 1)


def plan_steps(nc, c, dst_t, src_t, attr_t, edge_w, wparts, dl, src, keys, blocks, block_row,
               attr_parts):
    with ExitStack() as ctx:
        sb = lambda name, shape, dt=F32: ctx.enter_context(nc.sbuf_tensor(name, shape, dt))
        sem = semaphores(nc, ctx)
        rows = ET // COUNT_P
        all_i, all_f = sb("all_i", [COUNT_P, rows * P], I32), sb("all_f", [COUNT_P, rows * P])
        below = sb("below", [COUNT_P, 2, rows * P], BF16)
        part = sb("part", [COUNT_P, NT])
        count = sb("count", [P, NT])
        ci, lo, hi = sb("ci", [P, NT], I32), sb("lo", [P, NT], I32), sb("hi", [P, NT], I32)
        steps_i = sb("steps_i", [P, NT], I32)
        lof, nsteps, some = sb("lof", [P, NT]), sb("nsteps", [P, NT]), sb("some", [P, NT])
        ends, starts = sb("ends", [P, NT]), sb("starts", [P, NT])
        base, dbase = sb("base", [P, NT]), sb("dbase", [P, NT])
        zero = sb("zero", [P, NT])
        pid = sb("pid", [P, SG])
        reached = sb("reached", [P, SG, 2, NT])
        nblocks, tbase, live = sb("nblocks", [P, SG]), sb("tbase", [P, SG]), sb("live", [P, SG])
        block_f, tile_f = sb("block_f", [P, SG]), sb("tile_f", [P, SG])
        block_i, tiles_i = sb("block_i", [P, SG], I32), sb("tiles_i", [P, SG, 2], I32)
        first_node = sb("first_node", [P, SG])
        dst_i, src_i = sb("dst_i", [P, 2 * SG, P], I32), sb("src_i", [P, 2 * SG, P], I32)
        dst_f, src_f = sb("dst_f", [P, 2 * SG, P]), sb("src_f", [P, 2 * SG, P])
        own = sb("own", [P, 2 * SG, P])
        attr = sb("attr", [P, 2 * SG, 4 * P])
        rest = sb("attr_rest", [P, 4 * P])
        split = sb("split", [P, SG, 3, 4, 2 * P], BF16)
        ew, ew_rest = sb("ew", [4, D]), sb("ew_rest", [4, D])
        ew_parts = sb("ew_parts", [4, 3, D], BF16)
        loaded, step_sem, counted, summed = sem("loaded"), sem("plan_step"), sem("counted"), sem("summed")
        tiles_ready, blocks_ready = sem("tiles_ready"), sem("blocks_ready")
        tables_in, attr_in = gather_semaphores(c, 2)
        iota_ready, split_ready = sem("iota_ready"), sem("split_ready")
        fields_ready, turned, taken, stored = sem("fields_ready"), sem("turned"), sem("taken"), sem("stored")
        ew_ready, wparts_in = sem("ew_ready"), sem("wparts_in")
        block = ctx.enter_context(nc.Block())

        @block.sync
        def _(sp):
            sp.dma_start(all_i[:], dst_t.rearrange("(p r) e -> p (r e)", p=COUNT_P)).then_inc(loaded, 16)
            sp.dma_start(ew[:], edge_w).then_inc(loaded, 16)
            sp.wait_ge(ew_ready, 3)
            for j in range(3):
                for i in range(3):
                    row = (j * 3 + i) * 4
                    sp.dma_start(wparts[row:row + 4, :], ew_parts[:, j, :]).then_inc(wparts_in, 16)
            sp.wait_ge(blocks_ready, 1)
            sp.dma_start(blocks.rearrange("o (g p) -> p (o g)", p=P), block_i[:],
                         allow_slow_non_contiguous=True).then_inc(stored, 16)
            sp.wait_ge(stored, 16)
            sp.dma_start(block_row[:], blocks).then_inc(stored, 16)
            for g in range(SG):
                sp.wait_ge(split_ready, g + 1)
                for i in range(3):
                    sp.dma_start(attr_parts[i * 4:i * 4 + 4, g * P:(g + 1) * P, :].rearrange("c p e -> p c e"),
                                 split[:, g, i, :, :]).then_inc(stored, 16)
            sp.wait_ge(stored, 16 * (2 + 3 * SG))
            sp.wait_ge(wparts_in, 9 * 16)

        @block.gpsimd
        def _(pool):
            nc.gpsimd.iota(pid[:], [[P, SG]], base=0, channel_multiplier=1,
                           allow_small_or_imprecise_dtypes=True).then_inc(iota_ready, 1)
            pool.wait_ge(tiles_ready, 1)
            for g in range(SG):
                for e in range(2):
                    at = bass.IndirectOffsetOnAxis(ap=tiles_i[:, g, e:e + 1], axis=0)
                    j = 2 * g + e
                    nc.gpsimd.indirect_dma_start(dst_i[:, j, :], None, dst_t, at).then_inc(tables_in, 16)
                    nc.gpsimd.indirect_dma_start(src_i[:, j, :], None, src_t, at).then_inc(tables_in, 16)
                    nc.gpsimd.indirect_dma_start(attr[:, j, :], None, attr_t, at).then_inc(attr_in, 16)

        @block.vector
        def _(dve):
            step = Steps()

            def done(ins):
                ins.then_inc(step_sem, 1)
                dve.wait_ge(step_sem, step.last())

            V = nc.vector
            dve.wait_ge(loaded, 32)
            V.tensor_copy(ew_parts[:, 0, :], ew[:]).then_inc(ew_ready, 1)
            dve.wait_ge(ew_ready, 1)
            done(V.tensor_tensor(ew_rest[:], ew[:], ew_parts[:, 0, :], ALU.subtract))
            V.tensor_copy(ew_parts[:, 1, :], ew_rest[:]).then_inc(ew_ready, 1)
            dve.wait_ge(ew_ready, 2)
            V.tensor_tensor(ew_parts[:, 2, :], ew_rest[:], ew_parts[:, 1, :], ALU.subtract).then_inc(ew_ready, 1)
            done(V.memset(zero[:], 0.0))
            done(V.tensor_copy(all_f[:], all_i[:]))
            for b in range(NT):
                if b >= 2:
                    dve.wait_ge(counted, b - 1)
                V.tensor_scalar(below[:, b % 2, :], all_f[:], float(b * P), 0.0, ALU.is_lt, ALU.add,
                                accum_out=part[:, b:b + 1]).then_inc(counted, 1)
            dve.wait_ge(summed, 1)
            done(V.tensor_copy(count[:], c.ps[0][:, 0:NT]))
            done(V.tensor_copy(ci[:], count[:]))
            B = NT - 1
            done(V.tensor_single_scalar(lo[:], ci[:], 7, ALU.arith_shift_right))
            done(V.tensor_scalar(count[:], count[:], 127.0, None, ALU.add))
            done(V.tensor_copy(ci[:], count[:]))
            done(V.tensor_single_scalar(hi[:], ci[:], 7, ALU.arith_shift_right))
            done(V.tensor_copy(lof[:], lo[:]))
            done(V.tensor_copy(nsteps[:], hi[:]))
            done(V.tensor_tensor(some[:, 0:B], count[:, 1:NT], count[:, 0:B], ALU.is_gt))
            done(V.tensor_tensor(ends[:, 0:B], nsteps[:, 1:NT], lof[:, 0:B], ALU.subtract))
            done(V.tensor_tensor(ends[:, 0:B], ends[:, 0:B], some[:, 0:B], ALU.mult))
            done(V.tensor_scalar(ends[:, 0:B], ends[:, 0:B], 1.0, None, ALU.add))
            done(V.tensor_copy(steps_i[:, 0:B], ends[:, 0:B]))
            done(V.tensor_single_scalar(steps_i[:, 0:B], steps_i[:, 0:B], 1, ALU.arith_shift_right))
            done(V.tensor_copy(nsteps[:, 0:B], steps_i[:, 0:B]))
            done(V.tensor_tensor_scan(ends[:, 0:B], nsteps[:, 0:B], zero[:, 0:B], 0.0, ALU.add, ALU.add))
            done(V.tensor_tensor(starts[:, 0:B], ends[:, 0:B], nsteps[:, 0:B], ALU.subtract))
            done(V.scalar_tensor_tensor(out=base[:, 0:B], in0=starts[:, 0:B], scalar=-2.0, in1=lof[:, 0:B],
                                        op0=ALU.mult, op1=ALU.add))
            done(V.tensor_copy(dbase[:, 0:1], base[:, 0:1]))
            done(V.tensor_tensor(dbase[:, 1:B], base[:, 1:B], base[:, 0:B - 1], ALU.subtract))
            dve.wait_ge(iota_ready, 1)
            for g in range(SG):
                done(V.tensor_scalar(reached[:, g, 0, 0:B], starts[:, 0:B], pid[:, g:g + 1], None, ALU.is_le))
                done(V.tensor_tensor(reached[:, g, 1, 0:B], reached[:, g, 0, 0:B], dbase[:, 0:B], ALU.mult))
                done(V.tensor_reduce(nblocks[:, g:g + 1], reached[:, g, 0, 0:B], AX.X, ALU.add))
                done(V.tensor_reduce(tbase[:, g:g + 1], reached[:, g, 1, 0:B], AX.X, ALU.add))
            done(V.tensor_scalar(live[:], pid[:], ends[:, B - 1:B], None, ALU.is_lt))
            done(V.tensor_scalar(block_f[:], nblocks[:], -1.0 - B, None, ALU.add))
            done(V.tensor_tensor(block_f[:], block_f[:], live[:], ALU.mult))
            done(V.tensor_scalar(block_f[:], block_f[:], float(B), None, ALU.add))
            done(V.scalar_tensor_tensor(out=tile_f[:], in0=pid[:], scalar=2.0, in1=tbase[:], op0=ALU.mult,
                                        op1=ALU.add))
            done(V.tensor_scalar(tile_f[:], tile_f[:], -(ET - 2.0), None, ALU.add))
            done(V.tensor_tensor(tile_f[:], tile_f[:], live[:], ALU.mult))
            done(V.tensor_scalar(tile_f[:], tile_f[:], ET - 2.0, None, ALU.add))
            V.tensor_copy(block_i[:], block_f[:]).then_inc(blocks_ready, 1)
            done(V.tensor_copy(tiles_i[:, :, 0], tile_f[:]))
            done(V.tensor_scalar(tile_f[:], tile_f[:], 1.0, None, ALU.add))
            V.tensor_copy(tiles_i[:, :, 1], tile_f[:]).then_inc(tiles_ready, 1)
            done(V.tensor_scalar(first_node[:], block_f[:], float(P), None, ALU.mult))
            dve.wait_ge(tables_in, 4 * SG * 16)
            done(V.tensor_copy(dst_f[:], dst_i[:]))
            V.tensor_copy(src_f[:], src_i[:]).then_inc(fields_ready, 1)
            for g in range(SG):
                own_g, dst_g = own[:, 2 * g:2 * g + 2, :], dst_f[:, 2 * g:2 * g + 2, :]
                done(V.tensor_scalar(dst_g, dst_g, first_node[:, g:g + 1], None, ALU.subtract))
                done(V.tensor_scalar(own_g, dst_g, 0.0, None, ALU.is_ge))
                done(V.scalar_tensor_tensor(out=own_g, in0=dst_g, scalar=float(P), in1=own_g, op0=ALU.is_lt,
                                            op1=ALU.mult))
                done(V.tensor_scalar(first_node[:, g:g + 1], first_node[:, g:g + 1], 1.0, None, ALU.add))
                V.scalar_tensor_tensor(out=own_g, in0=dst_g, scalar=first_node[:, g:g + 1], in1=own_g,
                                       op0=ALU.add, op1=ALU.mult).then_inc(fields_ready, 1)
            for g in range(SG):
                lo_, hi_ = g * P, min(NS, (g + 1) * P)
                dve.wait_ge(turned, g + 1)
                for j, (field, out) in enumerate(((0, dl), (1, src), (2, keys))):
                    bank = c.ps[1 + 3 * (g % 2) + j][:, 0:2 * P].rearrange("p (e n) -> p n e", e=2)
                    done(V.tensor_copy(out[:, lo_:hi_, :], bank[:, 0:hi_ - lo_, :]))
                dve.sem_inc(taken, 1)
            dve.wait_ge(attr_in, 2 * SG * 16)
            for g in range(SG):
                for e in range(2):
                    a = attr[:, 2 * g + e, :]
                    cut = lambda i: split[:, g, i, :, e * P:(e + 1) * P]
                    r = rest[:].rearrange("p (c e) -> p c e", c=4)
                    a = a.rearrange("p (c e) -> p c e", c=4)
                    done(V.tensor_copy(cut(0), a))
                    done(V.tensor_tensor(r, a, cut(0), ALU.subtract))
                    done(V.tensor_copy(cut(1), r))
                    done(V.tensor_tensor(cut(2), r, cut(1), ALU.subtract))
                dve.sem_inc(split_ready, 1)

        @block.tensor
        def _(pe):
            pe.wait_ge(counted, NT)
            nc.tensor.matmul(c.ps[0][:, 0:NT], c.ones[0:COUNT_P, :], part[:], start=True, stop=True
                             ).then_inc(summed, 1)
            pe.wait_ge(fields_ready, 1 + SG)
            for g in range(SG):
                if g >= 2:
                    pe.wait_ge(taken, g - 1)
                for j, field in enumerate((dst_f, src_f, own)):
                    for e in range(2):
                        last = nc.tensor.transpose(c.ps[1 + 3 * (g % 2) + j][:, e * P:(e + 1) * P],
                                                   field[:, 2 * g + e, :], c.ident[:])
                last.then_inc(turned, 1)


QUAD = 4
TILES = 2 * QUAD
NQ = NS // QUAD
assert NS % QUAD == 0


def load_blocks(nc, eng, block_row, q):
    _, blocks = nc.values_load_multi_w_load_instructions(block_row[0:1, bass.ds(q * QUAD, QUAD)], engines=[eng],
                                                         min_val=0, max_val=NT - 1)
    return blocks


def score_edges(nc, c, wparts, hparts, stab, attr_parts, dl, src, block_row, alpha):
    with ExitStack() as ctx:
        sb = lambda name, shape, dt=F32: ctx.enter_context(nc.sbuf_tensor(name, shape, dt))
        sem = semaphores(nc, ctx)
        att = sb("att_cols", [36, 2, QUAD * 2 * P], BF16)
        onehot, onehotT = sb("onehot", [P, 2, TILES, P], BF16), sb("onehotT", [P, 2, TILES, P], BF16)
        R = 4
        stage, ssrc = sb("src_stage", [P, R, TILES], I32), sb("ssrc", [P, R, TILES, HEADS])
        enc, prod = sb("enc", [P, 2, 2 * D]), sb("eprod", [P, 2, 2 * D])
        red = sb("red", [P, 2, TILES, HEADS])
        att_in = [sem(f"attr_in{s}") for s in range(2)]
        ssrc_in = gather_semaphores(c, R)
        staged, onehot_ready, turned, onehotT_ready = (
            sem("staged"), sem("onehot_ready"), sem("onehot_turned"), sem("onehotT_ready"))
        enc_made, enc_ready, hdst_made, prod_ready = (
            sem("enc_made"), sem("enc_ready"), sem("hdst_made"), sem("eprod_ready"))
        red_ready, sum_step, alpha_ready = sem("red_ready"), sem("sum_step"), sem("alpha_ready")
        block = ctx.enter_context(nc.Block())
        turn_ps = [c.ps[b][:, :].bitcast(BF16).rearrange("p (k e) -> p k e", k=TILES) for b in (0, 1)]
        enc_ps, hdst_ps = [c.ps[2], c.ps[3]], [c.ps[4], c.ps[5]]
        sdst_ps = [c.ps[b][:, 0:TILES * HEADS] for b in (6, 7)]

        @block.sync
        def _(sp):
            def load(q, s, i):
                if again(q, 2):
                    sp.wait_ge(enc_made, QUAD * (q - 1))
                for j in range(3):
                    sp.dma_start(att[12 * j:12 * j + 12, s, :],
                                 attr_parts[:, bass.ds(q * QUAD, QUAD), :].rearrange("c p e -> c (p e)")
                                 ).then_inc(att_in[s], 16)

            pipeline(sp, NQ, [(0, load)])

        @block.gpsimd
        def _(pool):
            def gather(q, s, i):
                if again(q, R):
                    pool.wait_ge(ssrc_in[s], 16 * TILES * i)
                    pool.wait_ge(alpha_ready, q - R + 1)
                nc.gpsimd.tensor_copy(stage[:, s, :], src[:, bass.ds(q * QUAD, QUAD), :].rearrange(
                    "p n e -> p (n e)")).then_inc(staged, 1)
                wait_apart(pool, staged, q + 1, c.passed)
                for k in range(TILES):
                    nc.gpsimd.indirect_dma_start(
                        ssrc[:, s, k, :], None, stab,
                        bass.IndirectOffsetOnAxis(ap=stage[:, s, k:k + 1], axis=0)).then_inc(ssrc_in[s], 16)

            pipeline(pool, NQ, [(0, gather)], R)

        @block.tensor
        def _(pe):
            def turn(q, s, i):
                pe.wait_ge(onehot_ready, q + 1)
                if again(q, 2):
                    pe.wait_ge(onehotT_ready, q - 1)
                for k in range(TILES):
                    last = nc.tensor.transpose(turn_ps[s][:, k, :], onehot[:, s, k, :], c.ident16[:])
                last.then_inc(turned, 1)

            def expand(q, s, i):
                blk = load_blocks(nc, mybir.EngineType.PE, block_row, q)
                pe.wait_ge(att_in[s], 48 * (i + 1))
                pe.wait_ge(onehotT_ready, q + 1)
                if again(q, 2):
                    pe.wait_ge(alpha_ready, q - 1)
                for k in range(QUAD):
                    u, b = q * QUAD + k, k % 2
                    if again(u, 2):
                        pe.wait_ge(enc_ready, u - 1)
                    for e in range(2):
                        t = 2 * k + e
                        last = nc.tensor.matmul(enc_ps[b][:, e * D:(e + 1) * D], att[:, s, t * P:(t + 1) * P],
                                                wparts[:], start=True, stop=True)
                    last.then_inc(enc_made, 1)
                    if again(u, 2):
                        pe.wait_ge(prod_ready, u - 1)
                    rows = lambda j, lo, hi: hparts[:, bass.ds(blk[k], 1), j, lo:hi].rearrange("p o n -> p (o n)")
                    for e in range(2):
                        t = 2 * k + e
                        for j in range(3):
                            nc.tensor.matmul(hdst_ps[b][:, e * D:(e + 1) * D], onehotT[:, s, t, :], rows(j, 0, D),
                                             start=(j == 0), stop=(j == 2))
                        for j in range(3):
                            last = nc.tensor.matmul(sdst_ps[s][:, t * HEADS:(t + 1) * HEADS], onehotT[:, s, t, :],
                                                    rows(j, D, HX), start=(j == 0), stop=(j == 2))
                    last.then_inc(hdst_made, 1)

            pipeline(pe, NQ, [(1, expand), (0, turn)])

        @block.scalar
        def _(act):
            def copy_onehotT(q, s, i):
                act.wait_ge(turned, q + 1)
                if again(q, 2):
                    act.wait_ge(hdst_made, QUAD * (q - 1))
                nc.scalar.copy(onehotT[:, s, :, :], turn_ps[s]).then_inc(onehotT_ready, 1)

            def relu(q, s, i):
                for k in range(QUAD):
                    u, b = q * QUAD + k, k % 2
                    act.wait_ge(enc_made, u + 1)
                    if again(u, 2):
                        act.wait_ge(prod_ready, u - 1)
                    nc.scalar.activation(enc[:, b, :], enc_ps[b][:], ACT.Relu).then_inc(enc_ready, 1)

            pipeline(act, NQ, [(1, relu), (0, copy_onehotT)])

        @block.vector
        def _(dve):
            V = nc.vector

            def onehots(q, s, i):
                if again(q, 2):
                    dve.wait_ge(turned, q - 1)
                for k in range(TILES):
                    last = V.tensor_scalar(
                        onehot[:, s % 2, k, :], c.lane16[:],
                        dl[:, bass.ds(q * QUAD + k // 2, 1), k % 2:k % 2 + 1].rearrange("p a b -> p (a b)"),
                        None, ALU.is_equal)
                last.then_inc(onehot_ready, 1)

            def score(q, s, i):
                for k in range(QUAD + 1):
                    if k < QUAD:
                        u, b = q * QUAD + k, k % 2
                        dve.wait_ge(enc_ready, u + 1)
                        dve.wait_ge(hdst_made, u + 1)
                        if again(u, 2):
                            dve.wait_ge(red_ready, u - 1)
                        V.tensor_tensor(prod[:, b, :], hdst_ps[b][:], enc[:, b, :], ALU.mult).then_inc(prod_ready, 1)
                    if k > 0:
                        u, b = q * QUAD + k - 1, (k - 1) % 2
                        dve.wait_ge(prod_ready, u + 1)
                        V.tensor_reduce(red[:, s % 2, 2 * k - 2:2 * k, :],
                                        prod[:, b, :].rearrange("p (e h d) -> p e h d", e=2, h=HEADS), AX.X, ALU.add
                                        ).then_inc(red_ready, 1)

            def close(q, s, i):
                dve.wait_ge(red_ready, QUAD * (q + 1))
                r = red[:, s % 2, :, :].rearrange("p k h -> p (k h)")
                V.tensor_tensor(r, sdst_ps[s % 2], r, ALU.add).then_inc(sum_step, 1)
                dve.wait_ge(sum_step, 2 * q + 1)
                dve.wait_ge(ssrc_in[s], 16 * TILES * (i + 1))
                V.tensor_tensor(r, r, ssrc[:, s, :, :].rearrange("p k h -> p (k h)"), ALU.add).then_inc(sum_step, 1)
                dve.wait_ge(sum_step, 2 * q + 2)
                V.scalar_tensor_tensor(out=alpha[:, bass.ds(q * TILES * HEADS, TILES * HEADS)], in0=r, scalar=0.2,
                                       in1=r, op0=ALU.mult, op1=ALU.max).then_inc(alpha_ready, 1)

            pipeline(dve, NQ, [(2, close), (0, onehots), (1, score)], R)


RANGES = P // HEADS
RC = 2 * NS // RANGES
RL = RC * P
FAR = 1e30
assert RC * RANGES == 2 * NS


def softmax_numerators(nc, c, keys, alpha, a, key, cross):
    with ExitStack() as ctx:
        sb = lambda name, shape, dt=F32: ctx.enter_context(nc.sbuf_tensor(name, shape, dt))
        sem = semaphores(nc, ctx)
        cut, top = sb("cut", [P, RL + 1]), sb("top", [P, RL])
        edge = sb("edge_keys", [P, 2])
        ends = sb("range_ends", [P, 2])
        row = sb("range_rows", [HEADS, 2, RANGES])
        carried = sb("carried", [HEADS, RANGES + 1])
        carry = sb("carry", [P, 2])
        turned, copied, ready, dma, step_sem = (
            sem("rows_turned"), sem("rows_copied"), sem("rows_ready"), sem("carry_dma"), sem("softmax_step"))
        wants_dma, back, back_copied = sem("wants_dma"), sem("turned_back"), sem("back_copied")
        exp_ready, ordered = sem("num_exp_ready"), sem("ordered")
        block = ctx.enter_context(nc.Block())
        groups = [(g0, min(4, RC - g0)) for g0 in range(0, RC, 4)]
        by_head = lambda x: x.rearrange("p (g t h) -> p t g h", g=RANGES, h=HEADS)
        key_cols = keys[:].rearrange("p n e -> p (n e)").rearrange("p (g t) -> p t g", g=RANGES)

        @block.tensor
        def _(pe):
            pe.wait_ge(ordered, 2)
            for n, (g0, w) in enumerate(groups):
                for j in range(2):
                    m = 2 * n + j
                    if m >= 4:
                        pe.wait_ge(copied, m - 3)
                    for t in range(w):
                        last = nc.tensor.transpose(c.ps[m % 4][:, t * P:(t + 1) * P],
                                                   (top, cut)[j][:, (g0 + t) * P:(g0 + t + 1) * P], c.ident[:])
                    last.then_inc(turned, 1)
            for n, (g0, w) in enumerate(groups):
                pe.wait_ge(exp_ready, 1)
                if n >= 4:
                    pe.wait_ge(back_copied, n - 3)
                for t in range(w):
                    last = nc.tensor.transpose(c.ps[4 + n % 4][:, t * P:(t + 1) * P],
                                               a[:, (g0 + t) * P:(g0 + t + 1) * P], c.ident[:])
                last.then_inc(back, 1)

        @block.scalar
        def _(act):
            nc.scalar.copy(top[:].rearrange("p (t g h) -> p t g h", g=RANGES, h=HEADS), by_head(alpha[:])
                           ).then_inc(ordered, 1)
            for n, (g0, w) in enumerate(groups):
                for j, out in enumerate((a, key)):
                    act.wait_ge(turned, 2 * n + j + 1)
                    nc.scalar.copy(out[:, g0 * P:(g0 + w) * P], c.ps[(2 * n + j) % 4][:, 0:w * P]
                                   ).then_inc(copied, 1)
            act.wait_ge(ready, 1)
            nc.scalar.activation(a, a, ACT.Exp).then_inc(ready, 1)
            for n, (g0, w) in enumerate(groups):
                act.wait_ge(back, n + 1)
                nc.scalar.copy(by_head(alpha[:])[:, g0:g0 + w],
                               c.ps[4 + n % 4][:, 0:w * P].rearrange("p (t g h) -> p t g h", t=w, g=RANGES)
                               ).then_inc(back_copied, 1)

        @block.sync
        def _(sp):
            n = 0

            def move(out, in_):
                nonlocal n
                sp.dma_start(out, in_, allow_slow_non_contiguous=True).then_inc(dma, 16)
                n += 1
                sp.wait_ge(dma, 16 * n)

            sp.wait_ge(wants_dma, 1)
            move(edge[HEADS:P, 0:1], key[0:P - HEADS, RL - 1:RL])
            move(edge[0:P - HEADS, 1:2], key[HEADS:P, 0:1])
            for d in range(2):
                sp.wait_ge(wants_dma, 2 + 2 * d)
                move(cross[d, :, :].rearrange("j p -> p j"), ends[:])
                move(row[:], cross[d, :, :].rearrange("j (g h) -> h j g", h=HEADS))
                sp.wait_ge(wants_dma, 3 + 2 * d)
                move(cross[2 + d, 0, :].rearrange("(g h) -> h g", h=HEADS),
                     carried[:, 0:RANGES] if d == 0 else carried[:, 1:RANGES + 1])
                move(carry[:, d:d + 1], cross[2 + d, 0, :].rearrange("(p o) -> p o", o=1))

        @block.vector
        def _(dve):
            V, step = nc.vector, Steps()

            def done(ins):
                ins.then_inc(step_sem, 1)
                dve.wait_ge(step_sem, step.last())

            V.tensor_copy(cut[:, 0:RL].rearrange("p (t g h) -> p t g h", g=RANGES, h=HEADS),
                          key_cols.unsqueeze(3).broadcast_to([P, RC, RANGES, HEADS])).then_inc(ordered, 1)
            V.memset(edge[:, 0:1], -1.0)
            done(V.memset(edge[:, 1:2], -1.0))
            dve.wait_ge(copied, 2 * len(groups))
            dve.sem_inc(wants_dma, 1)
            done(V.tensor_scalar(top[:], key, 0.0, None, ALU.is_gt))
            done(V.tensor_tensor(a, a, top[:], ALU.mult))
            done(V.tensor_scalar(top[:], top[:], -1.0, FAR, ALU.add, ALU.mult))
            done(V.tensor_tensor(a, a, top[:], ALU.add))
            done(V.tensor_tensor(cut[:, 1:RL], key[:, 1:RL], key[:, 0:RL - 1], ALU.not_equal))
            dve.wait_ge(dma, 32)
            done(V.tensor_tensor(cut[:, 0:1], key[:, 0:1], edge[:, 0:1], ALU.not_equal))
            done(V.tensor_tensor(cut[:, RL:RL + 1], key[:, RL - 1:RL], edge[:, 1:2], ALU.not_equal))
            done(V.tensor_scalar(cut[:], cut[:], -FAR, None, ALU.mult))
            for d in range(2):
                if d == 0:
                    cuts, vals, out, last = cut[:, 0:RL], a, top[:], top[:, RL - 1:RL]
                else:
                    cuts, vals, out, last = cut[:, RL:0:-1], top[:, ::-1], top[:, ::-1], top[:, 0:1]
                if d == 0:
                    done(V.tensor_tensor_scan(out, cuts, vals, -FAR, ALU.add, ALU.max))
                else:
                    done(V.tensor_tensor_scan(key[:, ::-1], cuts, vals, -FAR, ALU.add, ALU.max))
                    last = key[:, 0:1]
                V.tensor_copy(ends[:, 1:2], last)
                done(V.tensor_reduce(ends[:, 0:1], cuts, AX.X, ALU.min))
                dve.sem_inc(wants_dma, 1)
                dve.wait_ge(dma, 32 + 32 + 64 * d)
                if d == 0:
                    done(V.memset(carried[:, 0:1], -FAR))
                    done(V.tensor_tensor_scan(carried[:, 1:], row[:, 0, :], row[:, 1, :], -FAR, ALU.add, ALU.max))
                else:
                    done(V.memset(carried[:, RANGES:], -FAR))
                    done(V.tensor_tensor_scan(carried[:, RANGES - 1::-1], row[:, 0, ::-1], row[:, 1, ::-1], -FAR,
                                              ALU.add, ALU.max))
                dve.sem_inc(wants_dma, 1)
                dve.wait_ge(dma, 32 + 64 + 64 * d)
                if d == 0:
                    done(V.tensor_tensor_scan(out, cuts, vals, carry[:, 0:1], ALU.add, ALU.max))
                else:
                    done(V.tensor_tensor_scan(key[:, ::-1], cuts, vals, carry[:, 1:2], ALU.add, ALU.max))
            done(V.tensor_scalar(top[:], a, -0.5 * FAR, None, ALU.is_gt))
            V.tensor_tensor(a, a, key, ALU.subtract).then_inc(ready, 1)
            dve.wait_ge(ready, 2)
            V.tensor_tensor(a, a, top[:], ALU.mult).then_inc(exp_ready, 1)


NN = NT - 1


def sum_messages_and_mix(nc, c, htab, dl, src, block_row, alpha, acc, mix, ksum, x, bias, b_out, w_norm2, qtab,
                         xntab, ytab):
    with ExitStack() as ctx:
        sb = lambda name, shape, dt=F32: ctx.enter_context(nc.sbuf_tensor(name, shape, dt))
        sem = semaphores(nc, ctx)
        R = 4
        onehot = sb("onehot32", [P, 2, TILES, P])
        stage, msg = sb("src_stage2", [P, R, TILES], I32), sb("msg", [P, R, TILES, HX])
        rows_in = gather_semaphores(c, R)
        staged, onehot_ready, msg_ready, sums_made = (
            sem("staged2"), sem("onehot32_ready"), sem("msg_ready"), sem("sums_made"))
        acc_ready, weights_ready = sem("acc_ready"), sem("weights_ready")
        rows_sb = sb("rows_in", [P, 2, D])
        b_row = sb("b_row", [1, D])
        q2, xn2, x2 = sb("q2", [P, 2, D]), sb("xn2", [P, 2, D]), sb("x2", [P, 2, D])
        prod, qz, qT = sb("prod", [P, 2, D]), sb("qz", [P, 2, D]), sb("qT", [P, 2, D])
        den, z = sb("den", [P, 2, HEADS]), sb("z", [P, 2, HEADS])
        h, scaled = sb("h2", [P, 2, D]), sb("h2_scaled", [P, 2, D])
        ss, r2 = sb("ss", [P, 2]), sb("r2", [P, 2])
        y = sb("y", [P, 2, D])
        setup_in = sem("setup_in")
        qx_in = [sem(f"qx_in{s}") for s in range(2)]
        x_in = [sem(f"x2_in{s}") for s in range(2)]
        y_out = [sem(f"y_out{s}") for s in range(2)]
        q_step, y_step = sem("mix_q_step"), sem("mix_y_step")
        qz_ready, qT_made, qT_ready, att_made = sem("qz_ready"), sem("qT_made"), sem("qT_ready"), sem("att_made")
        h_ready, ss_ready, mean_ready, r2_ready, y_ready = (
            sem("h_ready"), sem("ss_ready"), sem("mean_ready"), sem("r2_ready"), sem("y_ready"))
        block = ctx.enter_context(nc.Block())
        SB = 4
        sum_ps = [c.ps[b][:, 0:HX] for b in range(SB)]
        qT_ps = [c.ps[b][:, 0:D] for b in (4, 5)]
        att_ps = [c.ps[b][:, 0:D] for b in (6, 7)]
        heads = lambda ap: ap.rearrange("p (h d) -> p h d", h=HEADS)
        NM = 2 * NN

        def tile_of(fn):
            def run(q, s, i):
                if s % 2 == 0:
                    fn(2 * i + s // 2, s // 2, i)
            return run

        @block.sync
        def _(sp):
            for j, row in enumerate((bias, w_norm2)):
                sp.dma_start(rows_sb[:, j, :], row.rearrange("(o d) -> o d", o=1).broadcast_to([P, D])
                             ).then_inc(setup_in, 16)
            sp.dma_start(b_row[:], b_out.rearrange("(o d) -> o d", o=1)).then_inc(setup_in, 16)

            def load_qx(t, s, i):
                if again(t, 2):
                    sp.wait_ge(h_ready, t - 1)
                for buf, table in ((q2, qtab), (xn2, xntab)):
                    sp.dma_start(buf[:, s, :], table[bass.ds(t * P, P), :]).then_inc(qx_in[s], 16)

            def load_x(t, s, i):
                if again(t, 2):
                    sp.wait_ge(y_ready, t - 1)
                sp.dma_start(x2[:, s, :], x[bass.ds(t * P, P), :]).then_inc(x_in[s], 16)

            def store(t, s, i):
                sp.wait_ge(y_ready, t + 1)
                sp.dma_start(ytab[bass.ds(t * P, P), :], y[:, s, :]).then_inc(y_out[s], 16)

            pipeline(sp, NM, [(0, tile_of(load_qx)), (2, tile_of(load_x)), (6, tile_of(store))], R)
            for s in range(2):
                sp.wait_ge(y_out[s], 16 * len(range(s, NN, 2)))

        @block.gpsimd
        def _(pool):
            def gather(q, s, i):
                if again(q, R):
                    pool.wait_ge(rows_in[s], 16 * TILES * i)
                    pool.wait_ge(sums_made, QUAD * (q - R + 1))
                nc.gpsimd.tensor_copy(stage[:, s, :], src[:, bass.ds(q * QUAD, QUAD), :].rearrange(
                    "p n e -> p (n e)")).then_inc(staged, 1)
                wait_apart(pool, staged, q + 1, c.passed)
                for k in range(TILES):
                    nc.gpsimd.indirect_dma_start(
                        msg[:, s, k, 0:D], None, htab,
                        bass.IndirectOffsetOnAxis(ap=stage[:, s, k:k + 1], axis=0)).then_inc(rows_in[s], 16)

            def inverse(t, s, i):
                if again(t, 2):
                    pool.wait_ge(y_ready, t - 1)
                wait_apart(pool, ss_ready, t + 1, c.passed)
                nc.gpsimd.tensor_scalar(r2[:, s:s + 1], ss[:, s:s + 1], 1.0 / D, RMS_EPS, ALU.mult,
                                        ALU.add).then_inc(mean_ready, 1)
                pool.wait_ge(mean_ready, t + 1)
                nc.gpsimd.tensor_tensor(r2[:, s:s + 1], r2[:, s:s + 1], c.minus_half[:],
                                        ALU.pow).then_inc(r2_ready, 1)

            pipeline(pool, NQ, [(6, tile_of(inverse), NM), (0, gather)], R)

        @block.vector
        def _(dve):
            V = nc.vector
            V.memset(acc, 0.0).then_inc(acc_ready, 1)
            dve.wait_ge(setup_in, 48)

            def onehots(q, s, k):
                for e in range(2):
                    V.tensor_scalar(onehot[:, s % 2, 2 * k + e, :], c.lane16[:],
                                    dl[:, bass.ds(q * QUAD + k, 1), e:e + 1].rearrange("p a b -> p (a b)"),
                                    None, ALU.is_equal).then_inc(onehot_ready, 1)

            def steps(q, s, i):
                inside = not isinstance(q, int)
                if again(q, 1):
                    blk = load_blocks(nc, mybir.EngineType.DVE, block_row, q - 1)
                if inside or q < NQ:
                    dve.wait_ge(rows_in[s], 16 * TILES * (i + 1))
                for k in range(QUAD):
                    if inside or q < NQ:
                        m = msg[:, s, 2 * k:2 * k + 2, 0:D].rearrange("p e (h d) -> p e h d", h=HEADS)
                        w = alpha[:, bass.ds((q * QUAD + k) * 2 * HEADS, 2 * HEADS)].rearrange("p (e h) -> p e h", e=2)
                        V.tensor_tensor(m, m, w.unsqueeze(3).broadcast_to([P, 2, HEADS, HD]), ALU.mult
                                        ).then_inc(msg_ready, 1)
                    if again(q, 1):
                        u = (q - 1) * QUAD + k
                        rows = acc[:, bass.ds(blk[k], 1), :].rearrange("p o n -> p (o n)")
                        dve.wait_ge(sums_made, u + 1)
                        dve.wait_ge(acc_ready, u + 1)
                        V.tensor_tensor(rows, sum_ps[k % SB], rows, ALU.add).then_inc(acc_ready, 1)
                    if inside or q + 1 < NQ:
                        onehots(q + 1, s + 1, k)

            def normalise_q(t, s, i):
                dve.wait_ge(qx_in[s], 32 * (i + 1))
                V.tensor_tensor(prod[:, s, :], q2[:, s, :], ksum[:], ALU.mult).then_inc(q_step, 1)
                dve.wait_ge(q_step, 4 * t + 1)
                V.tensor_reduce(den[:, s, :], heads(prod[:, s, :]), AX.X, ALU.add).then_inc(q_step, 1)
                dve.wait_ge(q_step, 4 * t + 2)
                V.tensor_scalar(den[:, s, :], den[:, s, :], ATT_EPS, None, ALU.add).then_inc(q_step, 1)
                dve.wait_ge(q_step, 4 * t + 3)
                V.reciprocal(z[:, s, :], den[:, s, :]).then_inc(q_step, 1)
                dve.wait_ge(q_step, 4 * t + 4)
                if again(t, 2):
                    dve.wait_ge(qT_made, t - 1)
                V.tensor_tensor(heads(qz[:, s, :]), heads(q2[:, s, :]),
                                z[:, s, :].unsqueeze(2).broadcast_to([P, HEADS, HD]), ALU.mult).then_inc(qz_ready, 1)

            def add_residual(t, s, i):
                dve.wait_ge(att_made, t + 1)
                if again(t, 2):
                    dve.wait_ge(ss_ready, t - 1)
                V.tensor_tensor(h[:, s, :], att_ps[s], xn2[:, s, :], ALU.add).then_inc(h_ready, 1)

            def finish(t, s, i):
                if again(t, 2):
                    dve.wait_ge(y_out[s], 16 * i)
                dve.wait_ge(x_in[s], 16 * (i + 1))
                V.tensor_tensor(y[:, s, :], x2[:, s, :], rows_sb[:, 0, :], ALU.add)
                dve.wait_ge(r2_ready, t + 1)
                V.scalar_tensor_tensor(out=scaled[:, s, :], in0=h[:, s, :], scalar=r2[:, s:s + 1],
                                       in1=rows_sb[:, 1, :], op0=ALU.mult, op1=ALU.mult).then_inc(y_step, 1)
                dve.wait_ge(y_step, 2 * t + 1)
                V.tensor_tensor(y[:, s, :], y[:, s, :], h[:, s, :], ALU.add).then_inc(y_step, 1)
                dve.wait_ge(y_step, 2 * t + 2)
                V.tensor_tensor(y[:, s, :], y[:, s, :], scaled[:, s, :], ALU.add).then_inc(y_ready, 1)

            for k in range(QUAD):
                onehots(0, 0, k)
            pipeline(dve, NQ, [(0, tile_of(normalise_q), NM), (3, tile_of(add_residual), NM), (0, steps, NQ + 1),
                               (6, tile_of(finish), NM)], R)

        @block.tensor
        def _(pe):
            pe.wait_ge(setup_in, 48)

            def reduce(q, s, i):
                pe.wait_ge(onehot_ready, TILES * (q + 1))
                pe.wait_ge(weights_ready, q + 1)
                for k in range(QUAD):
                    u = q * QUAD + k
                    pe.wait_ge(msg_ready, u + 1)
                    if again(u, SB):
                        pe.wait_ge(acc_ready, u - SB + 2)
                    for e in range(2):
                        last = nc.tensor.matmul(sum_ps[k % SB], onehot[:, s % 2, 2 * k + e, :],
                                                msg[:, s, 2 * k + e, :], start=(e == 0), stop=(e == 1))
                    last.then_inc(sums_made, 1)

            def transpose_q(t, s, i):
                pe.wait_ge(qz_ready, t + 1)
                if again(t, 2):
                    pe.wait_ge(qT_ready, t - 1)
                for k in range(KC):
                    last = nc.tensor.transpose(qT_ps[s][:, k * P:(k + 1) * P], qz[:, s, k * P:(k + 1) * P],
                                               c.ident[:])
                last.then_inc(qT_made, 1)

            def attend(t, s, i):
                pe.wait_ge(qT_ready, t + 1)
                if again(t, 2):
                    pe.wait_ge(h_ready, t - 1)
                for k in range(KC):
                    nc.tensor.matmul(att_ps[s], qT[:, s, k * P:(k + 1) * P], mix[:, k, :], start=(k == 0), stop=False)
                nc.tensor.matmul(att_ps[s], c.ones[0:1, :], b_row[:], start=False, stop=True).then_inc(att_made, 1)

            pipeline(pe, NQ, [(1, tile_of(transpose_q), NM), (2, tile_of(attend), NM), (0, reduce)], R)

        @block.scalar
        def _(act):
            def copy_weights(q, s, i):
                if again(q, R):
                    act.wait_ge(sums_made, QUAD * (q - R + 1))
                nc.scalar.copy(msg[:, s, :, D:HX], alpha[:, bass.ds(q * TILES * HEADS, TILES * HEADS)].rearrange(
                    "p (k h) -> p k h", k=TILES)).then_inc(weights_ready, 1)

            def copy_qT(t, s, i):
                act.wait_ge(qT_made, t + 1)
                if again(t, 2):
                    act.wait_ge(att_made, t - 1)
                nc.scalar.copy(qT[:, s, :], qT_ps[s]).then_inc(qT_ready, 1)

            def squares(t, s, i):
                act.wait_ge(h_ready, t + 1)
                if again(t, 2):
                    act.wait_ge(r2_ready, t - 1)
                    act.wait_ge(y_ready, t - 1)
                nc.scalar.activation(scaled[:, s, :], h[:, s, :], ACT.Square,
                                     accum_out=ss[:, s:s + 1]).then_inc(ss_ready, 1)

            pipeline(act, NQ, [(0, copy_weights), (1, tile_of(copy_qT), NM), (3, tile_of(squares), NM)], R)


EXPERTS = 8
HIDDEN = 1024
HIC = HIDDEN // P
TOPK = 2
MT = (TOPK * N + EXPERTS * (P - 1)) // P
BW = HIDDEN + D


def finish_nodes(nc, c, acc, ytab, x1tab, gate_w, gate_b, biases, normed, scores, bias_parts):
    with ExitStack() as ctx:
        sb = lambda name, shape, dt=F32: ctx.enter_context(nc.sbuf_tensor(name, shape, dt))
        sem = semaphores(nc, ctx)
        gw, gb = sb("gw", [P, KC, EXPERTS]), sb("gb", [P, EXPERTS])
        bias, bias_rest = sb("bias", [EXPERTS, BW]), sb("bias_rest", [EXPERTS, BW])
        bias16 = sb("bias16", [EXPERTS, 3, BW], BF16)
        y, part, x1 = sb("y7", [P, 2, D]), sb("part7", [P, 2, D]), sb("x17", [P, 2, D])
        den, rec = sb("den7", [P, 2, HEADS]), sb("rec7", [P, 2, HEADS])
        stats, mv, rstd = sb("stats7", [P, 2, 6]), sb("mv7", [P, 2, 2]), sb("rstd7", [P, 2])
        nT, fixed = sb("nT", [P, 2, D]), sb("normed_fixed", [P, 2, D])
        consts_in, bias_step, bias_out = sem("gate_in"), sem("bias_step"), sem("bias_out")
        y_in = [sem(f"y7_in{s}") for s in range(2)]
        x1_out = [sem(f"x1_out{s}") for s in range(2)]
        dve_step, x1_ready, mv_ready = sem("dve_step7"), sem("x1_ready"), sem("mv7_ready")
        eps_ready, rstd_ready, normed_ready = sem("eps_ready"), sem("rstd7_ready"), sem("normed_ready")
        turned, nT_ready, gate_made, gate_ready = sem("nT_made"), sem("nT_ready"), sem("gate_made"), sem("gate_ready")
        block = ctx.enter_context(nc.Block())
        nT_ps = [c.ps[b][:, 0:D] for b in (0, 1)]
        gate_ps = [c.ps[b][:, 0:EXPERTS] for b in (2, 3)]
        heads = lambda ap: ap.rearrange("p (h d) -> p h d", h=HEADS)
        at = lambda buf, t: buf[:, bass.ds(t, 1), :].rearrange("p o n -> p (o n)")

        @block.sync
        def _(sp):
            sp.dma_start(gw[:], gate_w.rearrange("(c p) n -> p c n", p=P)).then_inc(consts_in, 16)
            sp.dma_start(gb[:], gate_b.rearrange("(o d) -> o d", o=1).broadcast_to([P, EXPERTS])).then_inc(consts_in, 16)
            sp.dma_start(bias[:], biases).then_inc(consts_in, 16)

            def load(t, s, i):
                if again(t, 2):
                    sp.wait_ge(x1_ready, t - 1)
                sp.dma_start(y[:, s, :], ytab[bass.ds(t * P, P), :]).then_inc(y_in[s], 16)

            def store(t, s, i):
                sp.wait_ge(x1_ready, t + 1)
                sp.dma_start(x1tab[bass.ds(t * P, P), :], x1[:, s, :]).then_inc(x1_out[s], 16)

            pipeline(sp, NN, [(0, load), (1, store)])
            sp.wait_ge(bias_step, 5)
            sp.dma_start(bias_parts.rearrange("j e n -> e j n"), bias16[:]).then_inc(bias_out, 16)
            sp.wait_ge(bias_out, 16)
            for s in range(2):
                sp.wait_ge(x1_out[s], 16 * ((NN + 1 - s) // 2))

        @block.gpsimd
        def _(pool):
            pool.wait_ge(consts_in, 48)
            for n, (out, a, b) in enumerate(((bias16[:, 0, :], bias[:], None),
                                             (bias_rest[:], bias[:], bias16[:, 0, :]),
                                             (bias16[:, 1, :], bias_rest[:], None),
                                             (bias_rest[:], bias_rest[:], bias16[:, 1, :]),
                                             (bias16[:, 2, :], bias_rest[:], None))):
                ins = nc.gpsimd.tensor_copy(out, a) if b is None else nc.gpsimd.tensor_tensor(out, a, b, ALU.subtract)
                ins.then_inc(bias_step, 1)
                pool.wait_ge(bias_step, n + 1)

            def inverse(t, s, i):
                if again(t, 2):
                    pool.wait_ge(normed_ready, t - 1)
                wait_apart(pool, mv_ready, t + 1, c.passed)
                nc.gpsimd.tensor_scalar(rstd[:, s:s + 1], mv[:, s, 1:2], LN_EPS, None, ALU.add).then_inc(eps_ready, 1)
                pool.wait_ge(eps_ready, t + 1)
                nc.gpsimd.tensor_tensor(rstd[:, s:s + 1], rstd[:, s:s + 1], c.minus_half[:], ALU.pow
                                        ).then_inc(rstd_ready, 1)

            pipeline(pool, NN, [(0, inverse)])

        @block.vector
        def _(dve):
            V = nc.vector

            def add_graph(t, s, i):
                V.tensor_scalar(den[:, s, :], acc[:, bass.ds(t, 1), D:HX].rearrange("p o n -> p (o n)"), 1e-10, None,
                                ALU.max).then_inc(dve_step, 1)
                dve.wait_ge(dve_step, 4 * t + 1)
                V.reciprocal(rec[:, s, :], den[:, s, :]).then_inc(dve_step, 1)
                dve.wait_ge(dve_step, 4 * t + 2)
                V.tensor_tensor(heads(part[:, s, :]), heads(acc[:, bass.ds(t, 1), 0:D].rearrange("p o n -> p (o n)")),
                                rec[:, s, :].unsqueeze(2).broadcast_to([P, HEADS, HD]), ALU.mult).then_inc(dve_step, 1)
                dve.wait_ge(dve_step, 4 * t + 3)
                dve.wait_ge(y_in[s], 16 * (i + 1))
                if again(t, 2):
                    dve.wait_ge(x1_out[s], 16 * i)
                V.tensor_tensor(x1[:, s, :], y[:, s, :], part[:, s, :], ALU.add).then_inc(x1_ready, 1)
                dve.wait_ge(x1_ready, t + 1)
                V.bn_stats(stats[:, s, :], x1[:, s, :]).then_inc(dve_step, 1)
                wait_apart(dve, dve_step, 4 * t + 4, c.passed)
                V.bn_aggr(mv[:, s, :], stats[:, s, :]).then_inc(mv_ready, 1)

            def norm(t, s, i):
                dve.wait_ge(rstd_ready, t + 1)
                if again(t, 2):
                    dve.wait_ge(turned, t - 1)
                    dve.wait_ge(gate_ready, t - 1)
                V.tensor_scalar(fixed[:, s, :], x1[:, s, :], mv[:, s, 0:1], rstd[:, s:s + 1],
                                ALU.subtract, ALU.mult).then_inc(normed_ready, 1)

            def gate(t, s, i):
                dve.wait_ge(normed_ready, t + 1)
                V.tensor_copy(at(normed, t), fixed[:, s, :])
                dve.wait_ge(gate_made, t + 1)
                V.tensor_tensor(at(scores, t), gate_ps[s], gb[:], ALU.add).then_inc(gate_ready, 1)

            dve.wait_ge(consts_in, 48)
            pipeline(dve, NN, [(2, gate), (0, add_graph), (1, norm)])

        @block.tensor
        def _(pe):
            pe.wait_ge(consts_in, 48)

            def turn(t, s, i):
                pe.wait_ge(normed_ready, t + 1)
                if again(t, 2):
                    pe.wait_ge(nT_ready, t - 1)
                for k in range(KC):
                    last = nc.tensor.transpose(nT_ps[s][:, k * P:(k + 1) * P], fixed[:, s, k * P:(k + 1) * P],
                                               c.ident[:])
                last.then_inc(turned, 1)

            def gate(t, s, i):
                pe.wait_ge(nT_ready, t + 1)
                if again(t, 2):
                    pe.wait_ge(gate_ready, t - 1)
                for k in range(KC):
                    last = nc.tensor.matmul(gate_ps[s], nT[:, s, k * P:(k + 1) * P], gw[:, k, :],
                                            start=(k == 0), stop=(k == KC - 1))
                last.then_inc(gate_made, 1)

            pipeline(pe, NN, [(1, gate), (0, turn)])

        @block.scalar
        def _(act):
            def copy_nT(t, s, i):
                act.wait_ge(turned, t + 1)
                if again(t, 2):
                    act.wait_ge(gate_made, t - 1)
                nc.scalar.copy(nT[:, s, :], nT_ps[s]).then_inc(nT_ready, 1)

            pipeline(act, NN, [(0, copy_nT)])


def route(nc, c, scores, normed, xs, probs, slots, expert_row):
    with ExitStack() as ctx:
        sb = lambda name, shape, dt=F32: ctx.enter_context(nc.sbuf_tensor(name, shape, dt))
        sem = semaphores(nc, ctx)
        zeros = sb("zeros", [P, D])
        top, at = sb("top8", [P, NN, 8]), sb("at8", [P, NN, 8], mybir.dt.uint32)
        atf = sb("atf", [P, TOPK, NN])
        gap, one_plus = sb("gap", [P, NN]), sb("one_plus", [P, NN])
        expert_id = sb("expert_id", [P, EXPERTS])
        real = sb("real", [P, 1])
        chosen = sb("chosen", [P, TOPK, NN, EXPERTS])
        both = sb("both", [P, NN, EXPERTS])
        both16, before = sb("both16", [P, NN * EXPERTS], BF16), sb("before", [P, P], BF16)
        ones16 = sb("ones16", [P, P], BF16)
        place, total, running = (sb(n, [P, NN, EXPERTS]) for n in ("place", "total", "running"))
        nrows, ntiles, tend, tstart = (sb(n, [P, EXPERTS]) for n in ("nrows", "ntiles", "tend", "tstart"))
        ntiles_i = sb("ntiles_i", [P, EXPERTS], I32)
        zero = sb("zero8", [P, NN])
        tile_id, passed = sb("tile_id", [P, MT]), sb("passed", [P, MT, EXPERTS])
        expert_f = sb("expert_f", [P, MT])
        slot_f = sb("slot_f", [P, TOPK, NN])
        picked = sb("picked", [P, NN, EXPERTS])
        iota_ready, step_sem, zeroed, gap_ready, exp_ready = (
            sem("route_iota"), sem("route_step"), sem("xs_zeroed"), sem("gap_ready"), sem("exp8_ready"))
        both_ready, ranked, slots_ready = sem("both_ready"), sem("ranked"), sem("slots_ready")
        scattered, = gather_semaphores(c, 1)
        block = ctx.enter_context(nc.Block())

        @block.sync
        def _(sp):
            sp.wait_ge(iota_ready, 1)
            sp.dma_start(xs.rearrange("(p r) d -> p r d", p=P),
                         zeros[:].unsqueeze(1).broadcast_to([P, MT, D])).then_inc(zeroed, 16)

        @block.gpsimd
        def _(pool):
            nc.gpsimd.memset(zeros[:], 0.0).then_inc(iota_ready, 1)
            nc.gpsimd.iota(expert_id[:], [[1, EXPERTS]], base=0, channel_multiplier=0,
                           allow_small_or_imprecise_dtypes=True)
            nc.gpsimd.iota(real[:], [[0, 1]], base=0, channel_multiplier=1, allow_small_or_imprecise_dtypes=True)
            nc.gpsimd.iota(tile_id[:], [[1, MT]], base=0, channel_multiplier=0, allow_small_or_imprecise_dtypes=True)
            nc.gpsimd.memset(ones16[:], 1.0).then_inc(iota_ready, 1)
            pool.wait_ge(iota_ready, 2)
            nc.gpsimd.affine_select(out=before[:], in_=ones16[:], compare_op=ALU.is_gt, fill=0.0, base=0,
                                    pattern=[[1, P]], channel_multiplier=-1).then_inc(iota_ready, 1)
            pool.wait_ge(slots_ready, 1)
            pool.wait_ge(zeroed, 16)
            for t in range(NN):
                rows = P if t < LAST else LAST_ROWS
                for j in range(TOPK):
                    nc.gpsimd.indirect_dma_start(
                        xs, bass.IndirectOffsetOnAxis(ap=slots[0:rows, j, t:t + 1], axis=0),
                        normed[0:rows, t, :], None).then_inc(scattered, 16)
            pool.wait_ge(scattered, 16 * TOPK * NN)

        @block.scalar
        def _(act):
            act.wait_ge(gap_ready, 1)
            nc.scalar.activation(gap[:], gap[:], ACT.Exp).then_inc(exp_ready, 1)

        @block.tensor
        def _(pe):
            pe.wait_ge(both_ready, 1)
            pe.wait_ge(iota_ready, 3)
            nc.tensor.matmul(c.ps[0][:, 0:NN * EXPERTS], before[:], both16[:], start=True, stop=True)
            nc.tensor.matmul(c.ps[1][:, 0:NN * EXPERTS], ones16[:], both16[:], start=True, stop=True
                             ).then_inc(ranked, 1)

        @block.vector
        def _(dve):
            V, step = nc.vector, Steps()

            def done(ins):
                ins.then_inc(step_sem, 1)
                dve.wait_ge(step_sem, step.last())

            done(V.memset(zero[:], 0.0))
            for t in range(NN):
                last = V.max(top[:, t, :], scores[:, t, :])
            done(last)
            for t in range(NN):
                last = V.max_index(at[:, t, :], top[:, t, :], scores[:, t, :])
            done(last)
            V.tensor_tensor(gap[:], top[:, :, 1], top[:, :, 0], ALU.subtract).then_inc(gap_ready, 1)
            dve.wait_ge(exp_ready, 1)
            done(V.tensor_scalar(one_plus[:], gap[:], 1.0, None, ALU.add))
            done(V.reciprocal(probs[:, 0, :], one_plus[:]))
            V.tensor_tensor(probs[:, 1, :], probs[:, 0, :], gap[:], ALU.mult)
            dve.wait_ge(iota_ready, 3)
            done(V.tensor_copy(atf[:], at[:, :, 0:TOPK].rearrange("p t j -> p j t")))
            ids = expert_id[:].unsqueeze(1).broadcast_to([P, NN, EXPERTS])
            for j in range(TOPK):
                done(V.tensor_tensor(chosen[:, j, :, :], ids, atf[:, j, :].unsqueeze(2).broadcast_to([P, NN, EXPERTS]),
                                     ALU.is_equal))
            done(V.tensor_tensor(both[:], chosen[:, 0, :, :], chosen[:, 1, :, :], ALU.add))
            done(V.tensor_scalar(real[:], real[:], float(LAST_ROWS), None, ALU.is_lt))
            done(V.tensor_scalar(both[:, LAST, :], both[:, LAST, :], real[:], None, ALU.mult))
            V.tensor_copy(both16[:], both[:].rearrange("p t e -> p (t e)")).then_inc(both_ready, 1)
            dve.wait_ge(ranked, 1)
            flat = lambda ap: ap.rearrange("p t e -> p (t e)")
            done(V.tensor_copy(flat(place[:]), c.ps[0][:, 0:NN * EXPERTS]))
            done(V.tensor_copy(flat(total[:]), c.ps[1][:, 0:NN * EXPERTS]))
            for e in range(EXPERTS):
                last = V.tensor_tensor_scan(running[:, :, e], total[:, :, e], zero[:], 0.0, ALU.add, ALU.add)
            done(last)
            done(V.tensor_tensor(place[:], place[:], running[:], ALU.add))
            done(V.tensor_tensor(place[:], place[:], total[:], ALU.subtract))
            done(V.tensor_scalar(nrows[:], running[:, NN - 1, :], P - 1.0, None, ALU.add))
            done(V.tensor_copy(ntiles_i[:], nrows[:]))
            done(V.tensor_single_scalar(ntiles_i[:], ntiles_i[:], 7, ALU.arith_shift_right))
            done(V.tensor_copy(ntiles[:], ntiles_i[:]))
            done(V.tensor_tensor_scan(tend[:], ntiles[:], zero[:, 0:EXPERTS], 0.0, ALU.add, ALU.add))
            done(V.tensor_tensor(tstart[:], tend[:], ntiles[:], ALU.subtract))
            done(V.tensor_scalar(nrows[:], tstart[:], float(P), None, ALU.mult))
            done(V.tensor_tensor(place[:], place[:], nrows[:].unsqueeze(1).broadcast_to([P, NN, EXPERTS]), ALU.add))
            for j in range(TOPK):
                done(V.tensor_tensor(picked[:], place[:], chosen[:, j, :, :], ALU.mult))
                done(V.tensor_reduce(slot_f[:, j, :], picked[:], AX.X, ALU.add))
            V.tensor_copy(slots[:], slot_f[:]).then_inc(slots_ready, 1)
            done(V.tensor_tensor(passed[:], tstart[:].unsqueeze(1).broadcast_to([P, MT, EXPERTS]),
                                 tile_id[:].unsqueeze(2).broadcast_to([P, MT, EXPERTS]), ALU.is_le))
            done(V.tensor_reduce(expert_f[:], passed[:], AX.X, ALU.add))
            done(V.tensor_scalar(expert_f[:], expert_f[:], -1.0, None, ALU.add))
            V.tensor_copy(expert_row[:], expert_f[0:1, :])


def run_experts(nc, c, xs, ys, w1t, w2t, bias_parts, expert_row):
    with ExitStack() as ctx:
        sb = lambda name, shape, dt=F32: ctx.enter_context(nc.sbuf_tensor(name, shape, dt))
        sem = semaphores(nc, ctx)
        w1, w2 = sb("w1", [P, EXPERTS, KC, HIDDEN]), sb("w2", [P, EXPERTS, HIC, D])
        bias = sb("bias_rows", [3, EXPERTS, BW], BF16)
        ones16 = sb("ones3", [3, P], BF16)
        R = 4
        x, xT = sb("x9", [P, R, D]), sb("x9T", [P, 2, D])
        h, hT = sb("h9", [P, HIDDEN]), sb("h9T", [P, HIDDEN])
        y = sb("y9", [P, R, D])
        weights_in, ones_ready = sem("experts_in"), sem("ones3_ready")
        x_in = [sem(f"x9_in{s}") for s in range(R)]
        y_out = [sem(f"y9_out{s}") for s in range(R)]
        xT_made, xT_ready, h_made, h_ready = sem("x9T_made"), sem("x9T_ready"), sem("h9_made"), sem("h9_ready")
        hT_made, hT_ready, y_made, y_ready = sem("h9T_made"), sem("h9T_ready"), sem("y9_made"), sem("y9_ready")
        block = ctx.enter_context(nc.Block())
        xT_ps = [c.ps[0][:, 0:D], c.ps[7][:, 0:D]]
        h_ps, hT_ps = [c.ps[1], c.ps[2]], [c.ps[3], c.ps[4]]
        y_ps = [c.ps[5][:, 0:D], c.ps[6][:, 0:D]]

        @block.sync
        def _(sp):
            for e in range(EXPERTS):
                sp.dma_start(w1[:, e], w1t[e].rearrange("(c p) n -> p c n", p=P)).then_inc(weights_in, 16)
                sp.dma_start(w2[:, e], w2t[e].rearrange("(c p) n -> p c n", p=P)).then_inc(weights_in, 16)
            sp.dma_start(bias[:], bias_parts).then_inc(weights_in, 16)

            def load(t, s, i):
                if again(t, R):
                    sp.wait_ge(xT_made, t - R + 1)
                sp.dma_start(x[:, s, :], xs[bass.ds(t * P, P), :]).then_inc(x_in[s], 16)

            def store(t, s, i):
                sp.wait_ge(y_ready, t + 1)
                sp.dma_start(ys[bass.ds(t * P, P), :], y[:, s, :]).then_inc(y_out[s], 16)

            pipeline(sp, MT, [(0, load), (R - 1, store)], R)
            for s in range(R):
                sp.wait_ge(y_out[s], 16 * len(range(s, MT, R)))

        @block.tensor
        def _(pe):
            pe.wait_ge(weights_in, 16 * (2 * EXPERTS + 1))
            pe.wait_ge(ones_ready, 1)

            def turn_x(t, s, i):
                pe.wait_ge(x_in[s], 16 * (i + 1))
                if again(t, 2):
                    pe.wait_ge(xT_ready, t - 1)
                for k in range(KC):
                    last = nc.tensor.transpose(xT_ps[s % 2][:, k * P:(k + 1) * P], x[:, s, k * P:(k + 1) * P], c.ident[:])
                last.then_inc(xT_made, 1)

            def expert(t):
                return pe.value_load(expert_row[0:1, bass.ds(t, 1)], min_val=0, max_val=EXPERTS - 1)

            def hidden(t, s, i):
                e = expert(t)
                pe.wait_ge(xT_ready, t + 1)
                for n in range(2):
                    lo = n * 512
                    if again(t, 1):
                        pe.wait_ge(h_ready, 2 * t - 1 + n)
                    for k in range(KC):
                        nc.tensor.matmul(h_ps[n][:], xT[:, s % 2, k * P:(k + 1) * P],
                                         w1[:, bass.ds(e, 1), k, lo:lo + 512].rearrange("p o n -> p (o n)"),
                                         start=(k == 0), stop=False)
                    nc.tensor.matmul(h_ps[n][:], ones16[:],
                                     bias[:, bass.ds(e, 1), lo:lo + 512].rearrange("p o n -> p (o n)"),
                                     start=False, stop=True).then_inc(h_made, 1)

            def turn_h(t, s, i):
                for n in range(2):
                    pe.wait_ge(h_ready, 2 * t + n + 1)
                    if again(t, 1):
                        pe.wait_ge(hT_ready, 2 * t - 1 + n)
                    for k in range(4):
                        lo = (4 * n + k) * P
                        last = nc.tensor.transpose(hT_ps[n][:, k * P:(k + 1) * P], h[:, lo:lo + P], c.ident[:])
                    last.then_inc(hT_made, 1)

            def output(t, s, i):
                e = expert(t)
                if again(t, 2):
                    pe.wait_ge(y_ready, t - 1)
                for k in range(HIC):
                    if k % 4 == 0:
                        pe.wait_ge(hT_ready, 2 * t + k // 4 + 1)
                    nc.tensor.matmul(y_ps[s % 2], hT[:, k * P:(k + 1) * P],
                                     w2[:, bass.ds(e, 1), k, :].rearrange("p o n -> p (o n)"),
                                     start=(k == 0), stop=False)
                nc.tensor.matmul(y_ps[s % 2], ones16[:], bias[:, bass.ds(e, 1), HIDDEN:BW].rearrange("p o n -> p (o n)"),
                                 start=False, stop=True).then_inc(y_made, 1)

            pipeline(pe, MT, [(0, turn_x), (2, turn_h), (1, hidden), (2, output)], R)

        @block.scalar
        def _(act):
            def copy_xT(t, s, i):
                act.wait_ge(xT_made, t + 1)
                if again(t, 2):
                    act.wait_ge(h_made, 2 * (t - 1))
                nc.scalar.copy(xT[:, s % 2, :], xT_ps[s % 2]).then_inc(xT_ready, 1)

            def relu(t, s, i):
                for n in range(2):
                    act.wait_ge(h_made, 2 * t + n + 1)
                    if again(t, 1):
                        act.wait_ge(hT_made, 2 * t - 1 + n)
                    nc.scalar.activation(h[:, n * 512:(n + 1) * 512], h_ps[n][:], ACT.Relu).then_inc(h_ready, 1)

            pipeline(act, MT, [(0, copy_xT), (1, relu)], R)

        @block.vector
        def _(dve):
            nc.vector.memset(ones16[:], 1.0).then_inc(ones_ready, 1)

            def copy_hT(t, s, i):
                for n in range(2):
                    dve.wait_ge(hT_made, 2 * t + n + 1)
                    if again(t, 1):
                        dve.wait_ge(y_made, t)
                    nc.vector.tensor_copy(hT[:, n * 512:(n + 1) * 512], hT_ps[n][:]).then_inc(hT_ready, 1)

            def copy_y(t, s, i):
                dve.wait_ge(y_made, t + 1)
                if again(t, R):
                    dve.wait_ge(y_out[s], 16 * i)
                nc.vector.tensor_copy(y[:, s, :], y_ps[s % 2]).then_inc(y_ready, 1)

            pipeline(dve, MT, [(0, copy_hT), (0, copy_y)], R)


def combine(nc, c, x1tab, ys, probs, slots, out):
    with ExitStack() as ctx:
        sb = lambda name, shape, dt=F32: ctx.enter_context(nc.sbuf_tensor(name, shape, dt))
        sem = semaphores(nc, ctx)
        R = 3
        x1, y = sb("x1_last", [P, R, D]), sb("y_last", [P, R, TOPK, D])
        x1_in = [sem(f"x1_in{s}") for s in range(R)]
        y_in = gather_semaphores(c, R)
        out_done = [sem(f"out_done{s}") for s in range(R)]
        first, summed = sem("first_added"), sem("both_added")
        block = ctx.enter_context(nc.Block())
        rows = lambda t: P if t < LAST else LAST_ROWS

        @block.sync
        def _(sp):
            for t in range(NN + 1):
                if t < NN:
                    if t >= R:
                        sp.wait_ge(out_done[t % R], 16 * (t // R))
                    sp.dma_start(x1[0:rows(t), t % R, :], x1tab[t * P:t * P + rows(t), :]).then_inc(x1_in[t % R], 16)
                if t >= 1:
                    o = t - 1
                    sp.wait_ge(x1_in[o % R], 16 * (o // R + 1))
                    sp.wait_ge(summed, o + 1)
                    sp.dma_start(out[o * P:o * P + rows(o), :], x1[0:rows(o), o % R, :]).then_inc(out_done[o % R], 16)
            for s in range(R):
                sp.wait_ge(out_done[s], 16 * len(range(s, NN, R)))

        @block.gpsimd
        def _(pool):
            for t in range(NN):
                if t >= R:
                    pool.wait_ge(summed, t - R + 1)
                    pool.wait_ge(y_in[t % R], 32 * (t // R))
                for j in range(TOPK):
                    nc.gpsimd.indirect_dma_start(
                        y[0:rows(t), t % R, j, :], None, ys,
                        bass.IndirectOffsetOnAxis(ap=slots[0:rows(t), j, t:t + 1], axis=0)).then_inc(y_in[t % R], 16)

        @block.vector
        def _(dve):
            for t in range(NN):
                s, r = t % R, rows(t)
                dve.wait_ge(x1_in[s], 16 * (t // R + 1))
                dve.wait_ge(y_in[s], 32 * (t // R + 1))
                for j, sem_ in enumerate((first, summed)):
                    if j == 1:
                        dve.wait_ge(first, t + 1)
                    nc.vector.scalar_tensor_tensor(out=x1[0:r, s, :], in0=y[0:r, s, j, :],
                                                   scalar=probs[0:r, j, t:t + 1], in1=x1[0:r, s, :],
                                                   op0=ALU.mult, op1=ALU.add).then_inc(sem_, 1)


class Shared:
    pass


def build(nc, io):
    with ExitStack() as ctx:
        sb = lambda name, shape, dt=F32: ctx.enter_context(nc.sbuf_tensor(name, shape, dt))
        dram = lambda name, shape, dt=F32: nc.dram_tensor(name, shape, dt, kind="Internal").ap()
        c = Shared()
        c.ps = [ctx.enter_context(nc.psum_tensor(f"bank{b}", [P, 512], F32)) for b in range(8)]
        c.ident, c.ident16 = sb("ident", [P, P]), sb("ident16", [P, P], BF16)
        c.ones = sb("ones", [P, P])
        c.minus_half = sb("minus_half", [P, 1])
        c.gathered = [ctx.enter_context(nc.semaphore(f"gathered{s}")) for s in range(16)]
        c.passed = ctx.enter_context(nc.semaphore("passed"))
        c.lane16 = sb("lane16", [P, P], BF16)
        htab, stab = dram("htab", [NP, D]), dram("stab", [NP, HEADS])
        qtab, xntab = dram("qtab", [NP, D]), dram("xntab", [NP, D])
        ytab = dram("ytab", [NP, D])
        build_constants(nc, c)
        block_row = sb("block_row", [1, SG * P], I32)
        probs, slots = sb("probs", [P, TOPK, NN]), sb("slots", [P, TOPK, NN], I32)
        expert_row = sb("expert_row", [1, MT], I32)
        edge_ctx = ctx.enter_context(ExitStack())
        sb = lambda name, shape, dt=F32: edge_ctx.enter_context(nc.sbuf_tensor(name, shape, dt))
        dl, src, keys = sb("dl", [P, NS, 2]), sb("src", [P, NS, 2], I32), sb("keys", [P, NS, 2])
        blocks = dram("blocks", [1, SG * P], I32)
        attr_parts = dram("attr_parts", [12, SG * P, 2 * P], BF16)
        wparts = sb("wparts", [36, D], BF16)
        plan_steps(nc, c, io["dst"], io["src"], io["attr"], io["edge_w"], wparts, dl, src, keys, blocks, block_row,
                   attr_parts)
        big = sb("big", [P, NT * 3 * HX], BF16)
        hparts = big[:].rearrange("p (t j n) -> p t j n", t=NT, j=3)
        big32 = big[:].bitcast(F32)
        with ExitStack() as node_ctx:
            nb = lambda name, shape: node_ctx.enter_context(nc.sbuf_tensor(name, shape, F32))
            wall, x_all = nb("wall", [P, KC, WALL]), nb("x_all", [P, NT, D])
            mean, rstd, r1 = nb("mean", [P, NT]), nb("rstd", [P, NT]), nb("r1", [P, NT])
            fold_weights(nc, c, io["W"], io["WT"], io["a_src"], io["a_dst"], io["w_norm1"], io["w_qkv"], wall)
            row_norms(nc, c, io["x"], x_all, mean, rstd, r1)
            project_nodes(nc, c, x_all, mean, rstd, r1, wall, hparts, htab, stab, qtab, xntab)
        mix, ksum = sb("mix", [P, KC, D]), sb("ksum", [P, D])
        mix_weights(nc, c, io["w_out"], mix, ksum)
        alpha = sb("alpha", [P, 2 * NS * HEADS])
        score_edges(nc, c, wparts, hparts, stab, attr_parts, dl, src, block_row, alpha)
        softmax_numerators(nc, c, keys, alpha, big32[:, 0:RL], big32[:, RL:2 * RL], dram("cross", [4, 2, P]))
        x1tab = dram("x1tab", [NP, D])
        xs, ys = dram("xs", [MT * P, D]), dram("ys", [MT * P, D])
        bias_parts = dram("bias_parts", [3, EXPERTS, BW], BF16)
        acc = big32[:, 0:NT * HX].rearrange("p (t n) -> p t n", t=NT)
        sum_messages_and_mix(nc, c, htab, dl, src, block_row, alpha, acc, mix, ksum, io["x"], io["gnn_bias"],
                             io["b_out"], io["w_norm2"], qtab, xntab, ytab)
        with nc.sbuf_tensor("normed", [P, NN, D], F32) as normed, nc.sbuf_tensor("scores", [P, NN, EXPERTS], F32) as scores:
            finish_nodes(nc, c, acc, ytab, x1tab, io["gate_w"], io["gate_b"], io["biases"], normed, scores,
                         bias_parts)
            route(nc, c, scores, normed, xs, probs, slots, expert_row)
        edge_ctx.close()
        run_experts(nc, c, xs, ys, io["w1t"], io["w2t"], bias_parts, expert_row)
        combine(nc, c, x1tab, ys, probs, slots, io["out"])
        if "dbg" in io:
            io["dbg"](nc, c, locals())


def layout(inp):
    f = lambda name: np.asarray(inp[name])
    x = np.zeros((NP, D), np.float32)
    x[:N] = f("x")

    def edges(name, fill):
        a = np.full(ET * P, fill, np.int32)
        a[:E] = f(name)
        return a.reshape(ET, P)

    attr = np.zeros((ET * P, 4), np.float32)
    attr[:E, :3], attr[:E, 3] = f("edge_attr_3"), 1.0
    attr = attr.reshape(ET, P, 4).transpose(0, 2, 1)
    return {
        "x": x,
        "W": f("L0_gnn_W"), "WT": f("L0_gnn_W").T,
        "a_src": f("L0_gnn_a_src"), "a_dst": f("L0_gnn_a_dst"),
        "w_norm1": f("L0_mix_w_norm1"), "w_qkv": f("L0_mix_w_qkv"),
        "gnn_bias": f("L0_gnn_bias"), "w_out": f("L0_mix_w_out"), "b_out": f("L0_mix_b_out"),
        "w_norm2": f("L0_mix_w_norm2"),
        "gate_w": f("L0_ffn_Wg").T, "gate_b": f("L0_ffn_bg"),
        "biases": np.concatenate([f("L0_ffn_b1"), f("L0_ffn_b2")], axis=1),
        "w1t": f("L0_ffn_W1").transpose(0, 2, 1), "w2t": f("L0_ffn_W2").transpose(0, 2, 1),
        "dst": edges("dst", 2 * NP), "src": edges("src", 0), "attr": attr.reshape(ET, 4 * P),
        "edge_w": np.concatenate([f("L0_gnn_edge_W").T, f("L0_gnn_edge_b")[None]]),
    }


def kernel(**inputs):
    import concourse.bacc as bacc
    from concourse.bass_utils import run_bass_kernel_spmd

    arrays = {f"in_{n}": np.ascontiguousarray(a) for n, a in layout(inputs).items()}
    nc = bacc.Bacc("TRN2", target_bir_lowering=False, num_devices=1)
    io = {n[3:]: nc.dram_tensor(n, a.shape, mybir.dt.from_np(a.dtype), kind="ExternalInput").ap()
          for n, a in arrays.items()}
    io["out"] = nc.dram_tensor("out", [N, D], F32, kind="ExternalOutput").ap()
    build(nc, io)
    r = run_bass_kernel_spmd(nc, [arrays], core_ids=[0])
    return r.results[0]["out"]
```

```python
from contextlib import ExitStack

import numpy as np

import concourse.bass as bass
from concourse import mybir

ALU = mybir.AluOpType
ACT = mybir.ActivationFunctionType
AX = mybir.AxisListType
F32 = mybir.dt.float32
BF16 = mybir.dt.bfloat16
I32 = mybir.dt.int32

P = 128
D = 256
KC = D // P
HEADS = 8
HD = D // HEADS
N = 6250
NT = 50
NP = NT * P
LAST = N // P
LAST_ROWS = N - LAST * P
HC = D + 2 * HEADS
HW = HD + 1
HX = HEADS * HW
QC = 3 * D
COL_V, COL_QK, WALL = HC, HC + D, HC + D + 2 * D
E = 100000
ET = 784
NS = 440
SG = 4
QUAD = 4
TILES = 2 * QUAD
NQ = NS // QUAD
EARLY = 20
assert NS % QUAD == 0 and NQ % 2 == 0 and EARLY % 2 == 0
assert (ET - 2) * P >= E
assert 2 * NS >= (-(-E // P) + (NT - 2) + (NT - 1)) and NS <= SG * P
LN_EPS = 1e-5
RMS_EPS = 1e-6
ATT_EPS = 1e-6


class Steps:

    def __init__(self, base=0):
        self.base, self.n = base, 0

    def last(self):
        self.n += 1
        return self.base + self.n


def clear_after(nc, ctx, used):

    def clear():
        with nc.Block() as block:

            @block.gpsimd
            def _(pool):
                for s in used:
                    pool.sem_clear(s)

    ctx.callback(clear)


def semaphores(nc, ctx):
    made = []

    def sem(name):
        made.append(ctx.enter_context(nc.semaphore(name)))
        return made[-1]

    clear_after(nc, ctx, made)
    return sem


def gather_semaphores(c, n):
    return [c.gathered.pop() for _ in range(n)]


def build_constants(nc, c):
    with ExitStack() as ctx:
        pool_step = semaphores(nc, ctx)("pool_step")
        block = ctx.enter_context(nc.Block())

        @block.gpsimd
        def _(pool):
            step = Steps()
            nc.gpsimd.memset(c.ident[:], 0.0).then_inc(pool_step, 1)
            pool.wait_ge(pool_step, step.last())
            nc.gpsimd.affine_select(out=c.ident[:], in_=c.ident[:], compare_op=ALU.not_equal, fill=1.0,
                                    base=0, pattern=[[-1, P]], channel_multiplier=1).then_inc(pool_step, 1)
            pool.wait_ge(pool_step, step.last())
            nc.gpsimd.memset(c.ones[:], 1.0)
            nc.gpsimd.memset(c.zeros[:], 0.0)
            nc.gpsimd.memset(c.minus_half[:], -0.5)
            nc.gpsimd.iota(c.lane[:], [[0, 1]], base=0, channel_multiplier=1, allow_small_or_imprecise_dtypes=True)
            nc.gpsimd.iota(c.lane16[:], [[1, P]], base=0, channel_multiplier=0,
                           allow_small_or_imprecise_dtypes=True)


def fold_weights(nc, c, W, WT, a_src, a_dst, w_norm1, w_qkv, wall, x, x_all, stats):
    with ExitStack() as ctx:
        sb = lambda name, shape, dt=F32: ctx.enter_context(nc.sbuf_tensor(name, shape, dt))
        sem = semaphores(nc, ctx)
        w_rows = sb("w_rows", [P, KC, D])
        att = sb("att", [P, KC, 2 * HEADS])
        norm1 = sb("norm1", [P, KC])
        CH = 5
        CT = NT // CH
        x_in = [sem(f"x_in{n}") for n in range(CH)]
        weights_in, att_zero, att_in, folded, scaled = (
            sem("weights_in"), sem("att_zero"), sem("att_in"), sem("folded"), sem("scaled"))
        block = ctx.enter_context(nc.Block())

        @block.sync
        def _(sp):
            sp.dma_start(w_rows[:], W.rearrange("(c p) k -> p c k", p=P)).then_inc(weights_in, 16)
            for k in range(KC):
                sp.dma_start(wall[:, k, 0:HX].rearrange("p (h d) -> p h d", h=HEADS)[:, :, 0:HD],
                             WT[k * P:(k + 1) * P, :].rearrange("p (h d) -> p h d", h=HEADS)).then_inc(weights_in, 16)
            for n in range(CH):
                sp.dma_start(x_all[:, n * CT:(n + 1) * CT, :],
                             x[n * CT * P:(n + 1) * CT * P, :].rearrange("(t p) d -> p t d", p=P)).then_inc(x_in[n], 16)
            qkv = w_qkv.rearrange("(c p) n -> p c n", p=P)
            sp.dma_start(wall[:, :, COL_QK:COL_QK + 2 * D], qkv[:, :, 0:2 * D]).then_inc(weights_in, 16)
            sp.dma_start(wall[:, :, COL_V:COL_V + D], qkv[:, :, 2 * D:3 * D]).then_inc(weights_in, 16)
            sp.dma_start(norm1[:], w_norm1.rearrange("(c p) -> p c", p=P),
                         allow_slow_non_contiguous=True).then_inc(weights_in, 16)
            sp.wait_ge(att_zero, 1)
            for h in range(HEADS):
                rows = slice(HD * h % P, HD * h % P + HD)
                for j, a in enumerate((a_dst, a_src)):
                    sp.dma_start(att[rows, HD * h // P, j * HEADS + h:j * HEADS + h + 1],
                                 a[h, :].rearrange("(d o) -> d o", o=1),
                                 allow_slow_non_contiguous=True).then_inc(att_in, 16)

        @block.vector
        def _(dve):
            nc.vector.memset(att[:], 0.0).then_inc(att_zero, 1)
            for n in range(CH):
                dve.wait_ge(x_in[n], 16)
                for t in range(n * CT, (n + 1) * CT):
                    nc.vector.bn_stats(stats[:, t, :], x_all[:, t, :])
            dve.wait_ge(weights_in, 6 * 16)
            for k in range(KC):
                nc.vector.tensor_scalar(wall[:, k, COL_V:WALL], wall[:, k, COL_V:WALL], norm1[:, k:k + 1], None,
                                        ALU.mult).then_inc(scaled, 1)
            dve.wait_ge(folded, 1)
            att_ps = c.ps[0][:, 0:KC * 2 * HEADS].rearrange("p (k n) -> p k n", k=KC)
            nc.vector.tensor_copy(wall[:, :, 0:HX].rearrange("p k (h d) -> p k h d", h=HEADS)[:, :, :, HD],
                                  att_ps[:, :, 0:HEADS])
            nc.vector.tensor_copy(wall[:, :, HX:HC], att_ps[:, :, HEADS:2 * HEADS])

        @block.tensor
        def _(pe):
            pe.wait_ge(weights_in, 6 * 16)
            pe.wait_ge(att_in, 16 * 2 * HEADS)
            for k in range(KC):
                for m in range(KC):
                    last = nc.tensor.matmul(c.ps[0][:, k * 2 * HEADS:(k + 1) * 2 * HEADS],
                                            w_rows[:, m, k * P:(k + 1) * P], att[:, m, :],
                                            start=(m == 0), stop=(m == KC - 1))
            last.then_inc(folded, 1)


def wait_apart(eng, sem, value, passed):
    eng.wait_ge(sem, value)
    if not isinstance(value, int):
        eng.sem_inc(passed, 1)


def again(t, k):
    return not isinstance(t, int) or t >= k


def pipeline(eng, n, stages, unroll=2, straight=0):
    stages = [(*stage, n)[:3] for stage in stages]
    far, near = (pick(lag for lag, _, _ in stages) for pick in (max, min))

    def turn(T, r, j):
        for lag, fn, tiles in stages:
            t = T - lag if isinstance(T, int) else T + (r - lag)
            if not isinstance(T, int) or 0 <= t < tiles:
                fn(t, (r - lag) % unroll, j + (r - lag) // unroll)

    first = -(-max(far + 4, straight) // unroll) * unroll
    end = min(tiles + min(lag, 0) for lag, _, tiles in stages) // unroll * unroll
    for T in range(min(near, 0), first):
        turn(T, T % unroll, T // unroll)
    with eng.Fori(first // unroll, end // unroll) as j:
        for r in range(unroll):
            turn(j * unroll, r, j)
    for T in range(end, max(lag + tiles for lag, _, tiles in stages)):
        turn(T, T % unroll, T // unroll)


def moments(V, done, stats, mean, half, var):
    m0, m1, v0, v1 = (stats[:, :, j] for j in (1, 4, 2, 5))
    V.tensor_tensor(mean[:], m0, m1, ALU.add)
    V.tensor_tensor(half[:], m0, m1, ALU.subtract)
    done(V.tensor_tensor(var[:], v0, v1, ALU.add))
    V.tensor_scalar(mean[:], mean[:], 0.5, None, ALU.mult)
    done(V.tensor_scalar(half[:], half[:], 0.5, None, ALU.mult))
    done(V.tensor_tensor(half[:], half[:], half[:], ALU.mult))
    done(V.scalar_tensor_tensor(out=var[:], in0=var[:], scalar=1.0 / D, in1=half[:], op0=ALU.mult, op1=ALU.add))


def row_norms(nc, c, stats, mean, rstd, ms):
    with ExitStack() as ctx:
        sb = lambda name, shape, dt=F32: ctx.enter_context(nc.sbuf_tensor(name, shape, dt))
        sem = semaphores(nc, ctx)
        half, var = sb("half_gap", [P, NT]), sb("var", [P, NT])
        step_sem, var_ready, rstd_ready = sem("norm_step"), sem("var_ready"), sem("rstd_ready")
        block = ctx.enter_context(nc.Block())

        @block.vector
        def _(dve):
            V, step = nc.vector, Steps()

            def done(ins):
                ins.then_inc(step_sem, 1)
                dve.wait_ge(step_sem, step.last())

            moments(V, done, stats, mean, half, var)
            V.tensor_scalar(half[:], var[:], LN_EPS, None, ALU.add).then_inc(var_ready, 1)
            dve.wait_ge(rstd_ready, 1)
            done(V.tensor_tensor(ms[:], rstd[:], rstd[:], ALU.mult))
            done(V.tensor_tensor(ms[:], ms[:], var[:], ALU.mult))
            V.tensor_scalar(ms[:], ms[:], RMS_EPS, None, ALU.add)

        @block.gpsimd
        def _(pool):
            pool.wait_ge(var_ready, 1)
            nc.gpsimd.tensor_tensor(rstd[:], half[:], c.minus_half[:].broadcast_to([P, NT]), ALU.pow
                                    ).then_inc(rstd_ready, 1)


def project_graph(nc, c, x_all, mean, rstd, wall, hparts, htab, stab, xTtab, xntab):
    with ExitStack() as ctx:
        sb = lambda name, shape, dt=F32: ctx.enter_context(nc.sbuf_tensor(name, shape, dt))
        sem = semaphores(nc, ctx)
        R = 4
        xn, xT = sb("xn", [P, R, D]), sb("xT", [P, R, D])
        hrow, rest = sb("hrow", [P, R, HC]), sb("rest", [P, 2, HX])
        xn_ready, xT_made, xT_ready, proj_made = sem("xn_ready"), sem("xT_made"), sem("xT_ready"), sem("proj_made")
        hrow_ready, part1_ready = sem("hrow_ready"), sem("part1_ready")
        rest_ready, part2_ready, parts_made = sem("rest_ready"), sem("part2_ready"), sem("parts_made")
        xn_out = [sem(f"xn_out{s}") for s in range(R)]
        xT_out = [sem(f"xT_out{s}") for s in range(R)]
        h_out = [sem(f"h_out{s}") for s in range(R)]
        block = ctx.enter_context(nc.Block())
        xT_ps = [c.ps[b][:, 0:D] for b in (0, 1)]
        h_ps = [c.ps[b][:, 0:HC] for b in (2, 3)]
        at = lambda buf, t: buf[:, bass.ds(t, 1)]
        part = lambda t, j: hparts[:, bass.ds(t, 1), j, :].rearrange("p o n -> p (o n)")

        @block.sync
        def _(sp):
            def store_xn(t, s, i):
                sp.wait_ge(xn_ready, t + 1)
                sp.dma_start(xntab[bass.ds(t * P, P), :], xn[:, s, :]).then_inc(xn_out[s], 16)

            def store_xT(t, s, i):
                sp.wait_ge(xT_ready, t + 1)
                sp.dma_start(xTtab[bass.ds(t * P, P), :], xT[:, s, :]).then_inc(xT_out[s], 16)

            def store_h(t, s, i):
                rows = bass.ds(t * P, P)
                sp.wait_ge(hrow_ready, t + 1)
                sp.dma_start(htab[rows, :].rearrange("p (h d) -> p h d", h=HEADS),
                             hrow[:, s, 0:HX].rearrange("p (h d) -> p h d", h=HEADS)[:, :, 0:HD]).then_inc(h_out[s], 16)
                sp.dma_start(stab[rows, :], hrow[:, s, HX:HC]).then_inc(h_out[s], 16)

            pipeline(sp, NT, [(0, store_xn), (1, store_xT), (2, store_h)], R)
            for s in range(R):
                uses = len(range(s, NT, R))
                sp.wait_ge(xn_out[s], 16 * uses)
                sp.wait_ge(xT_out[s], 16 * uses)
                sp.wait_ge(h_out[s], 32 * uses)

        @block.vector
        def _(dve):
            def normalise(t, s, i):
                if again(t, R):
                    dve.wait_ge(xT_made, t - R + 1)
                    dve.wait_ge(xn_out[s], 16 * i)
                nc.vector.tensor_scalar(xn[:, s, :], at(x_all, t).rearrange("p o n -> p (o n)"),
                                        at(mean, t), at(rstd, t), ALU.subtract, ALU.mult).then_inc(xn_ready, 1)

            def first_part(t, s, i):
                dve.wait_ge(hrow_ready, t + 1)
                nc.vector.tensor_copy(part(t, 0), hrow[:, s, 0:HX]).then_inc(part1_ready, 1)

            def second_part(t, s, i):
                dve.wait_ge(rest_ready, t + 1)
                nc.vector.tensor_copy(part(t, 1), rest[:, s % 2, :]).then_inc(part2_ready, 1)

            pipeline(dve, NT, [(0, normalise), (4, second_part), (3, first_part)], R)

        @block.tensor
        def _(pe):
            def transpose_x(t, s, i):
                pe.wait_ge(xn_ready, t + 1)
                if again(t, 2):
                    pe.wait_ge(xT_ready, t - 1)
                for k in range(KC):
                    last = nc.tensor.transpose(xT_ps[s % 2][:, k * P:(k + 1) * P], xn[:, s, k * P:(k + 1) * P],
                                               c.ident[:])
                last.then_inc(xT_made, 1)

            def project(t, s, i):
                pe.wait_ge(xT_ready, t + 1)
                if again(t, 2):
                    pe.wait_ge(hrow_ready, t - 1)
                for k in range(KC):
                    last = nc.tensor.matmul(h_ps[s % 2], xT[:, s, k * P:(k + 1) * P], wall[:, k, 0:HC],
                                            start=(k == 0), stop=(k == KC - 1))
                last.then_inc(proj_made, 1)

            pipeline(pe, NT, [(2, project), (0, transpose_x)], R)

        @block.scalar
        def _(act):
            def copy_xT(t, s, i):
                act.wait_ge(xT_made, t + 1)
                if again(t, R):
                    act.wait_ge(proj_made, t - R + 1)
                    act.wait_ge(xT_out[s], 16 * i)
                nc.scalar.copy(xT[:, s, :], xT_ps[s % 2]).then_inc(xT_ready, 1)

            def copy_h(t, s, i):
                act.wait_ge(proj_made, t + 1)
                if again(t, R):
                    act.wait_ge(h_out[s], 32 * i)
                    act.wait_ge(rest_ready, t - R + 1)
                nc.scalar.copy(hrow[:, s, :], h_ps[s % 2]).then_inc(hrow_ready, 1)

            pipeline(act, NT, [(1, copy_xT), (2, copy_h)], R)

        @block.gpsimd
        def _(pool):
            def rest_of_first(t, s, i):
                pool.wait_ge(part1_ready, t + 1)
                if again(t, 2):
                    pool.wait_ge(parts_made, t - 1)
                nc.gpsimd.tensor_tensor(rest[:, s % 2, :], hrow[:, s, 0:HX], part(t, 0), ALU.subtract
                                        ).then_inc(rest_ready, 1)

            def third_part(t, s, i):
                pool.wait_ge(part2_ready, t + 1)
                nc.gpsimd.tensor_tensor(part(t, 2), rest[:, s % 2, :], part(t, 1), ALU.subtract).then_inc(parts_made, 1)

            pipeline(pool, NT, [(1, third_part), (0, rest_of_first)], R)


def gather_s_src(nc, q, stab, src, s_src, gathered):
    for k in range(TILES):
        col = (q * TILES + k) * HEADS
        nc.gpsimd.indirect_dma_start(
            s_src[:, col:col + HEADS], None, stab,
            bass.IndirectOffsetOnAxis(ap=src[:, q * QUAD + k // 2, k % 2:k % 2 + 1], axis=0)).then_inc(gathered, 16)


def project_dense(nc, c, ms, r1, wall, xTtab, qtab, stab, src, s_src):
    with ExitStack() as ctx:
        sb = lambda name, shape, dt=F32: ctx.enter_context(nc.sbuf_tensor(name, shape, dt))
        sem = semaphores(nc, ctx)
        gathered, = gather_semaphores(c, 1)
        R = 4
        xT, qk = sb("xT2", [P, R, D]), sb("qk", [P, R, 2 * D])
        neg, pos = sb("neg", [P, 2, 2 * D]), sb("pos", [P, 2, 2 * D])
        v = sb("v", [P, R, KC, P + 1])
        scale = sb("scale", [P, 2])
        proj_made, neg_ready, v_ready, exp_ready, qk_ready = (
            sem("proj2_made"), sem("neg_ready"), sem("v_ready"), sem("exp_ready"), sem("qk_ready"))
        scale_ready, kv_used, one_ready, r1_ready = (
            sem("scale_ready"), sem("kv_used"), sem("one_ready"), sem("r1_ready"))
        xT_in = [sem(f"xT_in{s}") for s in range(R)]
        q_out = [sem(f"q_out{s}") for s in range(R)]
        block = ctx.enter_context(nc.Block())
        v_ps = [c.ps[b][:, 0:D] for b in (0, 1)]
        qk_ps = [c.ps[2], c.ps[3]]
        kv_ps = c.ps[4][:, 0:KC * (P + 1)].rearrange("p (c n) -> p c n", c=KC)

        @block.sync
        def _(sp):
            def load(t, s, i):
                if again(t, R):
                    sp.wait_ge(proj_made, t - R + 1)
                sp.dma_start(xT[:, s, :], xTtab[bass.ds(t * P, P), :]).then_inc(xT_in[s], 16)

            def store(t, s, i):
                sp.wait_ge(qk_ready, t + 1)
                sp.dma_start(qtab[bass.ds(t * P, P), :], qk[:, s, 0:D]).then_inc(q_out[s], 16)

            pipeline(sp, NT, [(0, load), (3, store)], R)
            for s in range(R):
                sp.wait_ge(q_out[s], 16 * len(range(s, NT, R)))

        @block.gpsimd
        def _(pool):
            nc.gpsimd.tensor_tensor(r1[:], ms[:], c.minus_half[:].broadcast_to([P, NT]), ALU.pow).then_inc(r1_ready, 1)
            for q in range(EARLY):
                gather_s_src(nc, q, stab, src, s_src, gathered)
            pool.wait_ge(gathered, 16 * TILES * EARLY)

        @block.vector
        def _(dve):
            nc.vector.memset(v[:, :, :, P:P + 1], 1.0).then_inc(one_ready, 1)
            dve.wait_ge(r1_ready, 1)

            def negative_part(t, s, i):
                if again(t, 2):
                    dve.wait_ge(exp_ready, t - 1)
                    dve.wait_ge(qk_ready, t - 1)
                nc.vector.tensor_copy(scale[:, s % 2:s % 2 + 1], r1[:, bass.ds(t, 1)]).then_inc(scale_ready, 1)
                dve.wait_ge(proj_made, t + 1)
                nc.vector.tensor_scalar(neg[:, s % 2, :], qk_ps[s % 2][:], 0.0, None, ALU.min
                                        ).then_inc(neg_ready, 1)

            def feature_map(t, s, i):
                dve.wait_ge(exp_ready, t + 1)
                if again(t, R):
                    if not (isinstance(t, int) and t - R >= LAST):
                        dve.wait_ge(kv_used, t - R + 1)
                    dve.wait_ge(q_out[s], 16 * i)
                nc.vector.tensor_tensor(qk[:, s, :], pos[:, s % 2, :], neg[:, s % 2, :], ALU.add
                                        ).then_inc(qk_ready, 1)

            pipeline(dve, NT, [(1, feature_map), (0, negative_part)], R)

        @block.tensor
        def _(pe):
            def project(t, s, i):
                pe.wait_ge(xT_in[s], 16 * (i + 1))
                if again(t, 2):
                    pe.wait_ge(exp_ready, t - 1)
                for out, lo, n in ((v_ps[s % 2], COL_V, D), (qk_ps[s % 2][:, :], COL_QK, 2 * D)):
                    for k in range(KC):
                        last = nc.tensor.matmul(out, xT[:, s, k * P:(k + 1) * P], wall[:, k, lo:lo + n],
                                                start=(k == 0), stop=(k == KC - 1))
                last.then_inc(proj_made, 1)

            def sum_kv(t, s, i):
                first, last = (t == 0, t == LAST) if isinstance(t, int) else (False, False)
                rows = LAST_ROWS if last else P
                pe.wait_ge(qk_ready, t + 1)
                pe.wait_ge(v_ready, t + 1)
                if isinstance(t, int) and t > LAST:
                    return
                for m in range(KC):
                    made = nc.tensor.matmul(kv_ps[:, m, :], qk[0:rows, s, D + m * P:D + (m + 1) * P], v[0:rows, s, m, :],
                                            start=(first and m == 0), stop=last, skip_group_check=True)
                made.then_inc(kv_used, 1)

            pe.wait_ge(one_ready, 1)
            pipeline(pe, NT, [(0, project), (2, sum_kv)], R)

        @block.scalar
        def _(act):
            def evacuate(t, s, i):
                act.wait_ge(proj_made, t + 1)
                if again(t, R):
                    act.wait_ge(kv_used, t - R + 1)
                act.wait_ge(scale_ready, t + 1)
                nc.scalar.activation(v[:, s, :, 0:P], v_ps[s % 2].rearrange("p (c n) -> p c n", c=KC), ACT.Copy,
                                     scale=scale[:, s % 2:s % 2 + 1]).then_inc(v_ready, 1)
                act.wait_ge(neg_ready, t + 1)
                if again(t, 2):
                    act.wait_ge(qk_ready, t - 1)
                nc.scalar.activation(pos[:, s % 2, :], qk_ps[s % 2][:], ACT.Relu, scale=scale[:, s % 2:s % 2 + 1])
                nc.scalar.activation(neg[:, s % 2, :], neg[:, s % 2, :], ACT.Exp, scale=scale[:, s % 2:s % 2 + 1]
                                     ).then_inc(exp_ready, 1)

            pipeline(act, NT, [(0, evacuate)], R)


def mix_weights(nc, c, w_out, mix, ksum):
    with ExitStack() as ctx:
        sb = lambda name, shape, dt=F32: ctx.enter_context(nc.sbuf_tensor(name, shape, dt))
        sem = semaphores(nc, ctx)
        wo, kv, kvT, diag = sb("wo", [P, KC, D]), sb("kv", [P, KC, P]), sb("kvT", [P, KC, P]), sb("diag", [P, KC, P])
        sums = sb("k_sums", [P, KC])
        wo_in, kv_zero, kv_ready, kv_turned, kvT_ready, mix_made = (
            sem("wo_in"), sem("kv_zero"), sem("kv_ready"), sem("kv_turned"), sem("kvT_ready"), sem("mix_made"))
        sums_ready, diag_ready = sem("k_sums_ready"), sem("diag_ready")
        block = ctx.enter_context(nc.Block())
        kv_ps = c.ps[4][:, 0:KC * (P + 1)].rearrange("p (c n) -> p c n", c=KC)
        kvT_ps = c.ps[1][:, 0:D].rearrange("p (c n) -> p c n", c=KC)
        mix_ps = c.ps[0][:, :].rearrange("p (c n) -> p c n", c=KC)
        ksum_ps = c.ps[2][:, 0:D].rearrange("p (c n) -> p c n", c=KC)

        @block.sync
        def _(sp):
            sp.dma_start(wo[:], w_out.rearrange("(c p) n -> p c n", p=P)).then_inc(wo_in, 16)

        @block.vector
        def _(dve):
            nc.vector.memset(kv[:], 0.0).then_inc(kv_zero, 1)
            nc.vector.tensor_copy(sums[:], kv_ps[:, :, P]).then_inc(sums_ready, 1)
            dve.wait_ge(kv_zero, 1)
            for hd in range(HEADS):
                rows = slice(HD * hd % P, HD * hd % P + HD)
                nc.vector.tensor_copy(kv[rows, HD * hd // P, rows], kv_ps[rows, HD * hd // P, rows]).then_inc(kv_ready, 1)
            dve.wait_ge(sums_ready, 1)
            for m in range(KC):
                nc.vector.tensor_scalar(diag[:, m, :], c.ident[:], sums[:, m:m + 1], None, ALU.mult
                                        ).then_inc(diag_ready, 1)
            dve.wait_ge(kv_turned, 1)
            nc.vector.tensor_copy(kvT[:], kvT_ps).then_inc(kvT_ready, 1)
            dve.wait_ge(mix_made, 1)
            nc.vector.tensor_copy(ksum[:].rearrange("p (c n) -> p c n", c=KC), ksum_ps)
            nc.vector.tensor_copy(mix[:], mix_ps)

        @block.tensor
        def _(pe):
            pe.wait_ge(kv_ready, HEADS)
            for m in range(KC):
                last = nc.tensor.transpose(kvT_ps[:, m, :], kv[:, m, :], c.ident[:])
            last.then_inc(kv_turned, 1)
            pe.wait_ge(diag_ready, KC)
            for m in range(KC):
                nc.tensor.matmul(ksum_ps[:, m, :], c.ones[:], diag[:, m, :], start=True, stop=True)
            pe.wait_ge(kvT_ready, 1)
            pe.wait_ge(wo_in, 16)
            for m in range(KC):
                last = nc.tensor.matmul(mix_ps[:, m, :], kvT[:, m, :], wo[:, m, :], start=True, stop=True)
            last.then_inc(mix_made, 1)


def plan_steps(nc, c, dst_t, src_t, attr_t, edge_w, wparts, dl, src, keys, blocks, block_row,
               attr_parts, dlrows):
    with ExitStack() as ctx:
        sb = lambda name, shape, dt=F32: ctx.enter_context(nc.sbuf_tensor(name, shape, dt))
        sem = semaphores(nc, ctx)
        dst16 = sb("dst16", [P, SG, 2 * P], BF16)
        all_i, all_blocks = sb("all_i", [P, ET], I32), sb("all_blocks", [P, ET], BF16)
        below = sb("below", [P, 2, ET], BF16)
        part = sb("part", [P, NT])
        count = sb("count", [P, NT])
        ci, lo, hi = sb("ci", [P, NT], I32), sb("lo", [P, NT], I32), sb("hi", [P, NT], I32)
        steps_i = sb("steps_i", [P, NT], I32)
        lof, nsteps, some = sb("lof", [P, NT]), sb("nsteps", [P, NT]), sb("some", [P, NT])
        ends, starts = sb("ends", [P, NT]), sb("starts", [P, NT])
        base, dbase = sb("base", [P, NT]), sb("dbase", [P, NT])
        zero = sb("zero", [P, NT])
        pid = sb("pid", [P, SG])
        reached = sb("reached", [P, SG, 2, NT])
        nblocks, tbase, live = sb("nblocks", [P, SG]), sb("tbase", [P, SG]), sb("live", [P, SG])
        block_f, tile_f = sb("block_f", [P, SG]), sb("tile_f", [P, SG])
        block_i, tiles_i = sb("block_i", [P, SG], I32), sb("tiles_i", [P, SG, 2], I32)
        first_node = sb("first_node", [P, SG])
        dst_i, src_i = sb("dst_i", [P, 2 * SG, P], I32), sb("src_i", [P, 2 * SG, P], I32)
        dst_f, src_f = sb("dst_f", [P, 2 * SG, P]), sb("src_f", [P, 2 * SG, P])
        own = sb("own", [P, 2 * SG, P])
        attr = sb("attr", [P, 2 * SG, 4 * P])
        rest = sb("attr_rest", [P, 4 * P])
        split = sb("split", [P, SG, 3, 4, 2 * P], BF16)
        ew, ew_rest = sb("ew", [4, HX]), sb("ew_rest", [4, HX])
        ew_parts = sb("ew_parts", [4, 3, HX], BF16)
        loaded, step_sem, counted, summed = sem("loaded"), sem("plan_step"), sem("counted"), sem("summed")
        tiles_ready, blocks_ready = sem("tiles_ready"), sem("blocks_ready")
        tables_in, attr_in = gather_semaphores(c, 2)
        iota_ready, split_ready = sem("iota_ready"), sem("split_ready")
        fields_ready, turned, taken, stored = sem("fields_ready"), sem("turned"), sem("taken"), sem("stored")
        ew_ready, wparts_in, rows_ready = sem("ew_ready"), sem("wparts_in"), sem("dl_rows_ready")
        block = ctx.enter_context(nc.Block())

        @block.sync
        def _(sp):
            sp.dma_start(all_i[:], dst_t.rearrange("t e -> (t e)").rearrange("(p n) -> p n", p=P)).then_inc(loaded, 16)
            sp.dma_start(ew[:], edge_w).then_inc(loaded, 16)
            sp.wait_ge(ew_ready, 3)
            for j in range(3):
                for i in range(3):
                    row = (j * 3 + i) * 4
                    sp.dma_start(wparts[row:row + 4, :], ew_parts[:, j, :]).then_inc(wparts_in, 16)
            sp.wait_ge(blocks_ready, 1)
            sp.dma_start(blocks.rearrange("o (g p) -> p (o g)", p=P), block_i[:],
                         allow_slow_non_contiguous=True).then_inc(stored, 16)
            sp.wait_ge(stored, 16)
            sp.dma_start(block_row[:], blocks).then_inc(stored, 16)
            sp.wait_ge(rows_ready, SG)
            for g in range(SG):
                sp.dma_start(dlrows.rearrange("q (k n) -> (q k) n", k=QUAD)[g * P:(g + 1) * P, :], dst16[:, g, :]
                             ).then_inc(stored, 16)
            for g in range(SG):
                sp.wait_ge(split_ready, g + 1)
                for i in range(3):
                    sp.dma_start(attr_parts[i * 4:i * 4 + 4, g * P:(g + 1) * P, :].rearrange("c p e -> p c e"),
                                 split[:, g, i, :, :]).then_inc(stored, 16)
            sp.wait_ge(stored, 16 * (2 + 4 * SG))
            sp.wait_ge(wparts_in, 9 * 16)

        @block.gpsimd
        def _(pool):
            nc.gpsimd.iota(pid[:], [[P, SG]], base=0, channel_multiplier=1,
                           allow_small_or_imprecise_dtypes=True).then_inc(iota_ready, 1)
            pool.wait_ge(tiles_ready, 1)
            for g in range(SG):
                for e in range(2):
                    at = bass.IndirectOffsetOnAxis(ap=tiles_i[:, g, e:e + 1], axis=0)
                    j = 2 * g + e
                    nc.gpsimd.indirect_dma_start(dst_i[:, j, :], None, dst_t, at).then_inc(tables_in, 16)
                    nc.gpsimd.indirect_dma_start(src_i[:, j, :], None, src_t, at).then_inc(tables_in, 16)
                    nc.gpsimd.indirect_dma_start(attr[:, j, :], None, attr_t, at).then_inc(attr_in, 16)

        @block.vector
        def _(dve):
            step = Steps()

            def done(ins):
                ins.then_inc(step_sem, 1)
                dve.wait_ge(step_sem, step.last())

            V = nc.vector
            dve.wait_ge(loaded, 32)
            V.tensor_copy(ew_parts[:, 0, :], ew[:]).then_inc(ew_ready, 1)
            dve.wait_ge(ew_ready, 1)
            done(V.tensor_tensor(ew_rest[:], ew[:], ew_parts[:, 0, :], ALU.subtract))
            V.tensor_copy(ew_parts[:, 1, :], ew_rest[:]).then_inc(ew_ready, 1)
            dve.wait_ge(ew_ready, 2)
            V.tensor_tensor(ew_parts[:, 2, :], ew_rest[:], ew_parts[:, 1, :], ALU.subtract).then_inc(ew_ready, 1)
            done(V.memset(zero[:], 0.0))
            done(V.tensor_single_scalar(all_i[:], all_i[:], 7, ALU.arith_shift_right))
            done(V.tensor_copy(all_blocks[:], all_i[:]))
            for b in range(NT):
                if b >= 2:
                    dve.wait_ge(counted, b - 1)
                V.tensor_scalar(below[:, b % 2, :], all_blocks[:], float(b), 0.0, ALU.is_lt, ALU.add,
                                accum_out=part[:, b:b + 1]).then_inc(counted, 1)
            dve.wait_ge(summed, 1)
            done(V.tensor_copy(count[:], c.ps[0][:, 0:NT]))
            done(V.tensor_copy(ci[:], count[:]))
            B = NT - 1
            done(V.tensor_single_scalar(lo[:], ci[:], 7, ALU.arith_shift_right))
            done(V.tensor_scalar(count[:], count[:], 127.0, None, ALU.add))
            done(V.tensor_copy(ci[:], count[:]))
            done(V.tensor_single_scalar(hi[:], ci[:], 7, ALU.arith_shift_right))
            done(V.tensor_copy(lof[:], lo[:]))
            done(V.tensor_copy(nsteps[:], hi[:]))
            done(V.tensor_tensor(some[:, 0:B], count[:, 1:NT], count[:, 0:B], ALU.is_gt))
            done(V.tensor_tensor(ends[:, 0:B], nsteps[:, 1:NT], lof[:, 0:B], ALU.subtract))
            done(V.tensor_tensor(ends[:, 0:B], ends[:, 0:B], some[:, 0:B], ALU.mult))
            done(V.tensor_scalar(ends[:, 0:B], ends[:, 0:B], 1.0, None, ALU.add))
            done(V.tensor_copy(steps_i[:, 0:B], ends[:, 0:B]))
            done(V.tensor_single_scalar(steps_i[:, 0:B], steps_i[:, 0:B], 1, ALU.arith_shift_right))
            done(V.tensor_copy(nsteps[:, 0:B], steps_i[:, 0:B]))
            done(V.tensor_tensor_scan(ends[:, 0:B], nsteps[:, 0:B], zero[:, 0:B], 0.0, ALU.add, ALU.add))
            done(V.tensor_tensor(starts[:, 0:B], ends[:, 0:B], nsteps[:, 0:B], ALU.subtract))
            done(V.scalar_tensor_tensor(out=base[:, 0:B], in0=starts[:, 0:B], scalar=-2.0, in1=lof[:, 0:B],
                                        op0=ALU.mult, op1=ALU.add))
            done(V.tensor_copy(dbase[:, 0:1], base[:, 0:1]))
            done(V.tensor_tensor(dbase[:, 1:B], base[:, 1:B], base[:, 0:B - 1], ALU.subtract))
            dve.wait_ge(iota_ready, 1)
            for g in range(SG):
                done(V.tensor_scalar(reached[:, g, 0, 0:B], starts[:, 0:B], pid[:, g:g + 1], None, ALU.is_le))
                done(V.tensor_tensor(reached[:, g, 1, 0:B], reached[:, g, 0, 0:B], dbase[:, 0:B], ALU.mult))
                done(V.tensor_reduce(nblocks[:, g:g + 1], reached[:, g, 0, 0:B], AX.X, ALU.add))
                done(V.tensor_reduce(tbase[:, g:g + 1], reached[:, g, 1, 0:B], AX.X, ALU.add))
            done(V.tensor_scalar(live[:], pid[:], ends[:, B - 1:B], None, ALU.is_lt))
            done(V.tensor_scalar(block_f[:], nblocks[:], -1.0 - B, None, ALU.add))
            done(V.tensor_tensor(block_f[:], block_f[:], live[:], ALU.mult))
            done(V.tensor_scalar(block_f[:], block_f[:], float(B), None, ALU.add))
            done(V.scalar_tensor_tensor(out=tile_f[:], in0=pid[:], scalar=2.0, in1=tbase[:], op0=ALU.mult,
                                        op1=ALU.add))
            done(V.tensor_scalar(tile_f[:], tile_f[:], -(ET - 2.0), None, ALU.add))
            done(V.tensor_tensor(tile_f[:], tile_f[:], live[:], ALU.mult))
            done(V.tensor_scalar(tile_f[:], tile_f[:], ET - 2.0, None, ALU.add))
            V.tensor_copy(block_i[:], block_f[:]).then_inc(blocks_ready, 1)
            done(V.tensor_copy(tiles_i[:, :, 0], tile_f[:]))
            done(V.tensor_scalar(tile_f[:], tile_f[:], 1.0, None, ALU.add))
            V.tensor_copy(tiles_i[:, :, 1], tile_f[:]).then_inc(tiles_ready, 1)
            done(V.tensor_scalar(first_node[:], block_f[:], float(P), None, ALU.mult))
            dve.wait_ge(tables_in, 4 * SG * 16)
            done(V.tensor_copy(dst_f[:], dst_i[:]))
            V.tensor_copy(src_f[:], src_i[:]).then_inc(fields_ready, 1)
            for g in range(SG):
                own_g, dst_g = own[:, 2 * g:2 * g + 2, :], dst_f[:, 2 * g:2 * g + 2, :]
                done(V.tensor_scalar(dst_g, dst_g, first_node[:, g:g + 1], None, ALU.subtract))
                done(V.tensor_scalar(own_g, dst_g, 0.0, None, ALU.is_ge))
                done(V.scalar_tensor_tensor(out=own_g, in0=dst_g, scalar=float(P), in1=own_g, op0=ALU.is_lt,
                                            op1=ALU.mult))
                done(V.tensor_scalar(first_node[:, g:g + 1], first_node[:, g:g + 1], 1.0, None, ALU.add))
                V.scalar_tensor_tensor(out=own_g, in0=dst_g, scalar=first_node[:, g:g + 1], in1=own_g,
                                       op0=ALU.add, op1=ALU.mult).then_inc(fields_ready, 1)
                V.tensor_copy(dst16[:, g, :], dst_g.rearrange("p e n -> p (e n)")).then_inc(rows_ready, 1)
            for g in range(SG):
                lo_, hi_ = g * P, min(NS, (g + 1) * P)
                dve.wait_ge(turned, g + 1)
                for j, (field, out) in enumerate(((0, dl), (1, src), (2, keys))):
                    bank = c.ps[1 + 3 * (g % 2) + j][:, 0:2 * P].rearrange("p (e n) -> p n e", e=2)
                    done(V.tensor_copy(out[:, lo_:hi_, :], bank[:, 0:hi_ - lo_, :]))
                dve.sem_inc(taken, 1)
            dve.wait_ge(attr_in, 2 * SG * 16)
            for g in range(SG):
                for e in range(2):
                    a = attr[:, 2 * g + e, :]
                    cut = lambda i: split[:, g, i, :, e * P:(e + 1) * P]
                    r = rest[:].rearrange("p (c e) -> p c e", c=4)
                    a = a.rearrange("p (c e) -> p c e", c=4)
                    done(V.tensor_copy(cut(0), a))
                    done(V.tensor_tensor(r, a, cut(0), ALU.subtract))
                    done(V.tensor_copy(cut(1), r))
                    done(V.tensor_tensor(cut(2), r, cut(1), ALU.subtract))
                dve.sem_inc(split_ready, 1)

        @block.tensor
        def _(pe):
            pe.wait_ge(counted, NT)
            nc.tensor.matmul(c.ps[0][:, 0:NT], c.ones[:], part[:], start=True, stop=True
                             ).then_inc(summed, 1)
            pe.wait_ge(fields_ready, 1 + SG)
            for g in range(SG):
                if g >= 2:
                    pe.wait_ge(taken, g - 1)
                for j, field in enumerate((dst_f, src_f, own)):
                    for e in range(2):
                        last = nc.tensor.transpose(c.ps[1 + 3 * (g % 2) + j][:, e * P:(e + 1) * P],
                                                   field[:, 2 * g + e, :], c.ident[:])
                last.then_inc(turned, 1)




def load_blocks(nc, eng, block_row, q):
    _, blocks = nc.values_load_multi_w_load_instructions(block_row[0:1, bass.ds(q * QUAD, QUAD)], engines=[eng],
                                                         min_val=0, max_val=NT - 1)
    return blocks


def score_edges(nc, c, wparts, hparts, stab, attr_parts, dlrows, src, block_row, alpha):
    with ExitStack() as ctx:
        sb = lambda name, shape, dt=F32: ctx.enter_context(nc.sbuf_tensor(name, shape, dt))
        sem = semaphores(nc, ctx)
        att = sb("att_cols", [36, 2, QUAD * 2 * P], BF16)
        dl_all = sb("dl_all", [P, 2, TILES * P], BF16)
        onehotT = sb("onehotT", [P, 2, TILES, P], BF16)
        R = 4
        GT = 2 * TILES
        stage, ssrc = sb("src_stage", [P, R, GT], I32), sb("ssrc", [P, R, GT, HEADS])
        enc, prod = sb("enc", [P, 2, 2, HX]), sb("eprod", [P, 2, 2, HX])
        red = sb("red", [P, 2, TILES, HEADS])
        att_in = [sem(f"attr_in{s}") for s in range(2)]
        dl_in = [sem(f"dl_in{s}") for s in range(2)]
        ssrc_in = gather_semaphores(c, R)
        staged, onehotT_ready = sem("staged"), sem("onehotT_ready")
        enc_made, enc_ready, hdst_made, prod_ready = (
            sem("enc_made"), sem("enc_ready"), sem("hdst_made"), sem("eprod_ready"))
        collected = sem("s_src_collected")
        red_ready, sum_step, alpha_ready = sem("red_ready"), sem("sum_step"), sem("alpha_ready")
        block = ctx.enter_context(nc.Block())
        enc_ps = [c.banks[:, b:b + 2, 0:HX] for b in (0, 2)]
        hdst_ps = [c.banks[:, b:b + 2, 0:HX] for b in (4, 6)]

        @block.sync
        def _(sp):
            def load(q, s, i):
                if again(q, 2):
                    sp.wait_ge(enc_made, QUAD * (q - 1))
                    sp.wait_ge(onehotT_ready, q - 1)
                for j in range(3):
                    sp.dma_start(att[12 * j:12 * j + 12, s, :],
                                 attr_parts[:, bass.ds(q * QUAD, QUAD), :].rearrange("c p e -> c (p e)")
                                 ).then_inc(att_in[s], 16)
                sp.dma_start(dl_all[:, s, :], dlrows[bass.ds(q, 1), :].broadcast_to([P, TILES * P])
                             ).then_inc(dl_in[s], 16)

            pipeline(sp, NQ, [(0, load)])

        @block.gpsimd
        def _(pool):
            def gather(g, s, i):
                if again(g, R):
                    pool.wait_ge(collected, g - R + 1)
                nc.gpsimd.tensor_copy(stage[:, s, :], src[:, bass.ds(2 * g * QUAD + EARLY * QUAD, 2 * QUAD), :].rearrange(
                    "p n e -> p (n e)")).then_inc(staged, 1)
                wait_apart(pool, staged, g + 1, c.passed)
                for k in range(GT):
                    nc.gpsimd.indirect_dma_start(
                        ssrc[:, s, k, :], None, stab,
                        bass.IndirectOffsetOnAxis(ap=stage[:, s, k:k + 1], axis=0)).then_inc(ssrc_in[s], 16)

            def collect(g, s, i):
                pool.wait_ge(ssrc_in[s], 16 * GT * (i + 1))
                nc.gpsimd.tensor_copy(alpha[:, bass.ds(g * GT * HEADS + EARLY * TILES * HEADS, GT * HEADS)],
                                      ssrc[:, s, :, :].rearrange("p k h -> p (k h)")).then_inc(collected, 1)

            pipeline(pool, (NQ - EARLY) // 2, [(2, collect), (0, gather)], R)

        @block.tensor
        def _(pe):
            def expand(q, s, i):
                blk = load_blocks(nc, mybir.EngineType.PE, block_row, q)
                pe.wait_ge(att_in[s], 48 * (i + 1))
                pe.wait_ge(onehotT_ready, q + 1)
                for k in range(QUAD):
                    u, b = q * QUAD + k, k % 2
                    if again(u, 2):
                        pe.wait_ge(enc_ready, u - 1)
                    for e in range(2):
                        last = nc.tensor.matmul(enc_ps[b][:, e, :], att[:, s, (2 * k + e) * P:(2 * k + e + 1) * P],
                                                wparts[:], start=True, stop=True)
                    last.then_inc(enc_made, 1)
                    if again(u, 2):
                        pe.wait_ge(prod_ready, u - 1)
                    for e in range(2):
                        for j in range(3):
                            last = nc.tensor.matmul(hdst_ps[b][:, e, :], onehotT[:, s, 2 * k + e, :],
                                                    hparts[:, bass.ds(blk[k], 1), j, :].rearrange("p o n -> p (o n)"),
                                                    start=(j == 0), stop=(j == 2))
                    last.then_inc(hdst_made, 1)

            pipeline(pe, NQ, [(0, expand)])

        @block.scalar
        def _(act):
            def relu(q, s, i):
                for k in range(QUAD):
                    u, b = q * QUAD + k, k % 2
                    act.wait_ge(enc_made, u + 1)
                    if again(u, 2):
                        act.wait_ge(prod_ready, u - 1)
                    nc.scalar.activation(enc[:, b], enc_ps[b], ACT.Relu).then_inc(enc_ready, 1)

            pipeline(act, NQ, [(0, relu)])

        @block.vector
        def _(dve):
            V = nc.vector

            def onehots(q, s, i):
                dve.wait_ge(dl_in[s % 2], 16 * (2 * i + s // 2 + 1))
                if again(q, 2):
                    dve.wait_ge(hdst_made, QUAD * (q - 1))
                V.tensor_scalar(onehotT[:, s % 2, :, :].rearrange("p k e -> p (k e)"), dl_all[:, s % 2, :], c.lane[:],
                                None, ALU.is_equal).then_inc(onehotT_ready, 1)

            def score(q, s, i):
                for k in range(QUAD + 1):
                    if k < QUAD:
                        u, b = q * QUAD + k, k % 2
                        dve.wait_ge(enc_ready, u + 1)
                        dve.wait_ge(hdst_made, u + 1)
                        if again(u, 2):
                            dve.wait_ge(red_ready, u - 1)
                        V.tensor_tensor(prod[:, b], hdst_ps[b], enc[:, b], ALU.mult).then_inc(prod_ready, 1)
                    if k > 0:
                        u, b = q * QUAD + k - 1, (k - 1) % 2
                        dve.wait_ge(prod_ready, u + 1)
                        V.tensor_reduce(red[:, s % 2, 2 * k - 2:2 * k, :],
                                        prod[:, b].rearrange("p e (h d) -> p e h d", h=HEADS), AX.X, ALU.add
                                        ).then_inc(red_ready, 1)

            def close(q, s, i):
                dve.wait_ge(red_ready, QUAD * (q + 1))
                r = red[:, s % 2, :, :].rearrange("p k h -> p (k h)")
                if not isinstance(q, int) or q >= EARLY:
                    dve.wait_ge(collected, 2 * i + s // 2 - EARLY // 2 + 1)
                s_src = alpha[:, bass.ds(q * TILES * HEADS, TILES * HEADS)]
                V.tensor_tensor(r, r, s_src, ALU.add).then_inc(sum_step, 1)
                dve.wait_ge(sum_step, q + 1)
                V.scalar_tensor_tensor(out=alpha[:, bass.ds(q * TILES * HEADS, TILES * HEADS)], in0=r, scalar=0.2,
                                       in1=r, op0=ALU.mult, op1=ALU.max).then_inc(alpha_ready, 1)

            pipeline(dve, NQ, [(0, onehots), (2, close), (1, score)], R, straight=EARLY + R)


RANGES = P // HEADS
RC = 2 * NS // RANGES
RL = RC * P
FAR = 1e30
assert RC * RANGES == 2 * NS


def softmax_numerators(nc, c, keys, alpha, a, key, cross, xs):
    with ExitStack() as ctx:
        sb = lambda name, shape, dt=F32: ctx.enter_context(nc.sbuf_tensor(name, shape, dt))
        sem = semaphores(nc, ctx)
        cut, top = sb("cut", [P, RL + 1]), sb("top", [P, RL])
        edge = sb("edge_keys", [P, 2])
        ends = sb("range_ends", [P, 2])
        row = sb("range_rows", [HEADS, 2, RANGES])
        carried = sb("carried", [HEADS, RANGES + 1])
        carry = sb("carry", [P, 2])
        whole, set_back = sb("whole", [P, 1]), sb("set_back", [P, 2])
        turned, copied, ready, dma, step_sem = (
            sem("rows_turned"), sem("rows_copied"), sem("rows_ready"), sem("carry_dma"), sem("softmax_step"))
        wants_dma, back, back_copied = sem("wants_dma"), sem("turned_back"), sem("back_copied")
        exp_ready, ordered, zeroed = sem("num_exp_ready"), sem("ordered"), sem("xs_zeroed")
        block = ctx.enter_context(nc.Block())
        groups = [(g0, min(4, RC - g0)) for g0 in range(0, RC, 4)]
        by_head = lambda x: x.rearrange("p (g t h) -> p t g h", g=RANGES, h=HEADS)
        key_cols = keys[:].rearrange("p n e -> p (n e)").rearrange("p (g t) -> p t g", g=RANGES)

        @block.tensor
        def _(pe):
            pe.wait_ge(ordered, 2)
            for n, (g0, w) in enumerate(groups):
                for j in range(2):
                    m = 2 * n + j
                    if m >= 4:
                        pe.wait_ge(copied, m - 3)
                    for t in range(w):
                        last = nc.tensor.transpose(c.ps[m % 4][:, t * P:(t + 1) * P],
                                                   (top, cut)[j][:, (g0 + t) * P:(g0 + t + 1) * P], c.ident[:])
                    last.then_inc(turned, 1)
            for n, (g0, w) in enumerate(groups):
                pe.wait_ge(exp_ready, 1)
                if n >= 4:
                    pe.wait_ge(back_copied, n - 3)
                for t in range(w):
                    last = nc.tensor.transpose(c.ps[4 + n % 4][:, t * P:(t + 1) * P],
                                               a[:, (g0 + t) * P:(g0 + t + 1) * P], c.ident[:])
                last.then_inc(back, 1)

        @block.scalar
        def _(act):
            act.dma_start(xs.rearrange("(p r) d -> p r d", p=P), c.zeros[:].unsqueeze(1).broadcast_to([P, MT, D])
                          ).then_inc(zeroed, 16)
            nc.scalar.copy(top[:].rearrange("p (t g h) -> p t g h", g=RANGES, h=HEADS), by_head(alpha[:])
                           ).then_inc(ordered, 1)
            for n, (g0, w) in enumerate(groups):
                for j, out in enumerate((a, key)):
                    act.wait_ge(turned, 2 * n + j + 1)
                    nc.scalar.copy(out[:, g0 * P:(g0 + w) * P], c.ps[(2 * n + j) % 4][:, 0:w * P]
                                   ).then_inc(copied, 1)
            act.wait_ge(ready, 1)
            nc.scalar.activation(a, a, ACT.Exp, scale=-1.0).then_inc(exp_ready, 1)
            for n, (g0, w) in enumerate(groups):
                act.wait_ge(back, n + 1)
                nc.scalar.copy(by_head(alpha[:])[:, g0:g0 + w],
                               c.ps[4 + n % 4][:, 0:w * P].rearrange("p (t g h) -> p t g h", t=w, g=RANGES)
                               ).then_inc(back_copied, 1)
            act.wait_ge(zeroed, 16)

        @block.sync
        def _(sp):
            n = 0

            def move(out, in_):
                nonlocal n
                sp.dma_start(out, in_, allow_slow_non_contiguous=True).then_inc(dma, 16)
                n += 1
                sp.wait_ge(dma, 16 * n)

            sp.wait_ge(wants_dma, 1)
            move(edge[HEADS:P, 0:1], key[0:P - HEADS, RL - 1:RL])
            move(edge[0:P - HEADS, 1:2], key[HEADS:P, 0:1])
            for d in range(2):
                sp.wait_ge(wants_dma, 2 + 2 * d)
                move(cross[d, :, :].rearrange("j p -> p j"), ends[:])
                move(row[:], cross[d, :, :].rearrange("j (g h) -> h j g", h=HEADS))
                sp.wait_ge(wants_dma, 3 + 2 * d)
                move(cross[2 + d, 0, :].rearrange("(g h) -> h g", h=HEADS),
                     carried[:, 0:RANGES] if d == 0 else carried[:, 1:RANGES + 1])
                move(carry[:, d:d + 1], cross[2 + d, 0, :].rearrange("(p o) -> p o", o=1))

        @block.vector
        def _(dve):
            V, step = nc.vector, Steps()

            def done(ins):
                ins.then_inc(step_sem, 1)
                dve.wait_ge(step_sem, step.last())

            V.tensor_copy(cut[:, 0:RL].rearrange("p (t g h) -> p t g h", g=RANGES, h=HEADS),
                          key_cols.unsqueeze(3).broadcast_to([P, RC, RANGES, HEADS])).then_inc(ordered, 1)
            V.memset(edge[:, 0:1], -1.0)
            done(V.memset(edge[:, 1:2], -1.0))
            dve.wait_ge(copied, 2 * len(groups))
            dve.sem_inc(wants_dma, 1)
            done(V.tensor_scalar(top[:], key, 0.0, 2 * FAR, ALU.is_gt, ALU.mult))
            V.scalar_tensor_tensor(out=a, in0=top[:], scalar=-FAR, in1=a, op0=ALU.add, op1=ALU.min)
            V.tensor_tensor(cut[:, 1:RL], key[:, 1:RL], key[:, 0:RL - 1], ALU.not_equal)
            V.tensor_tensor(whole[:], key[:, 0:1], key[:, RL - 1:RL], ALU.not_equal)
            dve.wait_ge(dma, 32)
            V.tensor_tensor(cut[:, 0:1], key[:, 0:1], edge[:, 0:1], ALU.not_equal)
            done(V.tensor_tensor(cut[:, RL:RL + 1], key[:, RL - 1:RL], edge[:, 1:2], ALU.not_equal))
            V.tensor_tensor(set_back[:, 0:1], cut[:, 0:1], whole[:], ALU.max)
            done(V.tensor_tensor(set_back[:, 1:2], cut[:, RL:RL + 1], whole[:], ALU.max))
            V.tensor_scalar(set_back[:], set_back[:], -FAR, None, ALU.mult)
            done(V.tensor_scalar(cut[:], cut[:], -FAR, None, ALU.mult))
            for d in range(2):
                if d == 0:
                    out, cuts, vals, last = top[:], cut[:, 0:RL], a, top[:, RL - 1:RL]
                else:
                    out, cuts, vals, last = key[:, ::-1], cut[:, RL:0:-1], top[:, ::-1], key[:, 0:1]
                V.tensor_copy(ends[:, 0:1], set_back[:, d:d + 1])
                done(V.tensor_tensor_scan(out, cuts, vals, -FAR, ALU.add, ALU.max))
                done(V.tensor_copy(ends[:, 1:2], last))
                dve.sem_inc(wants_dma, 1)
                dve.wait_ge(dma, 32 + 32 + 64 * d)
                if d == 0:
                    done(V.memset(carried[:, 0:1], -FAR))
                    done(V.tensor_tensor_scan(carried[:, 1:], row[:, 0, :], row[:, 1, :], -FAR, ALU.add, ALU.max))
                else:
                    done(V.memset(carried[:, RANGES:], -FAR))
                    done(V.tensor_tensor_scan(carried[:, RANGES - 1::-1], row[:, 0, ::-1], row[:, 1, ::-1], -FAR,
                                              ALU.add, ALU.max))
                dve.sem_inc(wants_dma, 1)
                dve.wait_ge(dma, 32 + 64 + 64 * d)
                done(V.tensor_tensor_scan(out, cuts, vals, carry[:, d:d + 1], ALU.add, ALU.max))
            V.scalar_tensor_tensor(out=a, in0=key, scalar=-0.5 * FAR, in1=a, op0=ALU.max, op1=ALU.subtract
                                   ).then_inc(ready, 1)


NN = NT - 1


def sum_messages_and_mix(nc, c, htab, dl, src, block_row, alpha, acc, mix, ksum, x, bias, b_out, w_norm2, qtab,
                         xntab, ytab):
    with ExitStack() as ctx:
        sb = lambda name, shape, dt=F32: ctx.enter_context(nc.sbuf_tensor(name, shape, dt))
        sem = semaphores(nc, ctx)
        R = 4
        onehot = sb("onehot32", [P, 2, TILES, P])
        stage, msg = sb("src_stage2", [P, R, TILES], I32), sb("msg", [P, R, TILES, HX])
        rows_in = gather_semaphores(c, R)
        staged, onehot_ready, msg_ready, sums_made = (
            sem("staged2"), sem("onehot32_ready"), sem("msg_ready"), sem("sums_made"))
        acc_ready, weights_ready = sem("acc_ready"), sem("weights_ready")
        rows_sb = sb("rows_in", [P, 2, D])
        b_row = sb("b_row", [1, D])
        q2, xn2, x2 = sb("q2", [P, 2, D]), sb("xn2", [P, 2, D]), sb("x2", [P, 2, D])
        prod, qz, qT = sb("prod", [P, 2, D]), sb("qz", [P, 2, D]), sb("qT", [P, 2, D])
        den, z = sb("den", [P, 2, HEADS]), sb("z", [P, 2, HEADS])
        h, scaled = sb("h2", [P, 2, D]), sb("h2_scaled", [P, 2, D])
        ss, r2 = sb("ss", [P, 2]), sb("r2", [P, 2])
        y = sb("y", [P, 2, D])
        setup_in = sem("setup_in")
        qx_in = [sem(f"qx_in{s}") for s in range(2)]
        x_in = [sem(f"x2_in{s}") for s in range(2)]
        y_out = [sem(f"y_out{s}") for s in range(2)]
        q_step, y_step = sem("mix_q_step"), sem("mix_y_step")
        qz_ready, qT_made, qT_ready, att_made = sem("qz_ready"), sem("qT_made"), sem("qT_ready"), sem("att_made")
        h_ready, ss_ready, mean_ready, r2_ready, y_ready = (
            sem("h_ready"), sem("ss_ready"), sem("mean_ready"), sem("r2_ready"), sem("y_ready"))
        block = ctx.enter_context(nc.Block())
        SB = 4
        sum_ps = [c.ps[b][:, 0:HX] for b in range(SB)]
        qT_ps = [c.ps[b][:, 0:D] for b in (4, 5)]
        att_ps = [c.ps[b][:, 0:D] for b in (6, 7)]
        heads = lambda ap: ap.rearrange("p (h d) -> p h d", h=HEADS)
        NM = 2 * NN

        def tile_of(fn):
            def run(q, s, i):
                if s % 2 == 0:
                    fn(2 * i + s // 2, s // 2, i)
            return run

        @block.sync
        def _(sp):
            for j, row in enumerate((bias, w_norm2)):
                sp.dma_start(rows_sb[:, j, :], row.rearrange("(o d) -> o d", o=1).broadcast_to([P, D])
                             ).then_inc(setup_in, 16)
            sp.dma_start(b_row[:], b_out.rearrange("(o d) -> o d", o=1)).then_inc(setup_in, 16)

            def load_qx(t, s, i):
                if again(t, 2):
                    sp.wait_ge(h_ready, t - 1)
                for buf, table in ((q2, qtab), (xn2, xntab)):
                    sp.dma_start(buf[:, s, :], table[bass.ds(t * P, P), :]).then_inc(qx_in[s], 16)

            def load_x(t, s, i):
                if again(t, 2):
                    sp.wait_ge(y_ready, t - 1)
                sp.dma_start(x2[:, s, :], x[bass.ds(t * P, P), :]).then_inc(x_in[s], 16)

            def store(t, s, i):
                sp.wait_ge(y_ready, t + 1)
                sp.dma_start(ytab[bass.ds(t * P, P), :], y[:, s, :]).then_inc(y_out[s], 16)

            pipeline(sp, NM, [(0, tile_of(load_qx)), (2, tile_of(load_x)), (6, tile_of(store))], R)
            for s in range(2):
                sp.wait_ge(y_out[s], 16 * len(range(s, NN, 2)))

        @block.gpsimd
        def _(pool):
            def gather(q, s, i):
                if again(q, R):
                    pool.wait_ge(rows_in[s], 16 * TILES * i)
                    pool.wait_ge(sums_made, QUAD * (q - R + 1))
                wait_apart(pool, staged, q + 1, c.passed)
                for k in range(TILES):
                    nc.gpsimd.indirect_dma_start(
                        msg[:, s, k, 0:D], None, htab,
                        bass.IndirectOffsetOnAxis(ap=stage[:, s, k:k + 1], axis=0)).then_inc(rows_in[s], 16)

            def inverse(t, s, i):
                if again(t, 2):
                    pool.wait_ge(y_ready, t - 1)
                wait_apart(pool, ss_ready, t + 1, c.passed)
                nc.gpsimd.tensor_scalar(r2[:, s:s + 1], ss[:, s:s + 1], 1.0 / D, RMS_EPS, ALU.mult,
                                        ALU.add).then_inc(mean_ready, 1)
                pool.wait_ge(mean_ready, t + 1)
                nc.gpsimd.tensor_tensor(r2[:, s:s + 1], r2[:, s:s + 1], c.minus_half[:],
                                        ALU.pow).then_inc(r2_ready, 1)

            pipeline(pool, NQ, [(6, tile_of(inverse), NM), (0, gather)], R)

        @block.vector
        def _(dve):
            V = nc.vector
            V.memset(acc, 0.0).then_inc(acc_ready, 1)
            dve.wait_ge(setup_in, 48)

            def stage_sources(q, s, i):
                if again(q, R):
                    dve.wait_ge(rows_in[s], 16 * TILES * i)
                V.tensor_copy(stage[:, s, :], src[:, bass.ds(q * QUAD, QUAD), :].rearrange("p n e -> p (n e)")
                              ).then_inc(staged, 1)

            def onehots(q, s, k):
                for e in range(2):
                    V.tensor_scalar(onehot[:, s % 2, 2 * k + e, :], c.lane16[:],
                                    dl[:, bass.ds(q * QUAD + k, 1), e:e + 1].rearrange("p a b -> p (a b)"),
                                    None, ALU.is_equal).then_inc(onehot_ready, 1)

            def steps(q, s, i):
                inside = not isinstance(q, int)
                if again(q, 1):
                    blk = load_blocks(nc, mybir.EngineType.DVE, block_row, q - 1)
                if inside or q < NQ:
                    dve.wait_ge(rows_in[s], 16 * TILES * (i + 1))
                for k in range(QUAD):
                    if inside or q < NQ:
                        m = msg[:, s, 2 * k:2 * k + 2, 0:D].rearrange("p e (h d) -> p e h d", h=HEADS)
                        w = alpha[:, bass.ds((q * QUAD + k) * 2 * HEADS, 2 * HEADS)].rearrange("p (e h) -> p e h", e=2)
                        V.tensor_tensor(m, m, w.unsqueeze(3).broadcast_to([P, 2, HEADS, HD]), ALU.mult
                                        ).then_inc(msg_ready, 1)
                    if again(q, 1):
                        u = (q - 1) * QUAD + k
                        rows = acc[:, bass.ds(blk[k], 1), :].rearrange("p o n -> p (o n)")
                        dve.wait_ge(sums_made, u + 1)
                        dve.wait_ge(acc_ready, u + 1)
                        V.tensor_tensor(rows, sum_ps[k % SB], rows, ALU.add).then_inc(acc_ready, 1)
                    if inside or q + 1 < NQ:
                        onehots(q + 1, s + 1, k)

            def normalise_q(t, s, i):
                dve.wait_ge(qx_in[s], 32 * (i + 1))
                V.tensor_tensor(prod[:, s, :], q2[:, s, :], ksum[:], ALU.mult).then_inc(q_step, 1)
                dve.wait_ge(q_step, 4 * t + 1)
                V.tensor_reduce(den[:, s, :], heads(prod[:, s, :]), AX.X, ALU.add).then_inc(q_step, 1)
                dve.wait_ge(q_step, 4 * t + 2)
                V.tensor_scalar(den[:, s, :], den[:, s, :], ATT_EPS, None, ALU.add).then_inc(q_step, 1)
                dve.wait_ge(q_step, 4 * t + 3)
                V.reciprocal(z[:, s, :], den[:, s, :]).then_inc(q_step, 1)
                dve.wait_ge(q_step, 4 * t + 4)
                if again(t, 2):
                    dve.wait_ge(qT_made, t - 1)
                V.tensor_tensor(heads(qz[:, s, :]), heads(q2[:, s, :]),
                                z[:, s, :].unsqueeze(2).broadcast_to([P, HEADS, HD]), ALU.mult).then_inc(qz_ready, 1)

            def add_residual(t, s, i):
                dve.wait_ge(att_made, t + 1)
                if again(t, 2):
                    dve.wait_ge(ss_ready, t - 1)
                V.tensor_tensor(h[:, s, :], att_ps[s], xn2[:, s, :], ALU.add).then_inc(h_ready, 1)

            def finish(t, s, i):
                if again(t, 2):
                    dve.wait_ge(y_out[s], 16 * i)
                dve.wait_ge(x_in[s], 16 * (i + 1))
                V.tensor_tensor(y[:, s, :], x2[:, s, :], rows_sb[:, 0, :], ALU.add)
                dve.wait_ge(r2_ready, t + 1)
                V.scalar_tensor_tensor(out=scaled[:, s, :], in0=h[:, s, :], scalar=r2[:, s:s + 1],
                                       in1=rows_sb[:, 1, :], op0=ALU.mult, op1=ALU.mult).then_inc(y_step, 1)
                dve.wait_ge(y_step, 2 * t + 1)
                V.tensor_tensor(y[:, s, :], y[:, s, :], h[:, s, :], ALU.add).then_inc(y_step, 1)
                dve.wait_ge(y_step, 2 * t + 2)
                V.tensor_tensor(y[:, s, :], y[:, s, :], scaled[:, s, :], ALU.add).then_inc(y_ready, 1)

            for k in range(QUAD):
                onehots(0, 0, k)
            pipeline(dve, NQ, [(1 - R, stage_sources), (0, tile_of(normalise_q), NM), (3, tile_of(add_residual), NM), (0, steps, NQ + 1),
                               (6, tile_of(finish), NM)], R)

        @block.tensor
        def _(pe):
            pe.wait_ge(setup_in, 48)

            def reduce(q, s, i):
                pe.wait_ge(onehot_ready, TILES * (q + 1))
                pe.wait_ge(weights_ready, q + 1)
                for k in range(QUAD):
                    u = q * QUAD + k
                    pe.wait_ge(msg_ready, u + 1)
                    if again(u, SB):
                        pe.wait_ge(acc_ready, u - SB + 2)
                    for e in range(2):
                        last = nc.tensor.matmul(sum_ps[k % SB], onehot[:, s % 2, 2 * k + e, :],
                                                msg[:, s, 2 * k + e, :], start=(e == 0), stop=(e == 1))
                    last.then_inc(sums_made, 1)

            def transpose_q(t, s, i):
                pe.wait_ge(qz_ready, t + 1)
                if again(t, 2):
                    pe.wait_ge(qT_ready, t - 1)
                for k in range(KC):
                    last = nc.tensor.transpose(qT_ps[s][:, k * P:(k + 1) * P], qz[:, s, k * P:(k + 1) * P],
                                               c.ident[:])
                last.then_inc(qT_made, 1)

            def attend(t, s, i):
                pe.wait_ge(qT_ready, t + 1)
                if again(t, 2):
                    pe.wait_ge(h_ready, t - 1)
                for k in range(KC):
                    nc.tensor.matmul(att_ps[s], qT[:, s, k * P:(k + 1) * P], mix[:, k, :], start=(k == 0), stop=False)
                nc.tensor.matmul(att_ps[s], c.ones[0:1, :], b_row[:], start=False, stop=True).then_inc(att_made, 1)

            pipeline(pe, NQ, [(1, tile_of(transpose_q), NM), (2, tile_of(attend), NM), (0, reduce)], R)

        @block.scalar
        def _(act):
            def copy_weights(q, s, i):
                if again(q, R):
                    act.wait_ge(sums_made, QUAD * (q - R + 1))
                nc.scalar.copy(msg[:, s, :, D:HX], alpha[:, bass.ds(q * TILES * HEADS, TILES * HEADS)].rearrange(
                    "p (k h) -> p k h", k=TILES)).then_inc(weights_ready, 1)

            def copy_qT(t, s, i):
                act.wait_ge(qT_made, t + 1)
                if again(t, 2):
                    act.wait_ge(att_made, t - 1)
                nc.scalar.copy(qT[:, s, :], qT_ps[s]).then_inc(qT_ready, 1)

            def squares(t, s, i):
                act.wait_ge(h_ready, t + 1)
                if again(t, 2):
                    act.wait_ge(r2_ready, t - 1)
                    act.wait_ge(y_ready, t - 1)
                nc.scalar.activation(scaled[:, s, :], h[:, s, :], ACT.Square,
                                     accum_out=ss[:, s:s + 1]).then_inc(ss_ready, 1)

            pipeline(act, NQ, [(0, copy_weights), (1, tile_of(copy_qT), NM), (3, tile_of(squares), NM)], R)


EXPERTS = 8
HIDDEN = 1024
HIC = HIDDEN // P
TOPK = 2
MT = (TOPK * N + EXPERTS * (P - 1)) // P
BW = HIDDEN + D


def finish_nodes(nc, c, acc, ytab, x1tab, gate_w, gate_b, biases, scores, bias_parts, w2t, w2, w2_in):
    with ExitStack() as ctx:
        sb = lambda name, shape, dt=F32: ctx.enter_context(nc.sbuf_tensor(name, shape, dt))
        sem = semaphores(nc, ctx)
        R = 4
        gw, gb = sb("gw", [P, KC, EXPERTS]), sb("gb", [P, EXPERTS])
        bias, bias_rest = sb("bias", [EXPERTS, BW]), sb("bias_rest", [EXPERTS, BW])
        bias16 = sb("bias16", [EXPERTS, 3, BW], BF16)
        y = sb("y7", [P, R, D])
        den, rec = sb("den7", [P, NN, HEADS]), sb("rec7", [P, NN, HEADS])
        stats = sb("stats7", [P, NN, 6])
        half, mean, var, rstd = (sb(n, [P, NN]) for n in ("half7", "mean7", "var7", "rstd7"))
        fixed, nT = sb("normed_fixed", [P, R, D]), sb("nT", [P, 2, D])
        consts_in, bias_step, bias_out = sem("gate_in"), sem("bias_step"), sem("bias_out")
        y_in = [sem(f"y7_in{s}") for s in range(R)]
        x1_out, step_sem, divided, x1_ready = sem("x1_out"), sem("finish_step"), sem("divided"), sem("x1_ready")
        var_ready, rstd_ready = sem("var7_ready"), sem("rstd7_ready")
        fixed_ready, placed = sem("normed_ready"), sem("normed_placed")
        turned, nT_ready, gate_made = sem("nT_made"), sem("nT_ready"), sem("gate_made")
        block = ctx.enter_context(nc.Block())
        nT_ps = [c.ps[b][:, 0:D] for b in (0, 1)]
        gate_ps = c.ps[2]
        row = lambda t: acc[:, bass.ds(t, 1), 0:D].rearrange("p o n -> p (o n)")
        heads = lambda ap: ap.rearrange("p (h d) -> p h d", h=HEADS)

        @block.sync
        def _(sp):
            sp.dma_start(gw[:], gate_w.rearrange("(c p) n -> p c n", p=P)).then_inc(consts_in, 16)
            sp.dma_start(gb[:], gate_b.rearrange("(o d) -> o d", o=1).broadcast_to([P, EXPERTS])).then_inc(consts_in, 16)
            sp.dma_start(bias[:], biases).then_inc(consts_in, 16)

            def load(t, s, i):
                if again(t, R):
                    sp.wait_ge(x1_ready, t - R + 1)
                sp.dma_start(y[:, s, :], ytab[bass.ds(t * P, P), :]).then_inc(y_in[s], 16)

            def store(t, s, i):
                sp.wait_ge(x1_ready, t + 1)
                sp.dma_start(x1tab[bass.ds(t * P, P), :], row(t)).then_inc(x1_out, 16)

            pipeline(sp, NN, [(0, load), (R - 1, store)], R)
            for e in range(EXPERTS):
                sp.dma_start(w2[:, e], w2t[e].rearrange("(c p) n -> p c n", p=P)).then_inc(w2_in, 16)
            sp.wait_ge(bias_step, 5)
            sp.dma_start(bias_parts.rearrange("j e n -> e j n"), bias16[:]).then_inc(bias_out, 16)
            sp.wait_ge(bias_out, 16)
            sp.wait_ge(x1_out, 16 * NN)

        @block.gpsimd
        def _(pool):
            pool.wait_ge(consts_in, 48)
            for n, (out, a, b) in enumerate(((bias16[:, 0, :], bias[:], None),
                                             (bias_rest[:], bias[:], bias16[:, 0, :]),
                                             (bias16[:, 1, :], bias_rest[:], None),
                                             (bias_rest[:], bias_rest[:], bias16[:, 1, :]),
                                             (bias16[:, 2, :], bias_rest[:], None))):
                ins = nc.gpsimd.tensor_copy(out, a) if b is None else nc.gpsimd.tensor_tensor(out, a, b, ALU.subtract)
                ins.then_inc(bias_step, 1)
                pool.wait_ge(bias_step, n + 1)
            pool.wait_ge(var_ready, 1)
            nc.gpsimd.tensor_tensor(rstd[:], half[:], c.minus_half[:].broadcast_to([P, NN]), ALU.pow
                                    ).then_inc(rstd_ready, 1)

        @block.vector
        def _(dve):
            V, step = nc.vector, Steps()

            def done(ins):
                ins.then_inc(step_sem, 1)
                dve.wait_ge(step_sem, step.last())

            done(V.tensor_scalar(den[:], acc[:, 0:NN, D:HX], 1e-10, None, ALU.max))
            done(V.reciprocal(rec[:], den[:]))

            def divide(t, s, i):
                V.tensor_tensor(heads(row(t)), heads(row(t)),
                                rec[:, bass.ds(t, 1), :].rearrange("p o h -> p (o h)").unsqueeze(2).broadcast_to(
                                    [P, HEADS, HD]), ALU.mult).then_inc(divided, 1)

            def add(t, s, i):
                dve.wait_ge(divided, t + 1)
                dve.wait_ge(y_in[s], 16 * (i + 1))
                V.tensor_tensor(row(t), y[:, s, :], row(t), ALU.add).then_inc(x1_ready, 1)

            def gather_stats(t, s, i):
                dve.wait_ge(x1_ready, t + 1)
                V.bn_stats(stats[:, bass.ds(t, 1), :].rearrange("p o n -> p (o n)"), row(t))

            pipeline(dve, NN, [(2, gather_stats), (0, divide), (1, add)], R)
            done(V.memset(half[:], 0.0))
            moments(V, done, stats, mean, half, var)
            V.tensor_scalar(half[:], var[:], LN_EPS, None, ALU.add).then_inc(var_ready, 1)
            dve.wait_ge(rstd_ready, 1)

            def norm(t, s, i):
                if again(t, R):
                    dve.wait_ge(placed, t - R + 1)
                    dve.wait_ge(turned, t - R + 1)
                V.tensor_scalar(fixed[:, s, :], row(t), mean[:, bass.ds(t, 1)], rstd[:, bass.ds(t, 1)],
                                ALU.subtract, ALU.mult).then_inc(fixed_ready, 1)

            pipeline(dve, NN, [(0, norm)], R)
            dve.wait_ge(gate_made, NN)
            V.tensor_tensor(scores[:], gate_ps[:, 0:NN * EXPERTS].rearrange("p (t e) -> p t e", e=EXPERTS),
                            gb[:].unsqueeze(1).broadcast_to([P, NN, EXPERTS]), ALU.add)

        @block.tensor
        def _(pe):
            pe.wait_ge(consts_in, 48)

            def turn(t, s, i):
                pe.wait_ge(fixed_ready, t + 1)
                if again(t, 2):
                    pe.wait_ge(nT_ready, t - 1)
                for k in range(KC):
                    last = nc.tensor.transpose(nT_ps[s % 2][:, k * P:(k + 1) * P], fixed[:, s, k * P:(k + 1) * P],
                                               c.ident[:])
                last.then_inc(turned, 1)

            def gate(t, s, i):
                pe.wait_ge(nT_ready, t + 1)
                for k in range(KC):
                    last = nc.tensor.matmul(gate_ps[:, bass.ds(t * EXPERTS, EXPERTS)], nT[:, s % 2, k * P:(k + 1) * P],
                                            gw[:, k, :], start=(k == 0), stop=(k == KC - 1))
                last.then_inc(gate_made, 1)

            pipeline(pe, NN, [(0, turn), (1, gate)], R)

        @block.scalar
        def _(act):
            act.wait_ge(x1_out, 16 * NN)

            def copy_nT(t, s, i):
                act.wait_ge(turned, t + 1)
                if again(t, 2):
                    act.wait_ge(gate_made, t - 1)
                nc.scalar.copy(nT[:, s % 2, :], nT_ps[s % 2]).then_inc(nT_ready, 1)

            def place(t, s, i):
                act.wait_ge(fixed_ready, t + 1)
                nc.scalar.copy(row(t), fixed[:, s, :]).then_inc(placed, 1)

            pipeline(act, NN, [(0, copy_nT), (0, place)], R)


def route(nc, c, scores, normed, xs, probs, slots, expert_row):
    with ExitStack() as ctx:
        sb = lambda name, shape, dt=F32: ctx.enter_context(nc.sbuf_tensor(name, shape, dt))
        sem = semaphores(nc, ctx)
        top, at = sb("top8", [P, NN, 8]), sb("at8", [P, NN, 8], mybir.dt.uint32)
        atf = sb("atf", [P, TOPK, NN])
        gap, one_plus = sb("gap", [P, NN]), sb("one_plus", [P, NN])
        expert_id = sb("expert_id", [P, EXPERTS])
        real = sb("real", [P, 1])
        chosen = sb("chosen", [P, TOPK, NN, EXPERTS])
        both = sb("both", [P, NN, EXPERTS])
        both16, before = sb("both16", [P, NN * EXPERTS], BF16), sb("before", [P, P], BF16)
        ones16 = sb("ones16", [P, P], BF16)
        place, total, running = (sb(n, [P, NN, EXPERTS]) for n in ("place", "total", "running"))
        nrows, ntiles, tend, tstart = (sb(n, [P, EXPERTS]) for n in ("nrows", "ntiles", "tend", "tstart"))
        ntiles_i = sb("ntiles_i", [P, EXPERTS], I32)
        zero = sb("zero8", [P, NN])
        tile_id, passed = sb("tile_id", [P, MT]), sb("passed", [P, MT, EXPERTS])
        expert_f = sb("expert_f", [P, MT])
        slot_f = sb("slot_f", [P, TOPK, NN])
        picked = sb("picked", [P, NN, EXPERTS])
        iota_ready, step_sem, gap_ready, exp_ready = (
            sem("route_iota"), sem("route_step"), sem("gap_ready"), sem("exp8_ready"))
        both_ready, ranked, slots_ready = sem("both_ready"), sem("ranked"), sem("slots_ready")
        scattered, = gather_semaphores(c, 1)
        block = ctx.enter_context(nc.Block())

        @block.gpsimd
        def _(pool):
            nc.gpsimd.iota(expert_id[:], [[1, EXPERTS]], base=0, channel_multiplier=0,
                           allow_small_or_imprecise_dtypes=True)
            nc.gpsimd.iota(real[:], [[0, 1]], base=0, channel_multiplier=1, allow_small_or_imprecise_dtypes=True)
            nc.gpsimd.iota(tile_id[:], [[1, MT]], base=0, channel_multiplier=0, allow_small_or_imprecise_dtypes=True)
            nc.gpsimd.memset(ones16[:], 1.0).then_inc(iota_ready, 1)
            pool.wait_ge(iota_ready, 1)
            nc.gpsimd.affine_select(out=before[:], in_=ones16[:], compare_op=ALU.is_gt, fill=0.0, base=0,
                                    pattern=[[1, P]], channel_multiplier=-1).then_inc(iota_ready, 1)
            pool.wait_ge(slots_ready, 1)
            for t in range(NN):
                rows = P if t < LAST else LAST_ROWS
                for j in range(TOPK):
                    nc.gpsimd.indirect_dma_start(
                        xs, bass.IndirectOffsetOnAxis(ap=slots[0:rows, j, t:t + 1], axis=0),
                        normed[0:rows, t, 0:D], None).then_inc(scattered, 16)
            pool.wait_ge(scattered, 16 * TOPK * NN)

        @block.scalar
        def _(act):
            act.wait_ge(gap_ready, 1)
            nc.scalar.activation(gap[:], gap[:], ACT.Exp).then_inc(exp_ready, 1)

        @block.tensor
        def _(pe):
            pe.wait_ge(both_ready, 1)
            pe.wait_ge(iota_ready, 2)
            nc.tensor.matmul(c.ps[0][:, 0:NN * EXPERTS], before[:], both16[:], start=True, stop=True)
            nc.tensor.matmul(c.ps[1][:, 0:NN * EXPERTS], ones16[:], both16[:], start=True, stop=True
                             ).then_inc(ranked, 1)

        @block.vector
        def _(dve):
            V, step = nc.vector, Steps()

            def done(ins):
                ins.then_inc(step_sem, 1)
                dve.wait_ge(step_sem, step.last())

            done(V.memset(zero[:], 0.0))
            for t in range(NN):
                last = V.max(top[:, t, :], scores[:, t, :])
            done(last)
            for t in range(NN):
                last = V.max_index(at[:, t, :], top[:, t, :], scores[:, t, :])
            done(last)
            V.tensor_tensor(gap[:], top[:, :, 1], top[:, :, 0], ALU.subtract).then_inc(gap_ready, 1)
            dve.wait_ge(exp_ready, 1)
            done(V.tensor_scalar(one_plus[:], gap[:], 1.0, None, ALU.add))
            done(V.reciprocal(probs[:, 0, :], one_plus[:]))
            V.tensor_tensor(probs[:, 1, :], probs[:, 0, :], gap[:], ALU.mult)
            dve.wait_ge(iota_ready, 2)
            done(V.tensor_copy(atf[:], at[:, :, 0:TOPK].rearrange("p t j -> p j t")))
            ids = expert_id[:].unsqueeze(1).broadcast_to([P, NN, EXPERTS])
            for j in range(TOPK):
                done(V.tensor_tensor(chosen[:, j, :, :], ids, atf[:, j, :].unsqueeze(2).broadcast_to([P, NN, EXPERTS]),
                                     ALU.is_equal))
            done(V.tensor_tensor(both[:], chosen[:, 0, :, :], chosen[:, 1, :, :], ALU.add))
            done(V.tensor_scalar(real[:], real[:], float(LAST_ROWS), None, ALU.is_lt))
            done(V.tensor_scalar(both[:, LAST, :], both[:, LAST, :], real[:], None, ALU.mult))
            V.tensor_copy(both16[:], both[:].rearrange("p t e -> p (t e)")).then_inc(both_ready, 1)
            dve.wait_ge(ranked, 1)
            flat = lambda ap: ap.rearrange("p t e -> p (t e)")
            done(V.tensor_copy(flat(place[:]), c.ps[0][:, 0:NN * EXPERTS]))
            done(V.tensor_copy(flat(total[:]), c.ps[1][:, 0:NN * EXPERTS]))
            for e in range(EXPERTS):
                last = V.tensor_tensor_scan(running[:, :, e], total[:, :, e], zero[:], 0.0, ALU.add, ALU.add)
            done(last)
            done(V.tensor_tensor(place[:], place[:], running[:], ALU.add))
            done(V.tensor_tensor(place[:], place[:], total[:], ALU.subtract))
            done(V.tensor_scalar(nrows[:], running[:, NN - 1, :], P - 1.0, None, ALU.add))
            done(V.tensor_copy(ntiles_i[:], nrows[:]))
            done(V.tensor_single_scalar(ntiles_i[:], ntiles_i[:], 7, ALU.arith_shift_right))
            done(V.tensor_copy(ntiles[:], ntiles_i[:]))
            done(V.tensor_tensor_scan(tend[:], ntiles[:], zero[:, 0:EXPERTS], 0.0, ALU.add, ALU.add))
            done(V.tensor_tensor(tstart[:], tend[:], ntiles[:], ALU.subtract))
            done(V.tensor_scalar(nrows[:], tstart[:], float(P), None, ALU.mult))
            done(V.tensor_tensor(place[:], place[:], nrows[:].unsqueeze(1).broadcast_to([P, NN, EXPERTS]), ALU.add))
            for j in range(TOPK):
                done(V.tensor_tensor(picked[:], place[:], chosen[:, j, :, :], ALU.mult))
                done(V.tensor_reduce(slot_f[:, j, :], picked[:], AX.X, ALU.add))
            V.tensor_copy(slots[:], slot_f[:]).then_inc(slots_ready, 1)
            done(V.tensor_tensor(passed[:], tstart[:].unsqueeze(1).broadcast_to([P, MT, EXPERTS]),
                                 tile_id[:].unsqueeze(2).broadcast_to([P, MT, EXPERTS]), ALU.is_le))
            done(V.tensor_reduce(expert_f[:], passed[:], AX.X, ALU.add))
            done(V.tensor_scalar(expert_f[:], expert_f[:], -1.0, None, ALU.add))
            V.tensor_copy(expert_row[:], expert_f[0:1, :])


def run_experts(nc, c, xs, ys, w1t, w1, w2, w2_in, bias_parts, expert_row):
    with ExitStack() as ctx:
        sb = lambda name, shape, dt=F32: ctx.enter_context(nc.sbuf_tensor(name, shape, dt))
        sem = semaphores(nc, ctx)
        bias = sb("bias_rows", [3, EXPERTS, BW], BF16)
        ones16 = sb("ones3", [3, P], BF16)
        R = 4
        x, xT = sb("x9", [P, R, D]), sb("x9T", [P, 2, D])
        h, hT = sb("h9", [P, HIDDEN]), sb("h9T", [P, HIDDEN])
        y = sb("y9", [P, R, D])
        weights_in, ones_ready = sem("experts_in"), sem("ones3_ready")
        x_in = [sem(f"x9_in{s}") for s in range(R)]
        y_out = [sem(f"y9_out{s}") for s in range(R)]
        xT_made, xT_ready, h_made, h_ready = sem("x9T_made"), sem("x9T_ready"), sem("h9_made"), sem("h9_ready")
        hT_made, hT_ready, y_made, y_ready = sem("h9T_made"), sem("h9T_ready"), sem("y9_made"), sem("y9_ready")
        block = ctx.enter_context(nc.Block())
        xT_ps = [c.ps[0][:, 0:D], c.ps[7][:, 0:D]]
        h_ps, hT_ps = [c.ps[1], c.ps[2]], [c.ps[3], c.ps[4]]
        y_ps = [c.ps[5][:, 0:D], c.ps[6][:, 0:D]]

        @block.sync
        def _(sp):
            for e in range(EXPERTS):
                sp.dma_start(w1[:, e], w1t[e].rearrange("(c p) n -> p c n", p=P)).then_inc(weights_in, 16)
            sp.dma_start(bias[:], bias_parts).then_inc(weights_in, 16)

            def load(t, s, i):
                if again(t, R):
                    sp.wait_ge(xT_made, t - R + 1)
                sp.dma_start(x[:, s, :], xs[bass.ds(t * P, P), :]).then_inc(x_in[s], 16)

            def store(t, s, i):
                sp.wait_ge(y_ready, t + 1)
                sp.dma_start(ys[bass.ds(t * P, P), :], y[:, s, :]).then_inc(y_out[s], 16)

            pipeline(sp, MT, [(0, load), (R - 1, store)], R)
            for s in range(R):
                sp.wait_ge(y_out[s], 16 * len(range(s, MT, R)))

        @block.tensor
        def _(pe):
            pe.wait_ge(weights_in, 16 * (EXPERTS + 1))
            pe.wait_ge(w2_in, 16 * EXPERTS)
            pe.wait_ge(ones_ready, 1)

            def turn_x(t, s, i):
                pe.wait_ge(x_in[s], 16 * (i + 1))
                if again(t, 2):
                    pe.wait_ge(xT_ready, t - 1)
                for k in range(KC):
                    last = nc.tensor.transpose(xT_ps[s % 2][:, k * P:(k + 1) * P], x[:, s, k * P:(k + 1) * P], c.ident[:])
                last.then_inc(xT_made, 1)

            def expert(t):
                return pe.value_load(expert_row[0:1, bass.ds(t, 1)], min_val=0, max_val=EXPERTS - 1)

            def hidden(t, s, i):
                e = expert(t)
                pe.wait_ge(xT_ready, t + 1)
                for n in range(2):
                    lo = n * 512
                    if again(t, 1):
                        pe.wait_ge(h_ready, 2 * t - 1 + n)
                    for k in range(KC):
                        nc.tensor.matmul(h_ps[n][:], xT[:, s % 2, k * P:(k + 1) * P],
                                         w1[:, bass.ds(e, 1), k, lo:lo + 512].rearrange("p o n -> p (o n)"),
                                         start=(k == 0), stop=False)
                    nc.tensor.matmul(h_ps[n][:], ones16[:],
                                     bias[:, bass.ds(e, 1), lo:lo + 512].rearrange("p o n -> p (o n)"),
                                     start=False, stop=True).then_inc(h_made, 1)

            def turn_h(t, s, i):
                for n in range(2):
                    pe.wait_ge(h_ready, 2 * t + n + 1)
                    if again(t, 1):
                        pe.wait_ge(hT_ready, 2 * t - 1 + n)
                    for k in range(4):
                        lo = (4 * n + k) * P
                        last = nc.tensor.transpose(hT_ps[n][:, k * P:(k + 1) * P], h[:, lo:lo + P], c.ident[:])
                    last.then_inc(hT_made, 1)

            def output(t, s, i):
                e = expert(t)
                if again(t, 2):
                    pe.wait_ge(y_ready, t - 1)
                for k in range(HIC):
                    if k % 4 == 0:
                        pe.wait_ge(hT_ready, 2 * t + k // 4 + 1)
                    nc.tensor.matmul(y_ps[s % 2], hT[:, k * P:(k + 1) * P],
                                     w2[:, bass.ds(e, 1), k, :].rearrange("p o n -> p (o n)"),
                                     start=(k == 0), stop=False)
                nc.tensor.matmul(y_ps[s % 2], ones16[:], bias[:, bass.ds(e, 1), HIDDEN:BW].rearrange("p o n -> p (o n)"),
                                 start=False, stop=True).then_inc(y_made, 1)

            pipeline(pe, MT, [(0, turn_x), (2, turn_h), (1, hidden), (2, output)], R)

        @block.scalar
        def _(act):
            def copy_xT(t, s, i):
                act.wait_ge(xT_made, t + 1)
                if again(t, 2):
                    act.wait_ge(h_made, 2 * (t - 1))
                nc.scalar.copy(xT[:, s % 2, :], xT_ps[s % 2]).then_inc(xT_ready, 1)

            def relu(t, s, i):
                for n in range(2):
                    act.wait_ge(h_made, 2 * t + n + 1)
                    if again(t, 1):
                        act.wait_ge(hT_made, 2 * t - 1 + n)
                    nc.scalar.activation(h[:, n * 512:(n + 1) * 512], h_ps[n][:], ACT.Relu).then_inc(h_ready, 1)

            pipeline(act, MT, [(0, copy_xT), (1, relu)], R)

        @block.vector
        def _(dve):
            nc.vector.memset(ones16[:], 1.0).then_inc(ones_ready, 1)

            def copy_hT(t, s, i):
                for n in range(2):
                    dve.wait_ge(hT_made, 2 * t + n + 1)
                    if again(t, 1):
                        dve.wait_ge(y_made, t)
                    nc.vector.tensor_copy(hT[:, n * 512:(n + 1) * 512], hT_ps[n][:]).then_inc(hT_ready, 1)

            def copy_y(t, s, i):
                dve.wait_ge(y_made, t + 1)
                if again(t, R):
                    dve.wait_ge(y_out[s], 16 * i)
                nc.vector.tensor_copy(y[:, s, :], y_ps[s % 2]).then_inc(y_ready, 1)

            pipeline(dve, MT, [(0, copy_hT), (0, copy_y)], R)


def combine(nc, c, x1tab, ys, probs, slots, out):
    with ExitStack() as ctx:
        sb = lambda name, shape, dt=F32: ctx.enter_context(nc.sbuf_tensor(name, shape, dt))
        sem = semaphores(nc, ctx)
        R = 3
        x1, y = sb("x1_last", [P, R, D]), sb("y_last", [P, R, TOPK, D])
        x1_in = [sem(f"x1_in{s}") for s in range(R)]
        y_in = gather_semaphores(c, R)
        out_done = [sem(f"out_done{s}") for s in range(R)]
        first, summed = sem("first_added"), sem("both_added")
        block = ctx.enter_context(nc.Block())
        rows = lambda t: P if t < LAST else LAST_ROWS

        @block.sync
        def _(sp):
            for t in range(NN + 1):
                if t < NN:
                    if t >= R:
                        sp.wait_ge(out_done[t % R], 16 * (t // R))
                    sp.dma_start(x1[0:rows(t), t % R, :], x1tab[t * P:t * P + rows(t), :]).then_inc(x1_in[t % R], 16)
                if t >= 1:
                    o = t - 1
                    sp.wait_ge(x1_in[o % R], 16 * (o // R + 1))
                    sp.wait_ge(summed, o + 1)
                    sp.dma_start(out[o * P:o * P + rows(o), :], x1[0:rows(o), o % R, :]).then_inc(out_done[o % R], 16)
            for s in range(R):
                sp.wait_ge(out_done[s], 16 * len(range(s, NN, R)))

        @block.gpsimd
        def _(pool):
            for t in range(NN):
                if t >= R:
                    pool.wait_ge(summed, t - R + 1)
                    pool.wait_ge(y_in[t % R], 32 * (t // R))
                for j in range(TOPK):
                    nc.gpsimd.indirect_dma_start(
                        y[0:rows(t), t % R, j, :], None, ys,
                        bass.IndirectOffsetOnAxis(ap=slots[0:rows(t), j, t:t + 1], axis=0)).then_inc(y_in[t % R], 16)

        @block.vector
        def _(dve):
            for t in range(NN):
                s, r = t % R, rows(t)
                dve.wait_ge(x1_in[s], 16 * (t // R + 1))
                dve.wait_ge(y_in[s], 32 * (t // R + 1))
                for j, sem_ in enumerate((first, summed)):
                    if j == 1:
                        dve.wait_ge(first, t + 1)
                    nc.vector.scalar_tensor_tensor(out=x1[0:r, s, :], in0=y[0:r, s, j, :],
                                                   scalar=probs[0:r, j, t:t + 1], in1=x1[0:r, s, :],
                                                   op0=ALU.mult, op1=ALU.add).then_inc(sem_, 1)


class Shared:
    pass


def build(nc, io):
    with ExitStack() as ctx:
        sb = lambda name, shape, dt=F32: ctx.enter_context(nc.sbuf_tensor(name, shape, dt))
        dram = lambda name, shape, dt=F32: nc.dram_tensor(name, shape, dt, kind="Internal").ap()
        c = Shared()
        c.banks = ctx.enter_context(nc.psum_tensor("banks", [P, 8, 512], F32))
        c.ps = [c.banks[:, b, :] for b in range(8)]
        c.ident = sb("ident", [P, P])
        c.ones = sb("ones", [P, P])
        c.zeros, c.lane = sb("zeros", [P, D]), sb("lane", [P, 1])
        c.minus_half = sb("minus_half", [P, 1])
        c.gathered = [ctx.enter_context(nc.semaphore(f"gathered{s}")) for s in range(16)]
        c.passed = ctx.enter_context(nc.semaphore("passed"))
        c.lane16 = sb("lane16", [P, P], BF16)
        htab, stab = dram("htab", [NP, D]), dram("stab", [NP, HEADS])
        qtab, xntab = dram("qtab", [NP, D]), dram("xntab", [NP, D])
        xTtab = dram("xTtab", [NP, D])
        ytab = dram("ytab", [NP, D])
        build_constants(nc, c)
        block_row = sb("block_row", [1, SG * P], I32)
        probs, slots = sb("probs", [P, TOPK, NN]), sb("slots", [P, TOPK, NN], I32)
        expert_row = sb("expert_row", [1, MT], I32)
        big = sb("big", [P, NT * 3 * HX], BF16)
        hparts = big[:].rearrange("p (t j n) -> p t j n", t=NT, j=3)
        big32 = big[:].bitcast(F32)
        acc = big32[:, 0:NT * HX].rearrange("p (t n) -> p t n", t=NT)
        w1 = big32[:, 0:EXPERTS * KC * HIDDEN].rearrange("p (e c n) -> p e c n", e=EXPERTS, c=KC)
        blocks = dram("blocks", [1, SG * P], I32)
        attr_parts = dram("attr_parts", [12, SG * P, 2 * P], BF16)
        dlrows = dram("dlrows", [SG * P // QUAD, TILES * P], BF16)
        xs, ys = dram("xs", [MT * P, D]), dram("ys", [MT * P, D])
        with ExitStack() as edge_ctx:
            sb = lambda name, shape, dt=F32: edge_ctx.enter_context(nc.sbuf_tensor(name, shape, dt))
            dl, src, keys = sb("dl", [P, NS, 2]), sb("src", [P, NS, 2], I32), sb("keys", [P, NS, 2])
            wparts = sb("wparts", [36, HX], BF16)
            plan_steps(nc, c, io["dst"], io["src"], io["attr"], io["edge_w"], wparts, dl, src, keys, blocks,
                       block_row, attr_parts, dlrows)
            wall, ms = sb("wall", [P, KC, WALL]), sb("ms", [P, NT])
            with ExitStack() as node_ctx:
                nb = lambda name, shape: node_ctx.enter_context(nc.sbuf_tensor(name, shape, F32))
                x_all = nb("x_all", [P, NT, D])
                stats = nb("stats", [P, NT, 6])
                mean, rstd = nb("mean", [P, NT]), nb("rstd", [P, NT])
                fold_weights(nc, c, io["W"], io["WT"], io["a_src"], io["a_dst"], io["w_norm1"], io["w_qkv"], wall,
                             io["x"], x_all, stats)
                row_norms(nc, c, stats, mean, rstd, ms)
                project_graph(nc, c, x_all, mean, rstd, wall, hparts, htab, stab, xTtab, xntab)
            alpha = sb("alpha", [P, 2 * NS * HEADS])
            with nc.sbuf_tensor("r1", [P, NT], F32) as r1:
                project_dense(nc, c, ms, r1, wall, xTtab, qtab, stab, src, alpha)
            mix, ksum = sb("mix", [P, KC, D]), sb("ksum", [P, D])
            mix_weights(nc, c, io["w_out"], mix, ksum)
            score_edges(nc, c, wparts, hparts, stab, attr_parts, dlrows, src, block_row, alpha)
            softmax_numerators(nc, c, keys, alpha, big32[:, 0:RL], big32[:, RL:2 * RL], dram("cross", [4, 2, P]), xs)
            sum_messages_and_mix(nc, c, htab, dl, src, block_row, alpha, acc, mix, ksum, io["x"], io["gnn_bias"],
                                 io["b_out"], io["w_norm2"], qtab, xntab, ytab)
        x1tab = dram("x1tab", [NP, D])
        bias_parts = dram("bias_parts", [3, EXPERTS, BW], BF16)
        with nc.sbuf_tensor("w2", [P, EXPERTS, HIC, D], F32) as w2, nc.semaphore("w2_in") as w2_in:
            with nc.sbuf_tensor("scores", [P, NN, EXPERTS], F32) as scores:
                finish_nodes(nc, c, acc, ytab, x1tab, io["gate_w"], io["gate_b"], io["biases"], scores, bias_parts,
                             io["w2t"], w2, w2_in)
                route(nc, c, scores, acc, xs, probs, slots, expert_row)
            run_experts(nc, c, xs, ys, io["w1t"], w1, w2, w2_in, bias_parts, expert_row)
        combine(nc, c, x1tab, ys, probs, slots, io["out"])
        if "dbg" in io:
            io["dbg"](nc, c, locals())


def layout(inp):
    f = lambda name: np.asarray(inp[name])
    x = np.zeros((NP, D), np.float32)
    x[:N] = f("x")

    def edges(name, fill):
        a = np.full(ET * P, fill, np.int32)
        a[:E] = f(name)
        return a.reshape(ET, P)

    attr = np.zeros((ET * P, 4), np.float32)
    attr[:E, :3], attr[:E, 3] = f("edge_attr_3"), 1.0
    attr = attr.reshape(ET, P, 4).transpose(0, 2, 1)
    edge_w = np.zeros((4, HEADS, HW), np.float32)
    edge_w[:3, :, :HD] = f("L0_gnn_edge_W").T.reshape(3, HEADS, HD)
    edge_w[3, :, :HD] = f("L0_gnn_edge_b").reshape(HEADS, HD)
    edge_w[3, :, HD] = 1.0
    return {
        "x": x,
        "W": f("L0_gnn_W"), "WT": f("L0_gnn_W").T,
        "a_src": f("L0_gnn_a_src"), "a_dst": f("L0_gnn_a_dst"),
        "w_norm1": f("L0_mix_w_norm1"), "w_qkv": f("L0_mix_w_qkv"),
        "gnn_bias": f("L0_gnn_bias"), "w_out": f("L0_mix_w_out"), "b_out": f("L0_mix_b_out"),
        "w_norm2": f("L0_mix_w_norm2"),
        "gate_w": f("L0_ffn_Wg").T, "gate_b": f("L0_ffn_bg"),
        "biases": np.concatenate([f("L0_ffn_b1"), f("L0_ffn_b2")], axis=1),
        "w1t": f("L0_ffn_W1").transpose(0, 2, 1), "w2t": f("L0_ffn_W2").transpose(0, 2, 1),
        "dst": edges("dst", 2 * NP), "src": edges("src", 0), "attr": attr.reshape(ET, 4 * P),
        "edge_w": edge_w.reshape(4, HX),
    }


def kernel(**inputs):
    import concourse.bacc as bacc
    from concourse.bass_utils import run_bass_kernel_spmd

    arrays = {f"in_{n}": np.ascontiguousarray(a) for n, a in layout(inputs).items()}
    nc = bacc.Bacc("TRN2", target_bir_lowering=False, num_devices=1)
    io = {n[3:]: nc.dram_tensor(n, a.shape, mybir.dt.from_np(a.dtype), kind="ExternalInput").ap()
          for n, a in arrays.items()}
    io["out"] = nc.dram_tensor("out", [N, D], F32, kind="ExternalOutput").ap()
    build(nc, io)
    r = run_bass_kernel_spmd(nc, [arrays], core_ids=[0])
    return r.results[0]["out"]
```
